# Optimizing a Trainium2 kernel written in Bass

```python
import numpy as np
import jax
import jax.numpy as jnp

def _softmax(x, axis=-1):
    return jax.nn.softmax(x, axis=axis)

def _gelu(x):
    return jax.nn.gelu(x, approximate=True)

def _silu(x):
    return jax.nn.silu(x)

def _sigmoid(x):
    return jax.nn.sigmoid(x)

def _layernorm(x, axis=-1, eps=1e-05):
    m = jnp.mean(x, axis=axis, keepdims=True)
    v = jnp.var(x, axis=axis, keepdims=True)
    return (x - m) / jnp.sqrt(v + eps)

def _scatter_add(tgt, idx, src, axis=0):
    return tgt.at[idx].add(src)

def _segment_sum(src, seg, n):
    return jax.ops.segment_sum(src, seg, n)
kernel_name = 'mk_seq_preln_d1_jaxref_r4_0d9228'

def setup_inputs(seed: int=0):
    np.random.seed(seed)
    _w = jnp.asarray

    def _L0_attn_setup():
        import jax, jax.numpy as jnp
        import numpy as np
        BASE_FREQUENCY = 10000.0
        LRP = 17
        MIN_L = 1.0 - LRP / 100.0
        SDT_L = (BASE_FREQUENCY - MIN_L * BASE_FREQUENCY) * 2.0
        ARM_ATTENTION = 2.0
        HEADS_DIM = 64

        def _nrope(xs, base, angle_range):
            N, T, d = xs.shape
            half = d // 2
            inv_freq = base ** (-jnp.arange(half, dtype=jnp.float32) / half)
            pos = jnp.arange(T, dtype=jnp.float32)
            scale = angle_range / jnp.maximum(T - 1, 1)
            ang = pos[:, None] * inv_freq[None, :] * scale
            cos, sin = (jnp.cos(ang), jnp.sin(ang))
            x1, x2 = (xs[..., :half], xs[..., half:])
            return jnp.concatenate([x1 * cos - x2 * sin, x1 * sin + x2 * cos], axis=-1)
        key = jax.random.key(seed)
        ks = jax.random.split(key, 9)
        B, T, E = (4, 256, 256)
        x = jax.random.normal(ks[0], (B, T, E), dtype=jnp.float32)

        def w(k):
            return jax.random.normal(k, (E, E), dtype=jnp.float32) * 0.02
        z = jnp.zeros((E,), dtype=jnp.float32)
        return {'x': x, 'Wq': w(ks[1]), 'bq': z, 'Wk': w(ks[2]), 'bk': z, 'Wv': w(ks[3]), 'bv': z, 'Wo': w(ks[4]), 'bo': z, 'nrope_freq': jnp.zeros((1,), dtype=jnp.float32)}
    _L0_attn_in = _L0_attn_setup()

    def _L0_ffn_setup():
        import jax, jax.numpy as jnp
        import numpy as np
        B, T, D = (4, 1024, 256)
        E = 8
        TOP_K = 2
        FFN = 768
        HALF = FFN // 2

        def _kaiming_uniform(key, shape, fan_in):
            bound = 1.0 / np.sqrt(fan_in)
            return jax.random.uniform(key, shape, jnp.float32, -bound, bound)
        key = jax.random.key(seed)
        ks = jax.random.split(key, 7)
        x = jax.random.normal(ks[0], (B, T, D), jnp.float32)
        gate_w = _kaiming_uniform(ks[1], (E, D), D) * 0.01
        w_up = _kaiming_uniform(ks[2], (E, FFN, D), D)
        w_down = _kaiming_uniform(ks[3], (E, D, HALF), HALF)
        sg_gate = _kaiming_uniform(ks[4], (HALF, D), D)
        sg_up = _kaiming_uniform(ks[5], (HALF, D), D)
        sg_down = _kaiming_uniform(ks[6], (D, HALF), HALF)
        return {'x': x, 'gate_w': gate_w, 'w_up': w_up, 'w_down': w_down, 'sg_gate': sg_gate, 'sg_up': sg_up, 'sg_down': sg_down}
    _L0_ffn_in = _L0_ffn_setup()
    _d = {'L0_attn_x': _L0_attn_in['x'], 'L0_attn_Wq': _L0_attn_in['Wq'], 'L0_attn_bq': _L0_attn_in['bq'], 'L0_attn_Wk': _L0_attn_in['Wk'], 'L0_attn_bk': _L0_attn_in['bk'], 'L0_attn_Wv': _L0_attn_in['Wv'], 'L0_attn_bv': _L0_attn_in['bv'], 'L0_attn_Wo': _L0_attn_in['Wo'], 'L0_attn_bo': _L0_attn_in['bo'], 'L0_attn_nrope_freq': _L0_attn_in['nrope_freq'], 'L0_ffn_gate_w': _L0_ffn_in['gate_w'], 'L0_ffn_w_up': _L0_ffn_in['w_up'], 'L0_ffn_w_down': _L0_ffn_in['w_down'], 'L0_ffn_sg_gate': _L0_ffn_in['sg_gate'], 'L0_ffn_sg_up': _L0_ffn_in['sg_up'], 'L0_ffn_sg_down': _L0_ffn_in['sg_down']}
    _x0 = _d['L0_attn_x']
    _d['L0_attn_x'] = jax.random.normal(jax.random.fold_in(jax.random.key(seed), 1), (2, 2048, 256), dtype=_x0.dtype)
    del _x0
    return _d

def reference(L0_attn_x, L0_attn_Wq, L0_attn_bq, L0_attn_Wk, L0_attn_bk, L0_attn_Wv, L0_attn_bv, L0_attn_Wo, L0_attn_bo, L0_attn_nrope_freq, L0_ffn_gate_w, L0_ffn_w_up, L0_ffn_w_down, L0_ffn_sg_gate, L0_ffn_sg_up, L0_ffn_sg_down):

    def _L0_attn_ref(x, Wq, bq, Wk, bk, Wv, bv, Wo, bo, nrope_freq):
        import jax, jax.numpy as jnp
        import numpy as np
        BASE_FREQUENCY = 10000.0
        LRP = 17
        MIN_L = 1.0 - LRP / 100.0
        SDT_L = (BASE_FREQUENCY - MIN_L * BASE_FREQUENCY) * 2.0
        ARM_ATTENTION = 2.0
        HEADS_DIM = 64

        def _nrope(xs, base, angle_range):
            N, T, d = xs.shape
            half = d // 2
            inv_freq = base ** (-jnp.arange(half, dtype=jnp.float32) / half)
            pos = jnp.arange(T, dtype=jnp.float32)
            scale = angle_range / jnp.maximum(T - 1, 1)
            ang = pos[:, None] * inv_freq[None, :] * scale
            cos, sin = (jnp.cos(ang), jnp.sin(ang))
            x1, x2 = (xs[..., :half], xs[..., half:])
            return jnp.concatenate([x1 * cos - x2 * sin, x1 * sin + x2 * cos], axis=-1)
        B, T, E = x.shape
        HD = HEADS_DIM
        H = E // HD
        half = HD // 2
        q = (x @ Wq + bq).reshape(B, T, H, HD).transpose(0, 2, 1, 3)
        k = (x @ Wk + bk).reshape(B, T, H, HD).transpose(0, 2, 1, 3)
        v = (x @ Wv + bv).reshape(B, T, H, HD).transpose(0, 2, 1, 3)
        q_content, q_spatial = (q[..., :half], q[..., half:])
        k_content, k_spatial = (k[..., :half], k[..., half:])
        base = jax.nn.sigmoid(nrope_freq[0]) * SDT_L + MIN_L * BASE_FREQUENCY
        rng = ARM_ATTENTION * jnp.pi
        q_spatial = _nrope(q_spatial.reshape(B * H, T, half), base, rng).reshape(B, H, T, half)
        k_spatial = _nrope(k_spatial.reshape(B * H, T, half), base, rng).reshape(B, H, T, half)
        q = jnp.concatenate([q_content, q_spatial], axis=-1)
        k = jnp.concatenate([k_content, k_spatial], axis=-1)
        score = jnp.einsum('bhqd,bhkd->bhqk', q, k) / jnp.sqrt(jnp.float32(HD))
        attn = jax.nn.softmax(score, axis=-1)
        out = jnp.einsum('bhqk,bhkd->bhqd', attn, v)
        out = out.transpose(0, 2, 1, 3).reshape(B, T, E)
        return out @ Wo + bo

    def _L0_ffn_ref(x, gate_w, w_up, w_down, sg_gate, sg_up, sg_down):
        import jax, jax.numpy as jnp
        import numpy as np
        B, T, D = (4, 1024, 256)
        E = 8
        TOP_K = 2
        FFN = 768
        HALF = FFN // 2

        def _kaiming_uniform(key, shape, fan_in):
            bound = 1.0 / np.sqrt(fan_in)
            return jax.random.uniform(key, shape, jnp.float32, -bound, bound)
        b, t, d = x.shape
        xf = x.reshape(b * t, d)
        N = xf.shape[0]
        logits = xf @ gate_w.T
        topk_logits, topk_idx = jax.lax.top_k(logits, TOP_K)
        topk_w = jax.nn.softmax(topk_logits.astype(jnp.float32), axis=-1).astype(x.dtype)
        comb = jnp.zeros((N, E), x.dtype).at[jnp.arange(N)[:, None], topk_idx].add(topk_w)
        wg = w_up[:, :HALF, :]
        wu = w_up[:, HALF:, :]
        out = jnp.zeros_like(xf)
        for e in range(E):
            g = xf @ wg[e].T
            u = xf @ wu[e].T
            y = jax.nn.silu(g) * u @ w_down[e].T
            out = out + comb[:, e:e + 1] * y
        shared = jax.nn.silu(xf @ sg_gate.T) * (xf @ sg_up.T) @ sg_down.T
        return (shared + out).reshape(b, t, d)
    x = L0_attn_x
    x = x + _L0_attn_ref(_layernorm(x, axis=-1), L0_attn_Wq, L0_attn_bq, L0_attn_Wk, L0_attn_bk, L0_attn_Wv, L0_attn_bv, L0_attn_Wo, L0_attn_bo, L0_attn_nrope_freq)
    x = x + _L0_ffn_ref(_layernorm(x, axis=-1), L0_ffn_gate_w, L0_ffn_w_up, L0_ffn_w_down, L0_ffn_sg_gate, L0_ffn_sg_up, L0_ffn_sg_down)
    return x

_drawn_inputs = setup_inputs


def setup_inputs(seed=0):
    import zlib

    import numpy as np

    out = dict(_drawn_inputs(seed))
    spreads = {'L0_attn_bq': (0.0, 0.8),
     'L0_attn_bk': (0.0, 0.8),
     'L0_attn_bv': (0.0, 0.1),
     'L0_attn_bo': (0.0, 0.1)}
    factors = {'L0_attn_Wq': 8.0, 'L0_attn_Wk': 8.0, 'L0_attn_Wv': 8.0}
    for name, (base, spread) in spreads.items():
        noise = np.random.default_rng([zlib.crc32(name.encode()), seed]).standard_normal(out[name].shape)
        drawn = base * np.exp(spread * noise) if base else spread * noise
        out[name] = jnp.asarray(drawn.astype(out[name].dtype))
    for name, factor in factors.items():
        out[name] = (out[name] * factor).astype(out[name].dtype)
    return out
```

```python
import concourse.bass as bass
from concourse import mybir
from contextlib import ExitStack
import numpy as np


def add_ffn_kernel(nc, x, wq, bq, wk, bk, wv, bv, wo, bo, freq, gate_t, experts, out):
    F32, F16, I32, U32 = mybir.dt.float32, mybir.dt.float16, mybir.dt.int32, mybir.dt.uint32
    ALU, ACT, AX = mybir.AluOpType, mybir.ActivationFunctionType, mybir.AxisListType
    ds = bass.ds

    P = 128
    N, D = x.shape
    B, H, HD = 2, 4, 64
    T = N // B
    NT, TB = N // P, T // P
    KD = D // P
    QB = 512
    NQ = T // QB
    NK = T // P
    HP = H // 2
    NBLK = B * NQ * HP
    RH = HD // 4
    EPS = 1e-5
    AHEAD = 1
    GS = 16
    WS = 16.0
    XS_ = 32.0
    NE, FF = 9, 384
    UPW = KD * 2 * FF
    DNW = 3 * D
    EARLY = 6
    CH = 2 * FF
    MT = 256
    SHARED_TILES = N // MT
    SLOT_TILES = 2 * N // MT + 8
    SDT = (10000.0 - (1.0 - 17 / 100.0) * 10000.0) * 2.0
    MINB = (1.0 - 17 / 100.0) * 10000.0
    ROT = 2.0 * np.pi / (T - 1)

    ctx = ExitStack()
    with ctx:
        def sb(name, shape, dt):
            return ctx.enter_context(nc.sbuf_tensor(name, shape, dt))

        def sem(name):
            return ctx.enter_context(nc.semaphore(name))

        UP16 = EARLY * UPW * 2
        QK16 = H * T
        wide = sb("wide", [P, UP16 + 4 * QK16 + 2 * TB * D], F16)
        UPC, DNC = NE * UPW * 2, NE * DNW * 2
        w_up = wide[:, 0:UPC]
        w_dn = wide[:, UPC:UPC + DNC]
        xs = wide[:, UPC + DNC:UPC + DNC + NT * 2 * D].rearrange("p (t n) -> p t n", t=NT)
        K1 = wide[:, UP16:UP16 + QK16].rearrange("p (h t) -> p h t", h=H)
        K2 = wide[:, UP16 + QK16:UP16 + 2 * QK16].rearrange("p (h t) -> p h t", h=H)
        Q1 = wide[:, UP16 + 2 * QK16:UP16 + 3 * QK16].rearrange("p (h t) -> p h t", h=H)
        Q2 = wide[:, UP16 + 3 * QK16:UP16 + 4 * QK16].rearrange("p (h t) -> p h t", h=H)
        V = wide[:, UP16 + 4 * QK16:].bitcast(F32).rearrange("p (t d) -> p t d", t=TB)
        xres = sb("xres", [P, NT, D], F32)
        ring = sb("ring", [P, 4 * 2 * QB], F32)
        Pr = ring[:, :].rearrange("p (s h q) -> p s h q", s=4, h=2)
        accp = sb("accp", [P, 2, QB], F32)
        accd = sb("accd", [P, 2, QB], F32)
        pvraw = sb("pvraw", [P, QB], F32)
        recip = sb("recip", [P, QB], F32)
        OT = sb("OT", [P, HP, QB], F32)
        stage = sb("stage", [P, 2, CH], F32)
        wqkv = sb("wqkv", [P, 2, KD, 3 * D], F16)
        wo_sb = sb("wo_sb", [P, KD, D], F32)
        bias = sb("bias", [P, 3 * D], F32)
        bo_sb = sb("bo_sb", [P, D], F32)
        cos = sb("cos", [P, TB, RH], F32)
        sin = sb("sin", [P, TB, RH], F32)
        mt = sb("mt", [P, 2 * QB // P, P], F16)
        mx = sb("mx", [P, 2 * QB // P, T // 512], F32)
        m8 = sb("m8", [P, 2 * QB // P], F32)
        idf = sb("idf", [P, P], F32)
        idh = sb("idh", [P, P], F16)
        ones = sb("ones", [P, HD], F32)
        stats = sb("stats", [P, NT, 6], F32)
        mv = sb("mv", [P, NT, 2], F32)
        rstd = sb("rstd", [P, NT], F32)
        sm = sb("sm", [P, 8], F32)
        jpos = sb("jpos", [P, RH + TB], F32)
        ang = stage[:, 0, 0:TB * RH].rearrange("p (t j) -> p t j", t=TB)
        wst = ring[:, 0:KD * 3 * D].rearrange("p (k n) -> p k n", k=KD)
        def slot(base, s, n):
            return ring[:, base + s * n:base + (s + 1) * n]
        xn = [slot(0, s, D) for s in range(2)]
        xh = [slot(512, s, D).bitcast(F16).rearrange("p (a d) -> p a d", a=2) for s in range(2)]
        xT = [slot(1024, s, D).bitcast(F16).rearrange("p (a c) -> p a c", a=4) for s in range(2)]
        qk = [slot(1536, s, 2 * D) for s in range(2)]
        ra = slot(2560, 0, 256).rearrange("p (h c j) -> p h c j", h=2 * H, c=2)
        rb = slot(2816, 0, 256).rearrange("p (h c j) -> p h c j", h=2 * H, c=2)
        qtok = [slot(3072, s, 256).bitcast(F16).rearrange("p (h c) -> p h c", h=H) for s in range(2)]
        ktok = [slot(3584, s, 256).bitcast(F16).rearrange("p (h c) -> p h c", h=H) for s in range(2)]
        zt = sb("zt", [P, 2 * D], F16)
        gate = sb("gate", [P, KD, 8], F32)
        tri = sb("tri", [P, P], F16)
        oneh = sb("oneh", [P, P], F16)
        iot = sb("iot", [P, SLOT_TILES + 16 + 8], F32)
        pos = sb("pos", [P, 2, NT], U32)
        wts = sb("wts", [P, 2, NT], F32)
        exid = sb("exid", [P, SLOT_TILES], I32)
        slots = nc.dram_tensor("slots", (SLOT_TILES * MT, 2 * D), F16, kind="Internal").ap()
        ydram = nc.dram_tensor("ydram", (SLOT_TILES * MT, D), F32, kind="Internal").ap()
        qlo = [accp[:, s, 0:128].bitcast(F16).rearrange("p (h c) -> p h c", h=H) for s in range(2)]

        psum = ctx.enter_context(nc.psum_tensor("psum", [P, 8, 512], F32))
        banks = [psum[:, i, :] for i in range(8)]

        def half(i):
            return banks[i].bitcast(F16)

        def spair(s):
            return psum[:, 2 * s:2 * s + 2, :]
        xtp = [half(4 + s)[:, 0:512].rearrange("p (a c) -> p a c", a=4) for s in range(2)]
        q1ps = half(6)[:, 0:512].rearrange("p (h c) -> p h c", h=H)
        qlps = half(6)[0:HD, 512:1024].rearrange("p (h c) -> p h c", h=H)
        kps = half(7)[:, 0:512].rearrange("p (h c) -> p h c", h=H)
        mtps = half(7).rearrange("p (h c) -> p h c", h=2)
        pvps = banks[6]

        def upc(m, part):
            return w_up[:, ds(m * (4 * FF) + part * 2 * FF, 2 * FF)]

        x_in = sem("x_in"); w_in = sem("w_in"); b_in = sem("b_in"); k_in = sem("k_in")
        pset = sem("pset"); dset = sem("dset"); aset = sem("aset"); ln_ready = sem("ln_ready")
        dch = sem("dch"); bn_done = sem("bn_done")
        xn_ready = sem("xn_ready"); xhi_ready = sem("xhi_ready"); xlo_ready = sem("xlo_ready")
        xtp_ready = sem("xtp_ready"); xt_ready = sem("xt_ready")
        qkv_ready = sem("qkv_ready"); qk_ready = sem("qk_ready"); v_ready = sem("v_ready")
        ra_ready = sem("ra_ready"); rope_done = sem("rope_done")
        hi_done = sem("hi_done"); qlo_done = sem("qlo_done"); tr_q = sem("tr_q"); tr_k = sem("tr_k")
        q_stored = sem("q_stored"); k_stored = sem("k_stored")
        a_ready = sem("a_ready"); max_done = sem("max_done"); m8_done = sem("m8_done")
        negm = sem("negm"); mT_ready = sem("mT_ready"); mrow = sem("mrow")
        s_ready = sem("s_ready"); exp_done = sem("exp_done"); pv_done = sem("pv_done")
        pacc = sem("pacc"); dacc = sem("dacc"); accp_free = sem("accp_free")
        den_ready = sem("den_ready"); recip_done = sem("recip_done"); pv_copied = sem("pv_copied")
        ot_ready = sem("ot_ready"); wo_ready = sem("wo_ready"); wo_added = sem("wo_added")
        bo_added = sem("bo_added"); st_in = [sem(f"st_in{s}") for s in range(2)]; wh_done = sem("wh_done"); wl_done = sem("wl_done")
        z_out = sem("z_out"); done = sem("done"); g_in = sem("g_in")
        st2 = sem("st2"); rs2 = sem("rs2"); xn2_ready = sem("xn2_ready"); hi2 = sem("hi2"); lo2 = sem("lo2")
        t2_ready = sem("t2_ready"); xf_ready = sem("xf_ready"); lg_ready = sem("lg_ready"); top_v = sem("top_v")
        top_i = sem("top_i"); lg_kept = sem("lg_kept"); rch = sem("rch"); cnt_in = sem("cnt_in"); cnt = sem("cnt"); ew = sem("ew")
        routed = sem("routed"); w2_in = [sem(f"w2_in{s}") for s in range(2)]; w2h = sem("w2h"); w2l = sem("w2l")
        scat = sem("scat"); xr_in = [sem(f"xr_in{s}") for s in range(2)]; xtT = sem("xtT"); xte = sem("xte")
        g_ready = sem("g_ready"); u_ready = sem("u_ready"); silu = sem("silu"); h_ready = sem("h_ready")
        hh_ready = sem("hh_ready"); hl_ready = sem("hl_ready"); y_ready = sem("y_ready"); y_read = sem("y_read")
        y_out = [sem(f"y_out{s}") for s in range(2)]; gat = [sem(f"gat{s}") for s in range(GS)]
        comb1 = sem("comb1"); comb2 = sem("comb2")

        def schedule(e, s1, s2, s3, b):
            s1(b, 0, 0)
            s2(b, 0, 0), s1(b, 1, 1)
            with e.Fori(0, TB // 2 - 1) as i:
                for j in range(2):
                    s2(b, i * 2 + j + 1, 1 - j), s3(b, i * 2 + j, j), s1(b, i * 2 + j + 2, j)
            s2(b, TB - 1, 1), s3(b, TB - 2, 0)
            s3(b, TB - 1, 1)

        def row_stats(dve, part_done, mv_done, before):
            for t in range(NT + 1):
                if t < NT:
                    nc.vector.bn_stats(stats[:, t, :], xres[:, t, :]).then_inc(part_done, 1)
                if t:
                    dve.wait_ge(part_done, before + t)
                    nc.vector.bn_aggr(mv[:, t - 1, :], stats[:, t - 1, :]).then_inc(mv_done, 1)

        def blocks(e, b, prologue, block, last):
            n = b * (NQ * HP)
            prologue(n, b)
            block(n, b, 0, 0, (0, 1), False, None)
            with e.Fori(0, NQ - 1) as q:
                m = b * (2 * NQ - 2) + q * 2
                block(n + q * 2 + 1, b, q, 1, (q + 1, 0), False, m)
                block(n + q * 2 + 2, b, q + 1, 0, (q + 1, 1), True, m + 1)
            block(n + 2 * NQ - 1, b, NQ - 1, 1, None, False, None)
            last(n, b)

        block_ = nc.Block()
        block_.__enter__()

        @block_.sync
        def _(sp):
            for c in range(4):
                sp.dma_start(xres[:, 8 * c:8 * c + 8, :],
                             x[c * 1024:(c + 1) * 1024, :].rearrange("(t p) d -> p t d", p=P)).then_inc(x_in, 16)
            for i, w in enumerate((wq, wk, wv)):
                sp.dma_start(wst[:, :, i * D:(i + 1) * D], w.rearrange("(k p) n -> p k n", p=P)).then_inc(w_in, 16)
            sp.dma_start(wo_sb[:, :, :], wo.rearrange("(k p) n -> p k n", p=P)).then_inc(k_in, 16)
            sp.dma_start(gate[:, :, :], gate_t.rearrange("(k p) e -> p k e", p=P)).then_inc(g_in, 16)
            sp.wait_ge(pset, 12)
            zrows = slots.rearrange("(c n p) d -> c p n d", p=P, n=10)
            for c in range(SLOT_TILES * MT // P // 10):
                sp.dma_start(zrows[c], zt[:, :].unsqueeze(1).broadcast_to([P, 10, 2 * D])).then_inc(z_out, 16)
            for i in range(2):
                sp.wait_ge(dset, 1)
                sp.dma_start(stage[:, i, :], experts[:, i * CH:(i + 1) * CH]).then_inc(st_in[i], 16)
            with sp.Fori(0, EARLY - 1) as i:
                for j in range(2):
                    sp.wait_ge(wl_done, i * 2 + j + 1)
                    sp.dma_start(stage[:, j, :], experts[:, ds((i * 2 + j + 2) * CH, CH)]).then_inc(st_in[j], 16)

        @block_.gpsimd
        def _(pool):
            pool.memset(idf[:, :], 0.0).then_inc(pset, 1)
            pool.memset(idh[:, :], 0.0).then_inc(pset, 1)
            pool.iota(jpos[:, 0:RH], pattern=[[1, RH]], base=0, channel_multiplier=0,
                      allow_small_or_imprecise_dtypes=True).then_inc(pset, 1)
            pool.iota(jpos[:, RH:RH + TB], pattern=[[P, TB]], base=0, channel_multiplier=1,
                      allow_small_or_imprecise_dtypes=True).then_inc(pset, 1)
            pool.wait_ge(pset, 4)
            for m in (idf, idh):
                pool.affine_select(out=m[:, :], in_=m[:, :], compare_op=ALU.not_equal, fill=1.0,
                                   base=0, pattern=[[-1, P]], channel_multiplier=1).then_inc(pset, 1)
            pool.memset(ones[:, :], 1.0).then_inc(pset, 1)
            pool.memset(mt[:, :, :].rearrange("p a c -> p (a c)").bitcast(U32), 0).then_inc(pset, 1)
            pool.wait_ge(pset, 8)
            pool.memset(K2[HD:P, :, :].rearrange("p a c -> p (a c)").bitcast(U32), 0).then_inc(pset, 1)
            pool.memset(Q2[HD:P, :, :].rearrange("p a c -> p (a c)").bitcast(U32), 0).then_inc(pset, 1)
            pool.wait_ge(pset, 10)
            pool.memset(K2[HD:HD + 1, :, :].rearrange("p a c -> p (a c)"), 1.0).then_inc(pset, 1)
            pool.wait_ge(pset, 11)
            pool.memset(zt[:, :].bitcast(U32), 0).then_inc(pset, 1)
            pool.memset(tri[:, :], 1.0).then_inc(pset, 1)
            pool.memset(oneh[:, :], 1.0).then_inc(pset, 1)
            pool.iota(iot[:, 0:SLOT_TILES], pattern=[[1, SLOT_TILES]], base=0, channel_multiplier=0,
                      allow_small_or_imprecise_dtypes=True).then_inc(pset, 1)
            pool.iota(iot[:, SLOT_TILES:SLOT_TILES + 16], pattern=[[MT, 16]], base=0, channel_multiplier=0,
                      allow_small_or_imprecise_dtypes=True).then_inc(pset, 1)
            pool.wait_ge(pset, 16)
            pool.affine_select(out=tri[:, :], in_=tri[:, :], compare_op=ALU.is_gt, fill=0.0,
                               base=0, pattern=[[1, P]], channel_multiplier=-1).then_inc(pset, 1)
            pool.sem_inc(accp_free, 1)
            for ahead in (rope_done, pacc):
                pool.sem_inc(ahead, AHEAD)

            def none(b, k, s):
                pass

            def rope(b, k, s):
                g = b * TB + k
                X = qk[s].rearrange("p (h c j) -> p h c j", h=2 * H, c=4)[:, :, 2:4, :]
                cb = cos[:, ds(k, 1), :].unsqueeze(2).broadcast_to([P, 2 * H, 2, RH])
                sbb = sin[:, ds(k, 1), :].unsqueeze(2).broadcast_to([P, 2 * H, 2, RH])
                pool.wait_ge(qk_ready, g + 1)
                pool.wait_ge(rope_done, (g) * 2 + AHEAD)
                pool.tensor_tensor(ra, X, cb, ALU.mult).then_inc(ra_ready, 1)
                pool.tensor_tensor(rb, X, sbb, ALU.mult).then_inc(ra_ready, 1)
                pool.wait_ge(ra_ready, (g + 1) * 2)
                pool.tensor_tensor(X[:, :, 0, :], ra[:, :, 0, :], rb[:, :, 1, :], ALU.subtract).then_inc(rope_done, 1)
                pool.tensor_tensor(X[:, :, 1, :], ra[:, :, 1, :], rb[:, :, 0, :], ALU.add).then_inc(rope_done, 1)

            def prologue(n, b):
                pool.wait_ge(xn_ready, b * TB + TB)
                bo4 = bo_sb[:, :].unsqueeze(1).broadcast_to([P, 4, D])
                for c in range(4):
                    xs = xres[:, ds(b * TB + 4 * c, 4), :]
                    pool.tensor_tensor(xs, xs, bo4, ALU.add).then_inc(bo_added, 1)

            def block(n, b, q, hp, nxt, add, m):
                pool.wait_ge(accp_free, n + 1)
                for j in range(1, 13):
                    pool.wait_ge(exp_done, n * NK + j + 1)
                    if j == 1:
                        pool.tensor_tensor(accp[:, :, :], Pr[:, 0, :, :], Pr[:, 1, :, :], ALU.add).then_inc(pacc, 1)
                    else:
                        pool.wait_ge(pacc, n * 12 + j - 1 + AHEAD)
                        pool.tensor_tensor(accp[:, :, :], accp[:, :, :], Pr[:, j % 4, :, :], ALU.add).then_inc(pacc, 1)

            pool.wait_ge(dch, 10)
            pool.wait_ge(k_in, 16)
            pool.wait_ge(b_in, 80)
            with pool.Fori(0, B) as b:
                schedule(pool, none, rope, none, b)
                blocks(pool, b, prologue, block, lambda n, b: None)

        @block_.scalar
        def _(act):
            for ahead in (q_stored, pv_copied):
                act.sem_inc(ahead, AHEAD)
            act.dma_start(sm[:, 0:1], freq.rearrange("(a n) -> a n", a=1).broadcast_to([P, 1])).then_inc(b_in, 16)
            for i, v in enumerate((bq, bk, bv)):
                act.dma_start(bias[:, i * D:(i + 1) * D],
                              v.rearrange("(a n) -> a n", a=1).broadcast_to([P, D])).then_inc(b_in, 16)
            act.dma_start(bo_sb[:, :], bo.rearrange("(a n) -> a n", a=1).broadcast_to([P, D])).then_inc(b_in, 16)
            act.wait_ge(b_in, 80)
            nc.scalar.activation(sm[:, 1:2], sm[:, 0:1], ACT.Exp, scale=-1.0).then_inc(aset, 1)
            act.wait_ge(dch, 3)
            nc.scalar.activation(sm[:, 5:6], sm[:, 4:5], ACT.Ln).then_inc(aset, 1)
            act.wait_ge(dch, 4)
            nc.scalar.activation(jpos[:, 0:RH], jpos[:, 0:RH], ACT.Exp, scale=-1.0 / RH).then_inc(aset, 1)
            act.wait_ge(dch, 7)
            nc.scalar.activation(sin[:, :, :], sin[:, :, :], ACT.Sin).then_inc(aset, 1)
            act.wait_ge(dch, 8)
            nc.scalar.activation(cos[:, :, :], cos[:, :, :], ACT.Sin).then_inc(aset, 1)
            act.wait_ge(ln_ready, 1)
            nc.scalar.activation(rstd[:, :], rstd[:, :], ACT.Sqrt).then_inc(aset, 1)
            act.wait_ge(w_in, 48)
            nc.scalar.activation(wqkv[:, 0, :, :], wst, ACT.Copy, scale=WS).then_inc(aset, 1)

            def s1(b, k, s):
                g = b * TB + k
                act.wait_ge(xn_ready, g + 1)
                nc.scalar.activation(xh[s][:, 0, :], xn[s], ACT.Copy).then_inc(xhi_ready, 1)

            def s1b(b, k, s):
                g = b * TB + k
                act.wait_ge(xtp_ready, g + 1)
                nc.scalar.activation(xT[s], xtp[s], ACT.Copy).then_inc(xt_ready, 1)

            def s3(b, k, s):
                g = b * TB + k
                act.wait_ge(rope_done, (g + 1) * 2 + AHEAD)
                qv = qk[s][:, 0:D].rearrange("p (h c) -> p h c", h=H)
                kv = qk[s][:, D:2 * D].rearrange("p (h c) -> p h c", h=H)
                nc.scalar.activation(qtok[s].rearrange("p h (a c) -> p h a c", a=2),
                                     qv.unsqueeze(2).broadcast_to([P, H, 2, HD]), ACT.Copy).then_inc(hi_done, 1)
                nc.scalar.activation(ktok[s][:, :, 0:HD], kv, ACT.Copy).then_inc(hi_done, 1)

            def s3b(b, k, s):
                g = b * TB + k
                act.wait_ge(tr_q, g + 1)
                nc.scalar.activation(Q1[:, :, ds(k * P, P)], q1ps, ACT.Copy).then_inc(q_stored, 1)
                nc.scalar.activation(Q2[0:HD, :, ds(k * P, P)], qlps, ACT.Copy).then_inc(q_stored, 1)

            def none(*a):
                pass

            def st1(b, k, s):
                s1(b, k, s)

            def block(n, b, q, hp, nxt, add, m):
                for kt in range(NK):
                    act.wait_ge(s_ready, n * NK + kt + 1)
                    if kt == 0:
                        act.wait_ge(pacc, n * 12 + AHEAD)
                    elif kt < 3:
                        act.wait_ge(dacc, n * 3 + 1)
                    elif kt == 3:
                        act.wait_ge(dacc, n * 3 + 3)
                    else:
                        act.wait_ge(pacc, n * 12 + max(kt - 4, 1) + AHEAD)
                    nc.scalar.activation(Pr[:, kt % 4, :, :], spair(kt % 2), ACT.Exp, scale=HD ** -0.5).then_inc(exp_done, 1)
                    if kt == 5 and m is not None:
                        act.wait_ge(st_in[1 - hp], b * ((NQ - 1) * 16) + (q + (hp == 1)) * 16)
                        nc.scalar.activation(upc(m, 0), stage[:, 1 - hp, :], ACT.Copy, scale=XS_).then_inc(wh_done, 1)
                act.wait_ge(pv_done, n + 1)
                act.wait_ge(ot_ready, n + AHEAD)
                nc.scalar.activation(pvraw[:, :], pvps, ACT.Copy).then_inc(pv_copied, 1)

            with act.Fori(0, B) as b:
                s1(b, 0, 0)
                s1(b, 1, 1), s1b(b, 0, 0)
                s1b(b, 1, 1)
                with act.Fori(0, TB // 2 - 1) as i:
                    for j in range(2):
                        k = i * 2 + j
                        s1(b, k + 2, j), s3(b, k, j), s1b(b, k + 2, j), s3b(b, k, j)
                s3(b, TB - 2, 0), s3b(b, TB - 2, 0)
                s3(b, TB - 1, 1), s3b(b, TB - 1, 1)
                blocks(act, b, none, block, none)

        @block_.vector
        def _(dve):
            chain = [0]

            def link(ins):
                chain[0] += 1
                ins.then_inc(dch, 1)
                dve.wait_ge(dch, chain[0])

            dve.wait_ge(aset, 1)
            link(nc.vector.tensor_scalar(sm[:, 2:3], sm[:, 1:2], 1.0, None, ALU.add))
            link(nc.vector.reciprocal(sm[:, 3:4], sm[:, 2:3]))
            link(nc.vector.tensor_scalar(sm[:, 4:5], sm[:, 3:4], SDT, MINB, ALU.mult, ALU.add))
            dve.wait_ge(aset, 2)
            dve.wait_ge(pset, 4)
            link(nc.vector.tensor_scalar(jpos[:, 0:RH], jpos[:, 0:RH], sm[:, 5:6], None, ALU.mult))
            dve.wait_ge(aset, 3)
            link(nc.vector.tensor_tensor(ang, jpos[:, RH:RH + TB].unsqueeze(2).broadcast_to([P, TB, RH]),
                                         jpos[:, 0:RH].unsqueeze(1).broadcast_to([P, TB, RH]), ALU.mult))
            PI = 3.1415925
            link(nc.vector.tensor_scalar(sin[:, :, :], ang, -ROT, float(np.pi), ALU.mult, ALU.add))
            link(nc.vector.tensor_scalar(sin[:, :, :], sin[:, :, :], PI, -PI, ALU.min, ALU.max))
            link(nc.vector.tensor_scalar(cos[:, :, :], ang, ROT / 2, PI, ALU.mult, ALU.min))
            dve.wait_ge(aset, 5)
            link(nc.vector.tensor_tensor(cos[:, :, :], cos[:, :, :], cos[:, :, :], ALU.mult))
            link(nc.vector.tensor_scalar(cos[:, :, :], cos[:, :, :], -2.0, 1.0, ALU.mult, ALU.add))
            dve.wait_ge(x_in, 64)
            row_stats(dve, bn_done, dset, 0)
            dve.wait_ge(dset, NT)
            nc.vector.tensor_scalar(rstd[:, :], mv[:, :, 1], EPS, None, ALU.add).then_inc(ln_ready, 1)
            dve.wait_ge(aset, 6)
            nc.vector.reciprocal(rstd[:, :], rstd[:, :]).then_inc(ln_ready, 1)
            dve.wait_ge(aset, 7)
            nc.vector.scalar_tensor_tensor(out=wqkv[:, 1, :, :].rearrange("p k n -> p (k n)"),
                                           in0=wst.rearrange("p k n -> p (k n)"), scalar=WS,
                                           in1=wqkv[:, 0, :, :].rearrange("p k n -> p (k n)"),
                                           op0=ALU.mult, op1=ALU.subtract).then_inc(ln_ready, 1)
            dve.wait_ge(ln_ready, 3)
            dve.wait_ge(b_in, 80)
            nc.vector.sem_inc(dacc, 3)
            for ahead in (ot_ready, recip_done, k_stored, wo_added):
                dve.sem_inc(ahead, AHEAD)

            def s1(b, k, s):
                g = b * TB + k
                nc.vector.tensor_scalar(xn[s], xres[:, ds(g, 1), :].rearrange("p a d -> p (a d)"),
                                        mv[:, ds(g, 1), 0], rstd[:, ds(g, 1)], ALU.subtract, ALU.mult).then_inc(xn_ready, 1)

            def s1b(b, k, s):
                g = b * TB + k
                dve.wait_ge(xhi_ready, g + 1)
                nc.vector.tensor_tensor(xh[s][:, 1, :], xn[s], xh[s][:, 0, :], ALU.subtract).then_inc(xlo_ready, 1)

            def s2(b, k, s):
                g = b * TB + k
                dve.wait_ge(qkv_ready, g + 1)
                nc.vector.scalar_tensor_tensor(out=qk[s], in0=banks[2 * s], scalar=1.0 / WS, in1=bias[:, 0:2 * D],
                                               op0=ALU.mult, op1=ALU.add).then_inc(qk_ready, 1)
                nc.vector.scalar_tensor_tensor(out=V[:, ds(k, 1), :].rearrange("p a d -> p (a d)"),
                                               in0=banks[2 * s + 1][:, 0:D], scalar=1.0 / WS,
                                               in1=bias[:, 2 * D:3 * D], op0=ALU.mult, op1=ALU.add).then_inc(v_ready, 1)

            def s3(b, k, s):
                g = b * TB + k
                dve.wait_ge(hi_done, (g + 1) * 2)
                qv = qk[s][:, 0:D].rearrange("p (h c) -> p h c", h=H)
                kv = qk[s][:, D:2 * D].rearrange("p (h c) -> p h c", h=H)
                nc.vector.tensor_tensor(qlo[s][:, :, :], qv, qtok[s][:, :, 0:HD], ALU.subtract).then_inc(qlo_done, 1)
                nc.vector.tensor_tensor(ktok[s][:, :, HD:P], kv, ktok[s][:, :, 0:HD], ALU.subtract).then_inc(qlo_done, 1)

            def s3b(b, k, s):
                g = b * TB + k
                dve.wait_ge(tr_k, g + 1)
                nc.vector.tensor_copy(K1[:, :, ds(k * P, P)], kps).then_inc(k_stored, 1)
                nc.vector.tensor_copy(K2[0:HD, :, ds(k * P, P)], kps[0:HD]).then_inc(k_stored, 1)

            def row_max(n, a):
                dve.wait_ge(a_ready, n * 32 + a + 1)
                nc.vector.tensor_reduce(mx[:, a // 4, a % 4:a % 4 + 1], banks[4 + a % 2][:, :], AX.X, ALU.max).then_inc(max_done, 1)

            def max_col(n):
                dve.wait_ge(max_done, (n + 1) * 32)
                nc.vector.tensor_reduce(m8[:, :], mx[:, :, :], AX.X, ALU.max).then_inc(m8_done, 1)
                dve.wait_ge(m8_done, n + 1)
                nc.vector.tensor_scalar(mt[:, :, HD:HD + 1], m8[:, :].unsqueeze(2), -1.0, None, ALU.mult).then_inc(negm, 1)

            def max_row(n, b, q, hp):
                dve.wait_ge(mT_ready, n + 1)
                nc.vector.tensor_copy(Q2[HD:HD + 1, 2 * hp:2 * hp + 2, ds(q * QB, QB)], mtps[HD:HD + 1]).then_inc(mrow, 1)

            def add_out(b, q, r):
                dve.wait_ge(wo_ready, (b * NQ + q) * 2 + r + 1)
                xs = xres[:, ds(b * TB + q * 4 + 2 * r, 2), :]
                nc.vector.tensor_tensor(xs, banks[7][:, :].rearrange("p (a d) -> p a d", a=2), xs, ALU.add).then_inc(wo_added, 1)

            def prologue(n, b):
                for a in range(32):
                    row_max(n, a)
                max_col(n)
                max_row(n, b, 0, 0)

            def block(n, b, q, hp, nxt, add, m):
                for kt in range(NK):
                    if nxt and kt < 8:
                        for a in range(4 * kt, 4 * kt + 4):
                            row_max(n + 1, a)
                    if add and kt == 4:
                        dve.wait_ge(bo_added, b * 4 + 4)
                        add_out(b, q - 1, 0)
                    if add and kt == 7:
                        add_out(b, q - 1, 1)
                    if nxt and kt == 8:
                        max_col(n + 1)
                    if nxt and kt == 11:
                        max_row(n + 1, b, *nxt)
                    if kt == 10 and m is not None:
                        dve.wait_ge(wh_done, m + 1)
                        nc.vector.scalar_tensor_tensor(out=upc(m, 1), in0=stage[:, 1 - hp, :], scalar=XS_, in1=upc(m, 0),
                                                       op0=ALU.mult, op1=ALU.subtract).then_inc(wl_done, 1)
                    if kt == 14:
                        dve.wait_ge(exp_done, n * NK + 15)
                        dve.wait_ge(den_ready, n + AHEAD)
                        nc.vector.tensor_tensor(accd[:, :, :], Pr[:, 1, :, :], Pr[:, 2, :, :], ALU.add).then_inc(dacc, 1)
                        dve.wait_ge(pacc, n * 12 + 12 + AHEAD)
                        dve.wait_ge(dacc, n * 3 + 4)
                        nc.vector.tensor_tensor(accd[:, :, :], accd[:, :, :], accp[:, :, :], ALU.add).then_inc(dacc, 1)
                        dve.wait_ge(dacc, n * 3 + 5)
                        nc.vector.sem_inc(accp_free, 1)
                dve.wait_ge(exp_done, n * NK + 16)
                nc.vector.tensor_tensor(accd[:, :, :], accd[:, :, :], Pr[:, 3, :, :], ALU.add).then_inc(dacc, 1)
                dve.wait_ge(den_ready, n + 1 + AHEAD)
                nc.vector.reciprocal(recip[:, :], banks[7][:, :]).then_inc(recip_done, 1)
                dve.wait_ge(recip_done, n + 1 + AHEAD)
                dve.wait_ge(pv_copied, n + 1 + AHEAD)
                nc.vector.tensor_tensor(OT[:, hp, :], pvraw[:, :], recip[:, :], ALU.mult).then_inc(ot_ready, 1)

            def last(n, b):
                for r in range(2):
                    add_out(b, NQ - 1, r)

            with dve.Fori(0, B) as b:
                s1(b, 0, 0), s1b(b, 0, 0)
                s1(b, 1, 1), s2(b, 0, 0), s1b(b, 1, 1)
                with dve.Fori(0, TB // 2 - 1) as i:
                    for j in range(2):
                        k = i * 2 + j
                        s1(b, k + 2, j), s2(b, k + 1, 1 - j), s3(b, k, j), s1b(b, k + 2, j), s3b(b, k, j)
                s2(b, TB - 1, 1), s3(b, TB - 2, 0), s3b(b, TB - 2, 0)
                s3(b, TB - 1, 1), s3b(b, TB - 1, 1)
                blocks(dve, b, prologue, block, last)

        @block_.tensor
        def _(pe):
            pe.sem_inc(den_ready, AHEAD)
            pe.wait_ge(pset, 17)
            pe.wait_ge(ln_ready, 3)
            pe.wait_ge(k_in, 16)

            def s1(b, k, s):
                g = b * TB + k
                pe.wait_ge(xlo_ready, g + 1)
                for a in range(4):
                    m = nc.tensor.transpose(xtp[s][:, a, :], xh[s][:, a // 2, (a % 2) * P:(a % 2 + 1) * P], idh[:, :])
                m.then_inc(xtp_ready, 1)

            def s2(b, k, s):
                g = b * TB + k
                pe.wait_ge(xt_ready, g + 1)
                parts = [(xp, wp, c) for xp, wp in ((0, 0), (0, 1), (1, 0)) for c in range(KD)]
                for o, (bank, lo, hi) in enumerate(((2 * s, 0, 2 * D), (2 * s + 1, 2 * D, 3 * D))):
                    for j, (xp, wp, c) in enumerate(parts):
                        m = nc.tensor.matmul(banks[bank][:, 0:hi - lo], xT[s][:, 2 * xp + c, :], wqkv[:, wp, c, lo:hi],
                                             start=(j == 0), stop=(j == len(parts) - 1))
                m.then_inc(qkv_ready, 1)

            def s3(b, k, s):
                g = b * TB + k
                pe.wait_ge(qlo_done, (g + 1) * 2)
                pe.wait_ge(k_stored, g * 2 + AHEAD)
                for h in range(H):
                    m = nc.tensor.transpose(kps[:, h, :], ktok[s][:, h, :], idh[:, :])
                m.then_inc(tr_k, 1)
                pe.wait_ge(q_stored, g * 2 + AHEAD)
                for h in range(H):
                    nc.tensor.transpose(q1ps[:, h, :], qtok[s][:, h, :], idh[:, :])
                for h in range(H):
                    m = nc.tensor.transpose(qlps[:, h, :], qlo[s][:, h, :], idh[:, :])
                m.then_inc(tr_q, 1)

            def a_mm(n, q, hp, a):
                hh, qt, kc = a // 16, a // 4 % 4, a % 4
                h = 2 * hp + hh
                if a >= 2:
                    pe.wait_ge(max_done, n * 32 + a - 1)
                nc.tensor.matmul(banks[4 + a % 2][:, :], Q1[:, h, ds(q * QB + qt * P, P)], K1[:, h, kc * 512:(kc + 1) * 512],
                                 start=True, stop=True).then_inc(a_ready, 1)

            def m_turn(n):
                pe.wait_ge(negm, n + 1)
                for j in range(8):
                    m = nc.tensor.transpose(mtps[:, j // 4, (j % 4) * P:(j % 4 + 1) * P], mt[:, j, :], idh[:, :])
                m.then_inc(mT_ready, 1)

            def scores(n, q, hp, kt):
                for hh in range(2):
                    h = 2 * hp + hh
                    o = banks[2 * (kt % 2) + hh][:, :]
                    nc.tensor.matmul(o, K1[:, h, kt * P:(kt + 1) * P], Q1[:, h, ds(q * QB, QB)], start=True, stop=False)
                    m = nc.tensor.matmul(o, K2[:, h, kt * P:(kt + 1) * P], Q2[:, h, ds(q * QB, QB)], start=False, stop=True)
                m.then_inc(s_ready, 1)

            def out_proj(b, q, r):
                for j in range(2):
                    c = 2 * r + j
                    for hp in range(HP):
                        m = nc.tensor.matmul(banks[7][:, j * D:(j + 1) * D], OT[:, hp, c * P:(c + 1) * P], wo_sb[:, hp, :],
                                             start=(hp == 0), stop=(hp == HP - 1))
                m.then_inc(wo_ready, 1)

            def prologue(n, b):
                pe.wait_ge(q_stored, (b + 1) * (2 * TB) + AHEAD)
                pe.wait_ge(k_stored, (b + 1) * (2 * TB) + AHEAD)
                for a in range(32):
                    a_mm(n, 0, 0, a)
                pe.wait_ge(wo_added, b * (2 * NQ) + AHEAD)
                m_turn(n)
                pe.wait_ge(mrow, n + 1)
                scores(n, 0, 0, 0)
                scores(n, 0, 0, 1)

            def block(n, b, q, hp, nxt, add, m):
                for kt in range(NK):
                    if nxt and kt < 8:
                        for a in range(4 * kt, 4 * kt + 4):
                            a_mm(n + 1, nxt[0], nxt[1], a)
                    if add and kt == 3:
                        pe.wait_ge(ot_ready, n + AHEAD)
                        out_proj(b, q - 1, 0)
                    if add and kt == 6:
                        pe.wait_ge(wo_added, (b * NQ + q - 1) * 2 + 1 + AHEAD)
                        out_proj(b, q - 1, 1)
                    if nxt and kt == 10:
                        if add:
                            pe.wait_ge(wo_added, (b * NQ + q) * 2 + AHEAD)
                        else:
                            pe.wait_ge(recip_done, n + AHEAD)
                        m_turn(n + 1)
                    pe.wait_ge(exp_done, n * NK + kt + 1)
                    if kt == 0:
                        pe.wait_ge(pv_copied, n + AHEAD)
                    for hh in range(2):
                        h = 2 * hp + hh
                        m = nc.tensor.matmul(banks[6][hh * HD:(hh + 1) * HD, :], V[:, kt, h * HD:(h + 1) * HD],
                                             Pr[:, kt % 4, hh, :], start=(kt == 0), stop=(kt == NK - 1))
                    if kt == NK - 1:
                        m.then_inc(pv_done, 1)
                    if kt < NK - 2:
                        scores(n, q, hp, kt + 2)
                    elif nxt:
                        if kt == NK - 2:
                            pe.wait_ge(mrow, n + 2)
                        scores(n + 1, nxt[0], nxt[1], kt + 2 - NK)
                pe.wait_ge(dacc, n * 3 + 6)
                if not nxt:
                    pe.wait_ge(recip_done, n + AHEAD)
                for hh in range(2):
                    m = nc.tensor.matmul(banks[7][hh * HD:(hh + 1) * HD, :], ones[:, :], accd[:, hh, :], start=True, stop=True)
                m.then_inc(den_ready, 1)

            def last(n, b):
                pe.wait_ge(ot_ready, n + 8 + AHEAD)
                out_proj(b, NQ - 1, 0)
                pe.wait_ge(wo_added, (b * NQ + NQ - 1) * 2 + 1 + AHEAD)
                out_proj(b, NQ - 1, 1)

            with pe.Fori(0, B) as b:
                schedule(pe, s1, s2, s3, b)
                blocks(pe, b, prologue, block, last)

        block_.__exit__(None, None, None)

        xn2 = [pvraw[:, s * D:(s + 1) * D] for s in range(2)]
        xf = [recip[:, s * D:(s + 1) * D].rearrange("p (k c) -> p k c", k=KD) for s in range(2)]
        st_sm = [stage[:, s, :] for s in range(2)]
        col = lambda i, n=NT * 8: ring[:, i * 256:i * 256 + n]
        lg = col(12).rearrange("p (t e) -> p t e", e=8)
        v8 = col(0).rearrange("p (t e) -> p t e", e=8)
        i8 = col(1).bitcast(U32).rearrange("p (t e) -> p t e", e=8)
        i8f = col(2, NT * 2).rearrange("p (t k) -> p t k", k=2)
        oh = [col(3 + k).rearrange("p (t e) -> p t e", e=8) for k in range(2)]
        m16 = col(5, 128).bitcast(F16)
        tot = col(6).rearrange("p (e t) -> p e t", e=8)
        inc = col(7).rearrange("p (e t) -> p e t", e=8)
        cmp = col(8, 128).rearrange("p (e j) -> p e j", e=8)
        nt = col(9, 8)
        endt = ring[:, 9 * 256 + 8:9 * 256 + 16]
        start = ring[:, 9 * 256 + 16:9 * 256 + 24]
        off = col(10).rearrange("p (t e) -> p t e", e=8)
        prod = [col(11 + k).rearrange("p (t e) -> p t e", e=8) for k in range(2)]
        posf = col(13, NT * 2).rearrange("p (k t) -> p k t", k=2)
        tcmp = ring[:, 14 * 256:14 * 256 + SLOT_TILES * 7].rearrange("p (j e) -> p j e", e=7)
        dif = ring[:, 13 * 256 + 64:13 * 256 + 96]
        edif = ring[:, 13 * 256 + 96:13 * 256 + 128]
        one = ring[:, 13 * 256 + 128:13 * 256 + 160]
        exf = ring[:, 13 * 256 + 160:13 * 256 + 160 + SLOT_TILES]
        LATE = 2 * (NE - EARLY)

        def late(i, part):
            return upc(2 * EARLY + i, part)

        def dnc(e, part):
            return w_dn[:, ds(e * (2 * DNW), 2 * DNW)].rearrange("p (k a d) -> p k a d", k=3, a=2)[:, :, part, :]

        def tiles3(e, s1, s2, s3, n):
            s1(0, 0, False)
            s1(1, 1, False), s2(0, 0, False)
            s1(2, 0, True), s2(1, 1, False), s3(0, 0, False)
            s1(3, 1, True), s2(2, 0, True), s3(1, 1, False)
            with e.Fori(0, n // 2 - 2) as i:
                for j in range(2):
                    k = i * 2 + j
                    s1(k + 4, j, True), s2(k + 3, 1 - j, True), s3(k + 2, j, True)
            s2(n - 1, 1, True), s3(n - 2, 0, True)
            s3(n - 1, 1, True)

        def none3(t, s, again):
            pass

        prep = nc.Block()
        prep.__enter__()

        @prep.sync
        def _(sp):
            for i in range(LATE + NE):
                if i >= 2:
                    sp.wait_ge(w2l, i - 1)
                o = (2 * EARLY + i) * CH if i < LATE else NE * UPW + (i - LATE) * DNW
                sp.dma_start(st_sm[i % 2], experts[:, o:o + CH]).then_inc(w2_in[i % 2], 16)

        @prep.scalar
        def _(act):
            act.wait_ge(st2, NT + 1)
            nc.scalar.activation(rstd[:, :], rstd[:, :], ACT.Sqrt).then_inc(rs2, 1)

            def s2(t, s, again):
                act.wait_ge(xn2_ready, t + 1)
                nc.scalar.activation(xs[:, ds(t, 1), 0:D], xn2[s].unsqueeze(1), ACT.Copy).then_inc(hi2, 1)
                act.wait_ge(t2_ready, t + 1)
                if again:
                    act.wait_ge(lg_ready, t - 1)
                nc.scalar.activation(xf[s], banks[s][:, 0:D].rearrange("p (k c) -> p k c", k=KD), ACT.Copy).then_inc(xf_ready, 1)

            tiles3(act, none3, s2, none3, NT)
            act.wait_ge(rch, 1)
            nc.scalar.activation(edif, dif, ACT.Exp).then_inc(ew, 1)
            for i in range(LATE + NE):
                act.wait_ge(w2_in[i % 2], (i // 2 + 1) * 16)
                if i < LATE:
                    nc.scalar.activation(late(i, 0), st_sm[i % 2], ACT.Copy, scale=XS_).then_inc(w2h, 1)
                else:
                    nc.scalar.activation(dnc(i - LATE, 0), st_sm[i % 2].rearrange("p (k d) -> p k d", k=3), ACT.Copy,
                                         scale=XS_).then_inc(w2h, 1)

        @prep.tensor
        def _(pe):
            pe.wait_ge(g_in, 16)

            def s2(t, s, again):
                pe.wait_ge(xn2_ready, t + 1)
                if again:
                    pe.wait_ge(xf_ready, t - 1)
                for c in range(KD):
                    m = nc.tensor.transpose(banks[s][:, c * P:(c + 1) * P], xn2[s][:, c * P:(c + 1) * P], idf[:, :])
                m.then_inc(t2_ready, 1)

            def s3(t, s, again):
                pe.wait_ge(xf_ready, t + 1)
                if again:
                    pe.wait_ge(lg_kept, t - 1)
                for c in range(KD):
                    m = nc.tensor.matmul(banks[2 + s][:, 0:8], xf[s][:, c, :], gate[:, c, :], start=(c == 0), stop=(c == KD - 1))
                m.then_inc(lg_ready, 1)

            tiles3(pe, none3, s2, s3, NT)
            pe.wait_ge(cnt_in, 1)
            nc.tensor.matmul(banks[4][:, 0:NT * 8], tri[:, :], m16, start=True, stop=True)
            nc.tensor.matmul(banks[5][:, 0:NT * 8], oneh[:, :], m16, start=True, stop=True).then_inc(cnt, 1)

        @prep.vector
        def _(dve):
            row_stats(dve, bn_done, st2, NT)
            dve.wait_ge(st2, NT)
            nc.vector.tensor_scalar(rstd[:, :], mv[:, :, 1], EPS, None, ALU.add).then_inc(st2, 1)
            dve.wait_ge(rs2, 1)
            nc.vector.reciprocal(rstd[:, :], rstd[:, :]).then_inc(rs2, 1)
            dve.wait_ge(rs2, 2)

            def s1(t, s, again):
                if again:
                    dve.wait_ge(t2_ready, t - 1)
                    dve.wait_ge(lo2, t - 1)
                nc.vector.tensor_scalar(xn2[s], xres[:, ds(t, 1), :].rearrange("p a d -> p (a d)"),
                                        mv[:, ds(t, 1), 0], rstd[:, ds(t, 1)], ALU.subtract, ALU.mult).then_inc(xn2_ready, 1)

            def s2(t, s, again):
                dve.wait_ge(hi2, t + 1)
                nc.vector.tensor_tensor(xs[:, ds(t, 1), D:2 * D], xn2[s].unsqueeze(1), xs[:, ds(t, 1), 0:D],
                                        ALU.subtract).then_inc(lo2, 1)

            def s3(t, s, again):
                dve.wait_ge(lg_ready, t + 1)
                nc.vector.tensor_copy(lg[:, ds(t, 1), :], banks[2 + s][:, 0:8].unsqueeze(1)).then_inc(lg_kept, 1)

            tiles3(dve, s1, s2, s3, NT)
            chain = [0]

            def link(ins):
                chain[0] += 1
                ins.then_inc(rch, 1)
                dve.wait_ge(rch, chain[0])

            dve.wait_ge(lg_kept, NT)
            for t in range(NT):
                nc.vector.max(v8[:, t, :], lg[:, t, :]).then_inc(top_v, 1)
            dve.wait_ge(top_v, NT)
            for t in range(NT):
                nc.vector.max_index(i8[:, t, :], v8[:, t, :], lg[:, t, :]).then_inc(top_i, 1)
            link(nc.vector.tensor_tensor(dif, v8[:, :, 1], v8[:, :, 0], ALU.subtract))
            dve.wait_ge(top_i, NT)
            link(nc.vector.tensor_copy(i8f, i8[:, :, 0:2]))
            for k in range(2):
                link(nc.vector.tensor_tensor(oh[k], iot[:, 0:8].unsqueeze(1).broadcast_to([P, NT, 8]),
                                             i8f[:, :, k:k + 1].broadcast_to([P, NT, 8]), ALU.is_equal))
            nc.vector.tensor_tensor(m16.rearrange("p (t e) -> p t e", e=8), oh[0], oh[1], ALU.add).then_inc(cnt_in, 1)
            link(nc.vector.memset(one, 1.0))
            dve.wait_ge(cnt, 1)
            link(nc.vector.tensor_copy(tot, banks[5][:, 0:NT * 8].rearrange("p (t e) -> p e t", e=8)))
            for e in range(8):
                link(nc.vector.tensor_tensor_scan(inc[:, e, :], one, tot[:, e, :], 0.0, ALU.mult, ALU.add))
            link(nc.vector.tensor_tensor(cmp, inc[:, :, NT - 1:NT].broadcast_to([P, 8, 16]),
                                         iot[:, SLOT_TILES:SLOT_TILES + 16].unsqueeze(1).broadcast_to([P, 8, 16]), ALU.is_gt))
            link(nc.vector.tensor_reduce(nt, cmp, AX.X, ALU.add))
            link(nc.vector.tensor_tensor_scan(endt, one[:, 0:8], nt, 0.0, ALU.mult, ALU.add))
            link(nc.vector.tensor_tensor(start, endt, nt, ALU.subtract))
            link(nc.vector.tensor_scalar(start, start, float(MT), None, ALU.mult))
            link(nc.vector.tensor_tensor(inc, inc, tot, ALU.subtract))
            link(nc.vector.tensor_tensor(inc, inc, start.unsqueeze(2).broadcast_to([P, 8, NT]), ALU.add))
            link(nc.vector.tensor_tensor(off, banks[4][:, 0:NT * 8].rearrange("p (t e) -> p t e", e=8),
                                         inc.rearrange("p e t -> p t e"), ALU.add))
            for k in range(2):
                link(nc.vector.tensor_tensor(prod[k], oh[k], off, ALU.mult))
                link(nc.vector.tensor_reduce(posf[:, k, :], prod[k], AX.X, ALU.add))
            link(nc.vector.tensor_copy(pos[:, :, :], posf))
            link(nc.vector.tensor_tensor(tcmp, iot[:, 0:SLOT_TILES].unsqueeze(2).broadcast_to([P, SLOT_TILES, 7]),
                                         endt[:, 0:7].unsqueeze(1).broadcast_to([P, SLOT_TILES, 7]), ALU.is_ge))
            link(nc.vector.tensor_reduce(exf, tcmp, AX.X, ALU.add))
            link(nc.vector.tensor_copy(exid[:, :], exf))
            dve.wait_ge(ew, 1)
            link(nc.vector.tensor_scalar(dif, edif, 1.0, None, ALU.add))
            link(nc.vector.reciprocal(dif, dif))
            link(nc.vector.tensor_scalar(wts[:, 0, :], dif, XS_ ** -2, None, ALU.mult))
            link(nc.vector.tensor_tensor(wts[:, 1, :], edif, wts[:, 0, :], ALU.mult))
            for i in range(LATE + NE):
                dve.wait_ge(w2h, i + 1)
                if i < LATE:
                    nc.vector.scalar_tensor_tensor(out=late(i, 1), in0=st_sm[i % 2], scalar=XS_, in1=late(i, 0),
                                                   op0=ALU.mult, op1=ALU.subtract).then_inc(w2l, 1)
                else:
                    nc.vector.scalar_tensor_tensor(out=dnc(i - LATE, 1), in0=st_sm[i % 2].rearrange("p (k d) -> p k d", k=3),
                                                   scalar=XS_, in1=dnc(i - LATE, 0), op0=ALU.mult, op1=ALU.subtract).then_inc(w2l, 1)

        prep.__exit__(None, None, None)

        def part(base, s, n):
            return ring[:, base + s * n:base + (s + 1) * n]
        XT = [part(0, s, 512).bitcast(F16).rearrange("p (a c t) -> p a c t", a=2, c=KD) for s in range(2)]
        SG = [part(1024, s, MT) for s in range(2)]
        HF = [part(1536, s, MT) for s in range(2)]
        HH = [part(2048, s, 384).bitcast(F16).rearrange("p (f t) -> p f t", f=3) for s in range(2)]
        HL = [part(2816, s, 384).bitcast(F16).rearrange("p (f t) -> p f t", f=3) for s in range(2)]
        xr = [accp[:, s, :].bitcast(F16).rearrange("p (u n) -> p u n", u=2) for s in range(2)]
        ys = [accd[:, s, :].rearrange("p (u d) -> p u d", u=2) for s in range(2)]
        gbuf = wide[:, UPC + DNC:UPC + DNC + NT * 2 * D].bitcast(F32)[:, 0:GS * D].rearrange("p (s d) -> p s d", s=GS)
        ST, RT = SHARED_TILES, SLOT_TILES

        def tiles(e, load, up, down, evac, first, n):
            load(0, 0, first)
            up(0, 0, first, lambda: load(1, 1, first + 1), None)
            up(1, 1, first + 1, lambda: load(2, 0, first + 2), lambda: (down(0, 0, first), evac(0, 0, first)))
            with e.Fori(0, n // 2 - 2) as i:
                for j in range(2):
                    k = i * 2 + (j + 2)
                    up(k, j, k + first, lambda: load(k + 1, 1 - j, k + (first + 1)),
                       lambda: (down(k - 1, 1 - j, k + (first - 1)), evac(k - 1, 1 - j, k + (first - 1))))
            k = n - 2
            up(k, 0, k + first, lambda: load(k + 1, 1, k + first + 1),
               lambda: (down(k - 1, 1, k + first - 1), evac(k - 1, 1, k + first - 1)))
            k = n - 1
            up(k, 1, k + first, None, lambda: (down(k - 1, 0, k + first - 1), evac(k - 1, 0, k + first - 1)))
            down(k, 1, k + first), evac(k, 1, k + first)

        def fs(s, f):
            return (s + f) % 2

        nothing = lambda *a: None

        moe = nc.Block()
        moe.__enter__()

        @moe.sync
        def _(sp):
            sp.wait_ge(scat, 16 * 2 * NT)
            for j in range(2):
                sp.dma_start(xr[j], slots[j * MT:(j + 1) * MT, :].rearrange("(u p) n -> p u n", p=P)).then_inc(xr_in[j], 16)
            with sp.Fori(0, RT // 2 - 1) as i:
                for j in range(2):
                    sp.wait_ge(xtT, i * 2 + (ST + j + 1))
                    sp.dma_start(xr[j], slots[ds((i * 2 + j + 2) * MT, MT), :].rearrange("(u p) n -> p u n", p=P)).then_inc(xr_in[j], 16)
            for c in range(8):
                sp.wait_ge(comb2, 4 * c + 4)
                sp.dma_start(out[c * 512:(c + 1) * 512, :].rearrange("(t p) d -> p t d", p=P),
                             xres[:, 4 * c:4 * c + 4, :]).then_inc(done, 16)
            sp.wait_ge(done, 128)

        @moe.gpsimd
        def _(pool):
            pool.wait_ge(z_out, 16 * 8)
            for t in range(NT):
                for k in range(2):
                    pool.indirect_dma_start(out=slots, out_offset=bass.IndirectOffsetOnAxis(ap=pos[:, k, t:t + 1], axis=0),
                                            in_=xs[:, t, :], in_offset=None).then_inc(scat, 16)
            pool.wait_ge(xte, ST + RT)
            pool.wait_ge(y_out[0], 16 * (RT // 2) + 16)
            pool.wait_ge(y_out[1], 16 * (RT // 2) + 16)
            for t in range(NT):
                for k in range(2):
                    i = 2 * t + k
                    if i >= GS:
                        pool.wait_ge(comb1 if k == 0 else comb2, (i - GS) // 2 + 1)
                    pool.indirect_dma_start(out=gbuf[:, i % GS, :], out_offset=None, in_=ydram,
                                            in_offset=bass.IndirectOffsetOnAxis(ap=pos[:, k, t:t + 1], axis=0)).then_inc(gat[i % GS], 16)

        @moe.scalar
        def _(act):
            for s in range(2):
                act.sem_inc(y_out[s], 16)
            def make(shared):
                def load(t, s, c):
                    act.wait_ge(xtT, c + 1)
                    nc.scalar.activation(XT[s], half(4 + s).rearrange("p (a c t) -> p a c t", a=2, c=KD), ACT.Copy).then_inc(xte, 1)

                def up(t, s, c, mid, late_):
                    for f in range(3):
                        act.wait_ge(g_ready, c * 3 + f + 1)
                        nc.scalar.activation(SG[fs(s, f)], banks[fs(s, f)][:, 0:MT], ACT.Silu, scale=1.0 / XS_).then_inc(silu, 1)
                        act.wait_ge(h_ready, c * 3 + f + 1)
                        nc.scalar.activation(HH[s][:, f, :], HF[fs(s, f)], ACT.Copy).then_inc(hh_ready, 1)
                        if f == 0 and mid:
                            mid()
                        if f == 1 and late_:
                            late_()

                def evac(t, s, c):
                    if shared:
                        return
                    act.wait_ge(y_ready, c + 1)
                    act.wait_ge(y_out[s], t * 8 - 8 * s + 16)
                    nc.scalar.activation(ys[s], banks[6 + s].rearrange("p (u d) -> p u d", u=2), ACT.Copy).then_inc(y_read, 1)
                    act.wait_ge(y_read, c + 1)
                    act.dma_start(ydram[ds(t * MT, MT), :].rearrange("(u p) d -> p u d", p=P), ys[s]).then_inc(y_out[s], 16)
                return load, up, nothing, evac

            tiles(act, *make(True), 0, ST)
            tiles(act, *make(False), ST, RT)

        @moe.vector
        def _(dve):
            def make(shared):
                def up(t, s, c, mid, late_):
                    for f in range(3):
                        dve.wait_ge(silu, c * 3 + f + 1)
                        dve.wait_ge(u_ready, c * 3 + f + 1)
                        nc.vector.tensor_tensor(HF[fs(s, f)], banks[2 + fs(s, f)][:, 0:MT], SG[fs(s, f)], ALU.mult).then_inc(h_ready, 1)
                        dve.wait_ge(hh_ready, c * 3 + f + 1)
                        nc.vector.tensor_tensor(HL[s][:, f, :], HF[fs(s, f)], HH[s][:, f, :], ALU.subtract).then_inc(hl_ready, 1)
                        if f == 1 and late_:
                            late_()

                def evac(t, s, c):
                    if not shared:
                        return
                    dve.wait_ge(y_ready, c + 1)
                    x2 = xres[:, ds(t * 2, 2), :].rearrange("p u d -> p (u d)")
                    nc.vector.scalar_tensor_tensor(out=x2, in0=banks[6 + s], scalar=XS_ ** -2, in1=x2,
                                                   op0=ALU.mult, op1=ALU.add).then_inc(y_read, 1)
                return nothing, up, nothing, evac

            tiles(dve, *make(True), 0, ST)
            tiles(dve, *make(False), ST, RT)
            for t in range(NT):
                for k in range(2):
                    i = 2 * t + k
                    dve.wait_ge(gat[i % GS], 16 * (i // GS + 1))
                    if k:
                        dve.wait_ge(comb1, t + 1)
                    nc.vector.scalar_tensor_tensor(out=xres[:, t, :], in0=gbuf[:, i % GS, :], scalar=wts[:, k, t:t + 1],
                                                   in1=xres[:, t, :], op0=ALU.mult, op1=ALU.add).then_inc(comb2 if k else comb1, 1)

        @moe.tensor
        def _(pe):
            def make(shared):
                def expert(t):
                    return NE - 1 if shared else pe.value_load(exid[0:1, ds(t, 1)], min_val=0, max_val=NE - 2)

                def load(t, s, c):
                    if not shared:
                        pe.wait_ge(xr_in[s], t * 8 + (16 - 8 * s))
                    if not (shared and isinstance(t, int) and t < 2):
                        pe.wait_ge(xte, c - 1)
                    for a in range(2):
                        for ch in range(KD):
                            for u in range(2):
                                src = xs[:, ds(t * 2 + u, 1), :].rearrange("p a n -> p (a n)") if shared else xr[s][:, u, :]
                                o = a * D + ch * P
                                j = (a * KD + ch) * 2 + u
                                m = nc.tensor.transpose(half(4 + s)[:, j * P:(j + 1) * P], src[:, o:o + P], idh[:, :])
                    m.then_inc(xtT, 1)

                def up(t, s, c, mid, late_):
                    pe.wait_ge(xte, c + 1)
                    e = expert(t)
                    for f in range(3):
                        for gu, sm_ in ((0, g_ready), (1, u_ready)):
                            b_ = banks[2 * gu + fs(s, f)][:, 0:MT]
                            if not (isinstance(c, int) and c * 3 + f < 2):
                                pe.wait_ge((silu, h_ready)[gu], c * 3 + (f - 1))
                            j = 0
                            for wp, xp in ((0, 0), (0, 1), (1, 0)):
                                for ch in range(KD):
                                    o = ch * 4 * FF + wp * 2 * FF + gu * FF + f * P
                                    m = nc.tensor.matmul(b_, w_up[:, ds(e * (2 * UPW) + o, P)], XT[s][:, xp, ch, :],
                                                         start=(j == 0), stop=(j == 5))
                                    j += 1
                            m.then_inc(sm_, 1)
                        if f == 0 and mid:
                            mid()
                        if f == 1 and late_:
                            late_()

                def down(t, s, c):
                    e = expert(t)
                    pe.wait_ge(hl_ready, c * 3 + 3)
                    if not (isinstance(c, int) and c < 2):
                        pe.wait_ge(y_read, c - 1)
                    for u in range(2):
                        j = 0
                        for f in range(3):
                            for hp_, wp in ((0, 0), (0, 1), (1, 0)):
                                hx = (HH, HL)[hp_][s]
                                m = nc.tensor.matmul(banks[6 + s][:, u * D:(u + 1) * D], hx[:, f, u * P:(u + 1) * P],
                                                     w_dn[:, ds(e * (2 * DNW) + (f * 2 + wp) * D, D)], start=(j == 0), stop=(j == 8))
                                j += 1
                    m.then_inc(y_ready, 1)
                return load, up, down, nothing

            tiles(pe, *make(True), 0, ST)
            tiles(pe, *make(False), ST, RT)

        moe.__exit__(None, None, None)


_INS = ["x", "wq", "bq", "wk", "bk", "wv", "bv", "wo", "bo", "freq", "gate_t", "experts"]


def kernel(L0_attn_x, L0_attn_Wq, L0_attn_bq, L0_attn_Wk, L0_attn_bk, L0_attn_Wv, L0_attn_bv, L0_attn_Wo, L0_attn_bo,
           L0_attn_nrope_freq, L0_ffn_gate_w, L0_ffn_w_up, L0_ffn_w_down, L0_ffn_sg_gate, L0_ffn_sg_up, L0_ffn_sg_down):
    import numpy as _np
    import concourse.bacc as _bacc
    from concourse import mybir as _mybir
    from concourse.bass_utils import run_bass_kernel_spmd as _run

    x = _np.asarray(L0_attn_x)
    D, P = x.shape[-1], 128
    sg = _np.concatenate([_np.asarray(L0_ffn_sg_gate), _np.asarray(L0_ffn_sg_up)], 0)[None]
    up = _np.concatenate([_np.asarray(L0_ffn_w_up), sg], 0)
    up = up.transpose(0, 2, 1).reshape(up.shape[0], D // P, P, -1).transpose(2, 0, 1, 3).reshape(P, -1)
    down = _np.concatenate([_np.asarray(L0_ffn_w_down), _np.asarray(L0_ffn_sg_down)[None]], 0)
    down = down.transpose(0, 2, 1).reshape(down.shape[0], -1, P, D).transpose(2, 0, 1, 3).reshape(P, -1)
    given = dict(x=x.reshape(-1, D), wq=L0_attn_Wq, bq=L0_attn_bq, wk=L0_attn_Wk, bk=L0_attn_bk, wv=L0_attn_Wv,
                 bv=L0_attn_bv, wo=L0_attn_Wo, bo=L0_attn_bo, freq=L0_attn_nrope_freq,
                 gate_t=_np.asarray(L0_ffn_gate_w).T, experts=_np.concatenate([up, down], 1))
    nc = _bacc.Bacc("TRN2", target_bir_lowering=False, num_devices=1)
    arrays, args = {}, []
    for name in _INS:
        a = _np.ascontiguousarray(given[name])
        arrays[f"in_{name}"] = a
        args.append(nc.dram_tensor(f"in_{name}", a.shape, _mybir.dt.from_np(a.dtype), kind="ExternalInput").ap())
    args.append(nc.dram_tensor("out_rows", (x.size // D, D), _mybir.dt.float32, kind="ExternalOutput").ap())
    add_ffn_kernel(nc, *args)
    r = _run(nc, [arrays], core_ids=[0])
    return r.results[0]["out_rows"].reshape(x.shape)
```

```python
import concourse.bass as bass
from concourse import mybir
from contextlib import ExitStack
import numpy as np


def add_ffn_kernel(nc, x, wq, bq, wk, bk, wv, bv, wo, bo, freq, gate_t, experts, out):
    F32, F16, I32, U32 = mybir.dt.float32, mybir.dt.float16, mybir.dt.int32, mybir.dt.uint32
    ALU, ACT, AX = mybir.AluOpType, mybir.ActivationFunctionType, mybir.AxisListType
    ds = bass.ds

    P = 128
    N, D = x.shape
    B, H, HD = 2, 4, 64
    T = N // B
    NT, TB = N // P, T // P
    KD = D // P
    QB = 512
    NQ = T // QB
    NK = T // P
    HP = H // 2
    NBLK = B * NQ * HP
    RH = HD // 4
    EPS = 1e-5
    AHEAD = 1
    GS = 16
    WS = 16.0
    XS_ = 32.0
    NE, FF = 9, 384
    UPW = KD * 2 * FF
    DNW = 3 * D
    EARLY = 6
    CH = 2 * FF
    MT = 256
    SHARED_TILES = N // MT
    S1 = 8
    SLOT_TILES = 2 * N // MT + 7
    SDT = (10000.0 - (1.0 - 17 / 100.0) * 10000.0) * 2.0
    MINB = (1.0 - 17 / 100.0) * 10000.0
    ROT = 2.0 * np.pi / (T - 1)

    ctx = ExitStack()
    with ctx:
        def sb(name, shape, dt):
            return ctx.enter_context(nc.sbuf_tensor(name, shape, dt))

        def sem(name):
            return ctx.enter_context(nc.semaphore(name))

        UP16 = EARLY * UPW * 2
        QK16 = H * T
        wide = sb("wide", [P, UP16 + 4 * QK16 + 2 * TB * D], F16)
        UPC, DNC = NE * UPW * 2, NE * DNW * 2
        w_up = wide[:, 0:UPC]
        w_dn = wide[:, UPC:UPC + DNC]
        xs = wide[:, UPC + DNC:UPC + DNC + NT * 2 * D].rearrange("p (t n) -> p t n", t=NT)
        K1 = wide[:, UP16:UP16 + QK16].rearrange("p (h t) -> p h t", h=H)
        K2 = wide[:, UP16 + QK16:UP16 + 2 * QK16].rearrange("p (h t) -> p h t", h=H)
        Q1 = wide[:, UP16 + 2 * QK16:UP16 + 3 * QK16].rearrange("p (h t) -> p h t", h=H)
        Q2 = wide[:, UP16 + 3 * QK16:UP16 + 4 * QK16].rearrange("p (h t) -> p h t", h=H)
        V = wide[:, UP16 + 4 * QK16:].bitcast(F32).rearrange("p (t d) -> p t d", t=TB)
        xres = sb("xres", [P, NT, D], F32)
        ring = sb("ring", [P, 4 * 2 * QB], F32)
        Pr = ring[:, :].rearrange("p (s h q) -> p s h q", s=4, h=2)
        accp = sb("accp", [P, 2, QB], F32)
        accd = sb("accd", [P, 2, QB], F32)
        pvraw = sb("pvraw", [P, QB], F32)
        recip = sb("recip", [P, QB], F32)
        OT = sb("OT", [P, HP, QB], F32)
        stage = sb("stage", [P, 2, CH], F32)
        wqkv = sb("wqkv", [P, 2, KD, 3 * D], F16)
        wo_sb = sb("wo_sb", [P, KD, D], F32)
        bias = sb("bias", [P, 3 * D], F32)
        bo_sb = sb("bo_sb", [P, D], F32)
        cos = sb("cos", [P, TB, RH], F32)
        sin = sb("sin", [P, TB, RH], F32)
        mt = sb("mt", [P, 2 * QB // P, P], F16)
        mx = sb("mx", [P, 2 * QB // P, T // 512], F32)
        m8 = sb("m8", [P, 2 * QB // P], F32)
        idf = sb("idf", [P, P], F32)
        idh = sb("idh", [P, P], F16)
        ones = sb("ones", [P, HD], F32)
        stats = sb("stats", [P, NT, 6], F32)
        mv = sb("mv", [P, NT, 2], F32)
        rstd = sb("rstd", [P, NT], F32)
        sm = sb("sm", [P, 8], F32)
        jpos = sb("jpos", [P, RH + TB], F32)
        ang = stage[:, 0, 0:TB * RH].rearrange("p (t j) -> p t j", t=TB)
        wst = ring[:, 0:KD * 3 * D].rearrange("p (k n) -> p k n", k=KD)
        def slot(base, s, n):
            return ring[:, base + s * n:base + (s + 1) * n]
        xn = [slot(0, s, D) for s in range(2)]
        xh = [slot(512, s, D).bitcast(F16).rearrange("p (a d) -> p a d", a=2) for s in range(2)]
        xT = [slot(1024, s, D).bitcast(F16).rearrange("p (a c) -> p a c", a=4) for s in range(2)]
        qk = [slot(1536, s, 2 * D) for s in range(2)]
        ra = slot(2560, 0, 256).rearrange("p (h c j) -> p h c j", h=2 * H, c=2)
        rb = slot(2816, 0, 256).rearrange("p (h c j) -> p h c j", h=2 * H, c=2)
        qtok = [slot(3072, s, 256).bitcast(F16).rearrange("p (h c) -> p h c", h=H) for s in range(2)]
        ktok = [slot(3584, s, 256).bitcast(F16).rearrange("p (h c) -> p h c", h=H) for s in range(2)]
        zt = sb("zt", [P, 2 * D], F16)
        gate = sb("gate", [P, KD, 8], F32)
        tri = sb("tri", [P, P], F16)
        oneh = sb("oneh", [P, P], F16)
        iot = sb("iot", [P, SLOT_TILES + 16 + 8], F32)
        pos = sb("pos", [P, 2, NT], U32)
        wts = sb("wts", [P, 2, NT], F32)
        exid = sb("exid", [P, SLOT_TILES], I32)
        slots = nc.dram_tensor("slots", (SLOT_TILES * MT, 2 * D), F16, kind="Internal").ap()
        ydram = nc.dram_tensor("ydram", (SLOT_TILES * MT, D), F32, kind="Internal").ap()
        qlo = [accp[:, s, 0:128].bitcast(F16).rearrange("p (h c) -> p h c", h=H) for s in range(2)]

        psum = ctx.enter_context(nc.psum_tensor("psum", [P, 8, 512], F32))
        banks = [psum[:, i, :] for i in range(8)]

        def half(i):
            return banks[i].bitcast(F16)

        def spair(s):
            return psum[:, 2 * s:2 * s + 2, :]
        xtp = [half(4 + s)[:, 0:512].rearrange("p (a c) -> p a c", a=4) for s in range(2)]
        q1ps = half(6)[:, 0:512].rearrange("p (h c) -> p h c", h=H)
        qlps = half(6)[0:HD, 512:1024].rearrange("p (h c) -> p h c", h=H)
        kps = half(7)[:, 0:512].rearrange("p (h c) -> p h c", h=H)
        mtps = half(7).rearrange("p (h c) -> p h c", h=2)
        pvps = banks[6]

        def upc(m, part):
            return w_up[:, ds(m * (4 * FF) + part * 2 * FF, 2 * FF)]

        x_in = sem("x_in"); w_in = sem("w_in"); b_in = sem("b_in"); k_in = sem("k_in")
        pset = sem("pset"); dset = sem("dset"); aset = sem("aset"); ln_ready = sem("ln_ready")
        dch = sem("dch"); bn_done = sem("bn_done")
        xn_ready = sem("xn_ready"); xhi_ready = sem("xhi_ready"); xlo_ready = sem("xlo_ready")
        xtp_ready = sem("xtp_ready"); xt_ready = sem("xt_ready")
        qkv_ready = sem("qkv_ready"); qk_ready = sem("qk_ready"); v_ready = sem("v_ready")
        ra_ready = sem("ra_ready"); rope_done = sem("rope_done")
        hi_done = sem("hi_done"); qlo_done = sem("qlo_done"); tr_q = sem("tr_q"); tr_k = sem("tr_k")
        q_stored = sem("q_stored"); k_stored = sem("k_stored")
        a_ready = sem("a_ready"); max_done = sem("max_done"); m8_done = sem("m8_done")
        negm = sem("negm"); mT_ready = sem("mT_ready"); mrow = sem("mrow")
        s_ready = sem("s_ready"); exp_done = sem("exp_done"); pv_done = sem("pv_done")
        pacc = sem("pacc"); dacc = sem("dacc"); accp_free = sem("accp_free")
        den_ready = sem("den_ready"); recip_done = sem("recip_done"); pv_copied = sem("pv_copied")
        ot_ready = sem("ot_ready"); wo_ready = sem("wo_ready"); wo_added = sem("wo_added")
        bo_added = sem("bo_added"); st_in = [sem(f"st_in{s}") for s in range(2)]; wh_done = sem("wh_done"); wl_done = sem("wl_done")
        z_out = sem("z_out"); done = sem("done"); g_in = sem("g_in")
        st2 = sem("st2"); rs2 = sem("rs2"); xn2_ready = sem("xn2_ready"); hi2 = sem("hi2"); lo2 = sem("lo2")
        t2_ready = sem("t2_ready"); xf_ready = sem("xf_ready"); lg_ready = sem("lg_ready"); top_v = sem("top_v")
        top_i = sem("top_i"); lg_kept = sem("lg_kept"); rch = sem("rch"); cnt_in = sem("cnt_in"); cnt = sem("cnt"); ew = sem("ew")
        routed = sem("routed"); w2_in = [sem(f"w2_in{s}") for s in range(2)]; w2h = sem("w2h"); w2l = sem("w2l")
        scat = sem("scat"); xr_in = [sem(f"xr_in{s}") for s in range(2)]; xtT = sem("xtT"); xte = sem("xte")
        g_ready = sem("g_ready"); u_ready = sem("u_ready"); silu = sem("silu"); h_ready = sem("h_ready")
        hh_ready = sem("hh_ready"); hl_ready = sem("hl_ready"); y_ready = sem("y_ready"); y_read = sem("y_read")
        y_out = [sem(f"y_out{s}") for s in range(2)]; gat = [sem(f"gat{s}") for s in range(GS)]
        comb1 = sem("comb1"); comb2 = sem("comb2")

        NORM, SPLIT, TURNX, PROJ, SPLITQK, STORE = 5, 4, 3, 2, 1, 0

        def reused(k):
            return not (isinstance(k, int) and k < 2)

        def schedule(e, b, *stages):
            def tick(k):
                for ahead, stage_ in stages:
                    if 0 <= k + ahead < TB:
                        stage_(b, k + ahead, (k + ahead) % 2)
            for k in range(-NORM, 0):
                tick(k)
            with e.Fori(0, (TB - NORM) // 2) as i:
                for j in range(2):
                    for ahead, stage_ in stages:
                        stage_(b, i * 2 + j + ahead, (j + ahead) % 2)
            for k in range((TB - NORM) // 2 * 2, TB):
                tick(k)

        def row_stats(dve, part_done, mv_done, before):
            for t in range(NT + 1):
                if t < NT:
                    nc.vector.bn_stats(stats[:, t, :], xres[:, t, :]).then_inc(part_done, 1)
                if t:
                    dve.wait_ge(part_done, before + t)
                    nc.vector.bn_aggr(mv[:, t - 1, :], stats[:, t - 1, :]).then_inc(mv_done, 1)

        ROWS = [1, 2, 3, 3, 3, 3, 3, 3, 3, 3, 3, 2, 0, 0, 0, 0]
        OUT0, OUT1, TURN = 6, 9, 13

        def rows_of(kt):
            return list(range(sum(ROWS[:kt]), sum(ROWS[:kt + 1])))

        def blocks(e, b, prologue, block, last):
            n = b * (NQ * HP)
            prologue(n, b)
            block(n, b, 0, 0, (0, 1), False, None)
            with e.Fori(0, NQ - 1) as q:
                m = b * (2 * NQ - 2) + q * 2
                block(n + q * 2 + 1, b, q, 1, (q + 1, 0), False, m)
                block(n + q * 2 + 2, b, q + 1, 0, (q + 1, 1), True, m + 1)
            block(n + 2 * NQ - 1, b, NQ - 1, 1, None, False, None)
            last(n, b)

        block_ = nc.Block()
        block_.__enter__()

        @block_.sync
        def _(sp):
            for c in range(4):
                sp.dma_start(xres[:, 8 * c:8 * c + 8, :],
                             x[c * 1024:(c + 1) * 1024, :].rearrange("(t p) d -> p t d", p=P)).then_inc(x_in, 16)
            for i, w in enumerate((wq, wk, wv)):
                sp.dma_start(wst[:, :, i * D:(i + 1) * D], w.rearrange("(k p) n -> p k n", p=P)).then_inc(w_in, 16)
            sp.dma_start(wo_sb[:, :, :], wo.rearrange("(k p) n -> p k n", p=P)).then_inc(k_in, 16)
            sp.dma_start(gate[:, :, :], gate_t.rearrange("(k p) e -> p k e", p=P)).then_inc(g_in, 16)
            sp.wait_ge(pset, 12)
            zrows = slots.rearrange("(c n p) d -> c p n d", p=P, n=13)
            for c in range(SLOT_TILES * MT // P // 13):
                sp.dma_start(zrows[c], zt[:, :].unsqueeze(1).broadcast_to([P, 13, 2 * D])).then_inc(z_out, 16)
            for i in range(2):
                sp.wait_ge(dset, 1)
                sp.dma_start(stage[:, i, :], experts[:, i * CH:(i + 1) * CH]).then_inc(st_in[i], 16)
            with sp.Fori(0, EARLY - 1) as i:
                for j in range(2):
                    sp.wait_ge(wl_done, i * 2 + j + 1)
                    sp.dma_start(stage[:, j, :], experts[:, ds((i * 2 + j + 2) * CH, CH)]).then_inc(st_in[j], 16)

        @block_.gpsimd
        def _(pool):
            pool.memset(idf[:, :], 0.0).then_inc(pset, 1)
            pool.memset(idh[:, :], 0.0).then_inc(pset, 1)
            pool.iota(jpos[:, 0:RH], pattern=[[1, RH]], base=0, channel_multiplier=0,
                      allow_small_or_imprecise_dtypes=True).then_inc(pset, 1)
            pool.iota(jpos[:, RH:RH + TB], pattern=[[P, TB]], base=0, channel_multiplier=1,
                      allow_small_or_imprecise_dtypes=True).then_inc(pset, 1)
            pool.wait_ge(pset, 4)
            for m in (idf, idh):
                pool.affine_select(out=m[:, :], in_=m[:, :], compare_op=ALU.not_equal, fill=1.0,
                                   base=0, pattern=[[-1, P]], channel_multiplier=1).then_inc(pset, 1)
            pool.memset(ones[:, :], 1.0).then_inc(pset, 1)
            pool.memset(mt[:, :, :].rearrange("p a c -> p (a c)").bitcast(U32), 0).then_inc(pset, 1)
            pool.wait_ge(pset, 8)
            pool.memset(K2[HD:P, :, :].rearrange("p a c -> p (a c)").bitcast(U32), 0).then_inc(pset, 1)
            pool.memset(Q2[HD:P, :, :].rearrange("p a c -> p (a c)").bitcast(U32), 0).then_inc(pset, 1)
            pool.wait_ge(pset, 10)
            pool.memset(K2[HD:HD + 1, :, :].rearrange("p a c -> p (a c)"), 1.0).then_inc(pset, 1)
            pool.wait_ge(pset, 11)
            pool.memset(zt[:, :].bitcast(U32), 0).then_inc(pset, 1)
            pool.memset(tri[:, :], 1.0).then_inc(pset, 1)
            pool.memset(oneh[:, :], 1.0).then_inc(pset, 1)
            pool.iota(iot[:, 0:SLOT_TILES], pattern=[[1, SLOT_TILES]], base=0, channel_multiplier=0,
                      allow_small_or_imprecise_dtypes=True).then_inc(pset, 1)
            pool.iota(iot[:, SLOT_TILES:SLOT_TILES + 16], pattern=[[MT, 16]], base=0, channel_multiplier=0,
                      allow_small_or_imprecise_dtypes=True).then_inc(pset, 1)
            pool.wait_ge(pset, 16)
            pool.affine_select(out=tri[:, :], in_=tri[:, :], compare_op=ALU.is_gt, fill=0.0,
                               base=0, pattern=[[1, P]], channel_multiplier=-1).then_inc(pset, 1)
            pool.sem_inc(accp_free, 1)
            for ahead in (rope_done, pacc):
                pool.sem_inc(ahead, AHEAD)

            def none(b, k, s):
                pass

            def rope(b, k, s):
                g = b * TB + k
                X = qk[s].rearrange("p (h c j) -> p h c j", h=2 * H, c=4)[:, :, 2:4, :]
                cb = cos[:, ds(k, 1), :].unsqueeze(2).broadcast_to([P, 2 * H, 2, RH])
                sbb = sin[:, ds(k, 1), :].unsqueeze(2).broadcast_to([P, 2 * H, 2, RH])
                pool.wait_ge(qk_ready, g + 1)
                pool.wait_ge(rope_done, (g) * 2 + AHEAD)
                pool.tensor_tensor(ra, X, cb, ALU.mult).then_inc(ra_ready, 1)
                pool.tensor_tensor(rb, X, sbb, ALU.mult).then_inc(ra_ready, 1)
                pool.wait_ge(ra_ready, (g + 1) * 2)
                pool.tensor_tensor(X[:, :, 0, :], ra[:, :, 0, :], rb[:, :, 1, :], ALU.subtract).then_inc(rope_done, 1)
                pool.tensor_tensor(X[:, :, 1, :], ra[:, :, 1, :], rb[:, :, 0, :], ALU.add).then_inc(rope_done, 1)

            def prologue(n, b):
                pool.wait_ge(xn_ready, b * TB + TB)
                bo4 = bo_sb[:, :].unsqueeze(1).broadcast_to([P, 4, D])
                for c in range(4):
                    xs = xres[:, ds(b * TB + 4 * c, 4), :]
                    pool.tensor_tensor(xs, xs, bo4, ALU.add).then_inc(bo_added, 1)

            def block(n, b, q, hp, nxt, add, m):
                pool.wait_ge(accp_free, n + 1)
                for j in range(1, 13):
                    pool.wait_ge(exp_done, n * NK + j + 1)
                    if j == 1:
                        pool.tensor_tensor(accp[:, :, :], Pr[:, 0, :, :], Pr[:, 1, :, :], ALU.add).then_inc(pacc, 1)
                    else:
                        pool.wait_ge(pacc, n * 12 + j - 1 + AHEAD)
                        pool.tensor_tensor(accp[:, :, :], accp[:, :, :], Pr[:, j % 4, :, :], ALU.add).then_inc(pacc, 1)

            pool.wait_ge(dch, 10)
            pool.wait_ge(k_in, 16)
            pool.wait_ge(b_in, 80)
            with pool.Fori(0, B) as b:
                schedule(pool, b, (PROJ, rope))
                blocks(pool, b, prologue, block, lambda n, b: None)

        @block_.scalar
        def _(act):
            for ahead in (q_stored, pv_copied):
                act.sem_inc(ahead, AHEAD)
            act.dma_start(sm[:, 0:1], freq.rearrange("(a n) -> a n", a=1).broadcast_to([P, 1])).then_inc(b_in, 16)
            for i, v in enumerate((bq, bk, bv)):
                act.dma_start(bias[:, i * D:(i + 1) * D],
                              v.rearrange("(a n) -> a n", a=1).broadcast_to([P, D])).then_inc(b_in, 16)
            act.dma_start(bo_sb[:, :], bo.rearrange("(a n) -> a n", a=1).broadcast_to([P, D])).then_inc(b_in, 16)
            act.wait_ge(b_in, 80)
            nc.scalar.activation(sm[:, 1:2], sm[:, 0:1], ACT.Exp, scale=-1.0).then_inc(aset, 1)
            act.wait_ge(dch, 3)
            nc.scalar.activation(sm[:, 5:6], sm[:, 4:5], ACT.Ln).then_inc(aset, 1)
            act.wait_ge(dch, 4)
            nc.scalar.activation(jpos[:, 0:RH], jpos[:, 0:RH], ACT.Exp, scale=-1.0 / RH).then_inc(aset, 1)
            act.wait_ge(dch, 7)
            nc.scalar.activation(sin[:, :, :], sin[:, :, :], ACT.Sin).then_inc(aset, 1)
            act.wait_ge(dch, 8)
            nc.scalar.activation(cos[:, :, :], cos[:, :, :], ACT.Sin).then_inc(aset, 1)
            act.wait_ge(ln_ready, 1)
            nc.scalar.activation(rstd[:, :], rstd[:, :], ACT.Sqrt).then_inc(aset, 1)
            act.wait_ge(w_in, 48)
            nc.scalar.activation(wqkv[:, 0, :, :], wst, ACT.Copy, scale=WS).then_inc(aset, 1)

            def s1(b, k, s):
                g = b * TB + k
                act.wait_ge(xn_ready, g + 1)
                if reused(k):
                    act.wait_ge(xtp_ready, g - 1)
                nc.scalar.activation(xh[s][:, 0, :], xn[s], ACT.Copy).then_inc(xhi_ready, 1)

            def s1b(b, k, s):
                g = b * TB + k
                act.wait_ge(xtp_ready, g + 1)
                if reused(k):
                    act.wait_ge(qkv_ready, g - 1)
                nc.scalar.activation(xT[s], xtp[s], ACT.Copy).then_inc(xt_ready, 1)

            def s3(b, k, s):
                g = b * TB + k
                act.wait_ge(rope_done, (g + 1) * 2 + AHEAD)
                qv = qk[s][:, 0:D].rearrange("p (h c) -> p h c", h=H)
                kv = qk[s][:, D:2 * D].rearrange("p (h c) -> p h c", h=H)
                nc.scalar.activation(qtok[s].rearrange("p h (a c) -> p h a c", a=2),
                                     qv.unsqueeze(2).broadcast_to([P, H, 2, HD]), ACT.Copy).then_inc(hi_done, 1)
                nc.scalar.activation(ktok[s][:, :, 0:HD], kv, ACT.Copy).then_inc(hi_done, 1)

            def s3b(b, k, s):
                g = b * TB + k
                act.wait_ge(tr_q, g + 1)
                nc.scalar.activation(Q1[:, :, ds(k * P, P)], q1ps, ACT.Copy).then_inc(q_stored, 1)
                nc.scalar.activation(Q2[0:HD, :, ds(k * P, P)], qlps, ACT.Copy).then_inc(q_stored, 1)

            def none(*a):
                pass

            def block(n, b, q, hp, nxt, add, m):
                for kt in range(NK):
                    act.wait_ge(s_ready, n * NK + kt + 1)
                    if kt == 0:
                        act.wait_ge(pacc, n * 12 + AHEAD)
                    elif kt < 3:
                        act.wait_ge(dacc, n * 3 + 1)
                    elif kt == 3:
                        act.wait_ge(dacc, n * 3 + 3)
                    else:
                        act.wait_ge(pacc, n * 12 + max(kt - 4, 1) + AHEAD)
                    nc.scalar.activation(Pr[:, kt % 4, :, :], spair(kt % 2), ACT.Exp, scale=HD ** -0.5).then_inc(exp_done, 1)
                    if kt == 5 and m is not None:
                        act.wait_ge(st_in[1 - hp], b * ((NQ - 1) * 16) + (q + (hp == 1)) * 16)
                        nc.scalar.activation(upc(m, 0), stage[:, 1 - hp, :], ACT.Copy, scale=XS_).then_inc(wh_done, 1)
                act.wait_ge(pv_done, n + 1)
                act.wait_ge(ot_ready, n + AHEAD)
                nc.scalar.activation(pvraw[:, :], pvps, ACT.Copy).then_inc(pv_copied, 1)

            with act.Fori(0, B) as b:
                schedule(act, b, (SPLIT, s1), (TURNX, s1b), (SPLITQK, s3), (STORE, s3b))
                blocks(act, b, none, block, none)

        @block_.vector
        def _(dve):
            chain = [0]

            def link(ins):
                chain[0] += 1
                ins.then_inc(dch, 1)
                dve.wait_ge(dch, chain[0])

            dve.wait_ge(aset, 1)
            link(nc.vector.tensor_scalar(sm[:, 2:3], sm[:, 1:2], 1.0, None, ALU.add))
            link(nc.vector.reciprocal(sm[:, 3:4], sm[:, 2:3]))
            link(nc.vector.tensor_scalar(sm[:, 4:5], sm[:, 3:4], SDT, MINB, ALU.mult, ALU.add))
            dve.wait_ge(aset, 2)
            dve.wait_ge(pset, 4)
            link(nc.vector.tensor_scalar(jpos[:, 0:RH], jpos[:, 0:RH], sm[:, 5:6], None, ALU.mult))
            dve.wait_ge(aset, 3)
            link(nc.vector.tensor_tensor(ang, jpos[:, RH:RH + TB].unsqueeze(2).broadcast_to([P, TB, RH]),
                                         jpos[:, 0:RH].unsqueeze(1).broadcast_to([P, TB, RH]), ALU.mult))
            PI = 3.1415925
            link(nc.vector.tensor_scalar(sin[:, :, :], ang, -ROT, float(np.pi), ALU.mult, ALU.add))
            link(nc.vector.tensor_scalar(sin[:, :, :], sin[:, :, :], PI, -PI, ALU.min, ALU.max))
            link(nc.vector.tensor_scalar(cos[:, :, :], ang, ROT / 2, PI, ALU.mult, ALU.min))
            dve.wait_ge(aset, 5)
            link(nc.vector.tensor_tensor(cos[:, :, :], cos[:, :, :], cos[:, :, :], ALU.mult))
            link(nc.vector.tensor_scalar(cos[:, :, :], cos[:, :, :], -2.0, 1.0, ALU.mult, ALU.add))
            dve.wait_ge(x_in, 64)
            row_stats(dve, bn_done, dset, 0)
            dve.wait_ge(dset, NT)
            nc.vector.tensor_scalar(rstd[:, :], mv[:, :, 1], EPS, None, ALU.add).then_inc(ln_ready, 1)
            dve.wait_ge(aset, 6)
            nc.vector.reciprocal(rstd[:, :], rstd[:, :]).then_inc(ln_ready, 1)
            dve.wait_ge(aset, 7)
            nc.vector.scalar_tensor_tensor(out=wqkv[:, 1, :, :].rearrange("p k n -> p (k n)"),
                                           in0=wst.rearrange("p k n -> p (k n)"), scalar=WS,
                                           in1=wqkv[:, 0, :, :].rearrange("p k n -> p (k n)"),
                                           op0=ALU.mult, op1=ALU.subtract).then_inc(ln_ready, 1)
            dve.wait_ge(ln_ready, 3)
            dve.wait_ge(b_in, 80)
            nc.vector.sem_inc(dacc, 3)
            for ahead in (ot_ready, recip_done, k_stored, wo_added):
                dve.sem_inc(ahead, AHEAD)

            def s1(b, k, s):
                g = b * TB + k
                if reused(k):
                    dve.wait_ge(xlo_ready, g - 1)
                nc.vector.tensor_scalar(xn[s], xres[:, ds(g, 1), :].rearrange("p a d -> p (a d)"),
                                        mv[:, ds(g, 1), 0], rstd[:, ds(g, 1)], ALU.subtract, ALU.mult).then_inc(xn_ready, 1)

            def s1b(b, k, s):
                g = b * TB + k
                dve.wait_ge(xhi_ready, g + 1)
                nc.vector.tensor_tensor(xh[s][:, 1, :], xn[s], xh[s][:, 0, :], ALU.subtract).then_inc(xlo_ready, 1)

            def s2(b, k, s):
                g = b * TB + k
                dve.wait_ge(qkv_ready, g + 1)
                if reused(k):
                    dve.wait_ge(qlo_done, (g - 1) * 2)
                nc.vector.scalar_tensor_tensor(out=qk[s], in0=banks[2 * s], scalar=1.0 / WS, in1=bias[:, 0:2 * D],
                                               op0=ALU.mult, op1=ALU.add).then_inc(qk_ready, 1)
                nc.vector.scalar_tensor_tensor(out=V[:, ds(k, 1), :].rearrange("p a d -> p (a d)"),
                                               in0=banks[2 * s + 1][:, 0:D], scalar=1.0 / WS,
                                               in1=bias[:, 2 * D:3 * D], op0=ALU.mult, op1=ALU.add).then_inc(v_ready, 1)

            def s3(b, k, s):
                g = b * TB + k
                dve.wait_ge(hi_done, (g + 1) * 2)
                qv = qk[s][:, 0:D].rearrange("p (h c) -> p h c", h=H)
                kv = qk[s][:, D:2 * D].rearrange("p (h c) -> p h c", h=H)
                nc.vector.tensor_tensor(qlo[s][:, :, :], qv, qtok[s][:, :, 0:HD], ALU.subtract).then_inc(qlo_done, 1)
                nc.vector.tensor_tensor(ktok[s][:, :, HD:P], kv, ktok[s][:, :, 0:HD], ALU.subtract).then_inc(qlo_done, 1)

            def s3b(b, k, s):
                g = b * TB + k
                dve.wait_ge(tr_k, g + 1)
                nc.vector.tensor_copy(K1[:, :, ds(k * P, P)], kps).then_inc(k_stored, 1)
                nc.vector.tensor_copy(K2[0:HD, :, ds(k * P, P)], kps[0:HD]).then_inc(k_stored, 1)

            def row_max(n, a):
                dve.wait_ge(a_ready, n * 32 + a + 1)
                nc.vector.tensor_reduce(mx[:, a // 4, a % 4:a % 4 + 1], banks[4 + a % 2][:, :], AX.X, ALU.max).then_inc(max_done, 1)

            def max_col(n):
                dve.wait_ge(max_done, (n + 1) * 32)
                nc.vector.tensor_reduce(m8[:, :], mx[:, :, :], AX.X, ALU.max).then_inc(m8_done, 1)
                dve.wait_ge(m8_done, n + 1)
                nc.vector.tensor_scalar(mt[:, :, HD:HD + 1], m8[:, :].unsqueeze(2), -1.0, None, ALU.mult).then_inc(negm, 1)

            def max_row(n, b, q, hp):
                dve.wait_ge(mT_ready, n + 1)
                nc.vector.tensor_copy(Q2[HD:HD + 1, 2 * hp:2 * hp + 2, ds(q * QB, QB)], mtps[HD:HD + 1]).then_inc(mrow, 1)

            def reciprocals(n, j):
                dve.wait_ge(den_ready, n + AHEAD)
                nc.vector.reciprocal(recip[:, j * P:(j + 1) * P], banks[7][:, j * P:(j + 1) * P]).then_inc(recip_done, 1)

            def normed(n, hp):
                dve.wait_ge(recip_done, n * 4 + AHEAD)
                dve.wait_ge(pv_copied, n + AHEAD)
                nc.vector.tensor_tensor(OT[:, hp, :], pvraw[:, :], recip[:, :], ALU.mult).then_inc(ot_ready, 1)

            def add_out(b, q, r):
                dve.wait_ge(wo_ready, (b * NQ + q) * 2 + r + 1)
                xs = xres[:, ds(b * TB + q * 4 + 2 * r, 2), :]
                nc.vector.tensor_tensor(xs, banks[7][:, :].rearrange("p (a d) -> p a d", a=2), xs, ALU.add).then_inc(wo_added, 1)

            def prologue(n, b):
                for a in range(32):
                    row_max(n, a)
                max_col(n)
                max_row(n, b, 0, 0)

            def block(n, b, q, hp, nxt, add, m):
                for kt in range(NK):
                    if kt < 4 and (hp or add):
                        reciprocals(n, kt)
                    if kt == 4 and (hp or add):
                        normed(n, 1 - hp)
                    if nxt:
                        for a in rows_of(kt):
                            row_max(n + 1, a)
                    if add and kt == OUT0:
                        dve.wait_ge(bo_added, b * 4 + 4)
                        add_out(b, q - 1, 0)
                    if add and kt == OUT1:
                        add_out(b, q - 1, 1)
                    if nxt and kt == 11:
                        max_col(n + 1)
                    if nxt and kt == TURN:
                        max_row(n + 1, b, *nxt)
                    if kt == 12 and m is not None:
                        dve.wait_ge(wh_done, m + 1)
                        nc.vector.scalar_tensor_tensor(out=upc(m, 1), in0=stage[:, 1 - hp, :], scalar=XS_, in1=upc(m, 0),
                                                       op0=ALU.mult, op1=ALU.subtract).then_inc(wl_done, 1)
                    if kt == 14:
                        dve.wait_ge(exp_done, n * NK + 15)
                        nc.vector.tensor_tensor(accd[:, :, :], Pr[:, 1, :, :], Pr[:, 2, :, :], ALU.add).then_inc(dacc, 1)
                        dve.wait_ge(pacc, n * 12 + 12 + AHEAD)
                        dve.wait_ge(dacc, n * 3 + 4)
                        nc.vector.tensor_tensor(accd[:, :, :], accd[:, :, :], accp[:, :, :], ALU.add).then_inc(dacc, 1)
                        dve.wait_ge(dacc, n * 3 + 5)
                        nc.vector.sem_inc(accp_free, 1)
                dve.wait_ge(exp_done, n * NK + 16)
                nc.vector.tensor_tensor(accd[:, :, :], accd[:, :, :], Pr[:, 3, :, :], ALU.add).then_inc(dacc, 1)

            def last(n, b):
                for j in range(4):
                    reciprocals(n + 8, j)
                normed(n + 8, 1)
                for r in range(2):
                    add_out(b, NQ - 1, r)

            with dve.Fori(0, B) as b:
                schedule(dve, b, (NORM, s1), (SPLIT, s1b), (PROJ, s2), (STORE, s3b), (SPLITQK, s3))
                blocks(dve, b, prologue, block, last)

        @block_.tensor
        def _(pe):
            pe.sem_inc(den_ready, AHEAD)
            pe.wait_ge(pset, 17)
            pe.wait_ge(ln_ready, 3)
            pe.wait_ge(k_in, 16)

            def s1(b, k, s):
                g = b * TB + k
                pe.wait_ge(xlo_ready, g + 1)
                if reused(k):
                    pe.wait_ge(xt_ready, g - 1)
                for a in range(4):
                    m = nc.tensor.transpose(xtp[s][:, a, :], xh[s][:, a // 2, (a % 2) * P:(a % 2 + 1) * P], idh[:, :])
                m.then_inc(xtp_ready, 1)

            def s2(b, k, s):
                g = b * TB + k
                pe.wait_ge(xt_ready, g + 1)
                if reused(k):
                    pe.wait_ge(v_ready, g - 1)
                parts = [(xp, wp, c) for xp, wp in ((0, 0), (0, 1), (1, 0)) for c in range(KD)]
                for o, (bank, lo, hi) in enumerate(((2 * s, 0, 2 * D), (2 * s + 1, 2 * D, 3 * D))):
                    for j, (xp, wp, c) in enumerate(parts):
                        m = nc.tensor.matmul(banks[bank][:, 0:hi - lo], xT[s][:, 2 * xp + c, :], wqkv[:, wp, c, lo:hi],
                                             start=(j == 0), stop=(j == len(parts) - 1))
                m.then_inc(qkv_ready, 1)

            def s3(b, k, s):
                g = b * TB + k
                pe.wait_ge(qlo_done, (g + 1) * 2)
                pe.wait_ge(k_stored, g * 2 + AHEAD)
                for h in range(H):
                    m = nc.tensor.transpose(kps[:, h, :], ktok[s][:, h, :], idh[:, :])
                m.then_inc(tr_k, 1)
                pe.wait_ge(q_stored, g * 2 + AHEAD)
                for h in range(H):
                    nc.tensor.transpose(q1ps[:, h, :], qtok[s][:, h, :], idh[:, :])
                for h in range(H):
                    m = nc.tensor.transpose(qlps[:, h, :], qlo[s][:, h, :], idh[:, :])
                m.then_inc(tr_q, 1)

            def a_mm(n, q, hp, a):
                hh, qt, kc = a // 16, a // 4 % 4, a % 4
                h = 2 * hp + hh
                if a >= 2:
                    pe.wait_ge(max_done, n * 32 + a - 1)
                nc.tensor.matmul(banks[4 + a % 2][:, :], Q1[:, h, ds(q * QB + qt * P, P)], K1[:, h, kc * 512:(kc + 1) * 512],
                                 start=True, stop=True).then_inc(a_ready, 1)

            def m_turn(n):
                pe.wait_ge(negm, n + 1)
                for j in range(8):
                    m = nc.tensor.transpose(mtps[:, j // 4, (j % 4) * P:(j % 4 + 1) * P], mt[:, j, :], idh[:, :])
                m.then_inc(mT_ready, 1)

            def scores(n, q, hp, kt, between=None):
                for hh in range(2):
                    if hh and between:
                        between()
                    h = 2 * hp + hh
                    o = banks[2 * (kt % 2) + hh][:, :]
                    nc.tensor.matmul(o, K1[:, h, kt * P:(kt + 1) * P], Q1[:, h, ds(q * QB, QB)], start=True, stop=False)
                    m = nc.tensor.matmul(o, K2[:, h, kt * P:(kt + 1) * P], Q2[:, h, ds(q * QB, QB)], start=False, stop=True)
                m.then_inc(s_ready, 1)

            def sums(n):
                pe.wait_ge(dacc, n * 3 + 3)
                for hh in range(2):
                    m = nc.tensor.matmul(banks[7][hh * HD:(hh + 1) * HD, :], ones[:, :], accd[:, hh, :], start=True, stop=True)
                m.then_inc(den_ready, 1)

            def out_proj(b, q, r):
                for j in range(2):
                    c = 2 * r + j
                    for hp in range(HP):
                        m = nc.tensor.matmul(banks[7][:, j * D:(j + 1) * D], OT[:, hp, c * P:(c + 1) * P], wo_sb[:, hp, :],
                                             start=(hp == 0), stop=(hp == HP - 1))
                m.then_inc(wo_ready, 1)

            def prologue(n, b):
                pe.wait_ge(q_stored, (b + 1) * (2 * TB) + AHEAD)
                pe.wait_ge(k_stored, (b + 1) * (2 * TB) + AHEAD)
                for a in range(32):
                    a_mm(n, 0, 0, a)
                pe.wait_ge(wo_added, b * (2 * NQ) + AHEAD)
                m_turn(n)
                pe.wait_ge(mrow, n + 1)
                scores(n, 0, 0, 0)
                scores(n, 0, 0, 1)

            def block(n, b, q, hp, nxt, add, m):
                for kt in range(NK):
                    rows = rows_of(kt) if nxt else []

                    def next_row():
                        if rows:
                            a_mm(n + 1, nxt[0], nxt[1], rows.pop(0))
                    if add and kt == OUT0:
                        pe.wait_ge(ot_ready, n + AHEAD)
                        out_proj(b, q - 1, 0)
                    if add and kt == OUT1:
                        pe.wait_ge(wo_added, (b * NQ + q - 1) * 2 + 1 + AHEAD)
                        out_proj(b, q - 1, 1)
                    if nxt and kt == TURN:
                        if add:
                            pe.wait_ge(wo_added, (b * NQ + q) * 2 + AHEAD)
                        elif hp:
                            pe.wait_ge(recip_done, n * 4 + AHEAD)
                        m_turn(n + 1)
                    if kt:
                        next_row()
                    pe.wait_ge(exp_done, n * NK + kt + 1)
                    if kt == 0:
                        pe.wait_ge(pv_copied, n + AHEAD)
                    for hh in range(2):
                        h = 2 * hp + hh
                        m = nc.tensor.matmul(banks[6][hh * HD:(hh + 1) * HD, :], V[:, kt, h * HD:(h + 1) * HD],
                                             Pr[:, kt % 4, hh, :], start=(kt == 0), stop=(kt == NK - 1))
                    if kt == NK - 1:
                        m.then_inc(pv_done, 1)
                    if kt == 0 and (hp or add):
                        sums(n)
                    next_row()
                    if kt < NK - 2:
                        scores(n, q, hp, kt + 2, next_row)
                    elif nxt:
                        if kt == NK - 2:
                            pe.wait_ge(mrow, n + 2)
                        scores(n + 1, nxt[0], nxt[1], kt + 2 - NK, next_row)
                    while rows:
                        next_row()
            def last(n, b):
                sums(n + 8)
                pe.wait_ge(ot_ready, n + 8 + AHEAD)
                out_proj(b, NQ - 1, 0)
                pe.wait_ge(wo_added, (b * NQ + NQ - 1) * 2 + 1 + AHEAD)
                out_proj(b, NQ - 1, 1)

            with pe.Fori(0, B) as b:
                schedule(pe, b, (TURNX, s1), (PROJ, s2), (STORE, s3))
                blocks(pe, b, prologue, block, last)

        block_.__exit__(None, None, None)

        xn2 = [pvraw[:, s * D:(s + 1) * D] for s in range(2)]
        xf = [recip[:, s * D:(s + 1) * D].rearrange("p (k c) -> p k c", k=KD) for s in range(2)]
        st_sm = [stage[:, s, :] for s in range(2)]
        col = lambda i, n=NT * 8: ring[:, i * 256:i * 256 + n]
        lg = col(12).rearrange("p (t e) -> p t e", e=8)
        v8 = col(0).rearrange("p (t e) -> p t e", e=8)
        i8 = col(1).bitcast(U32).rearrange("p (t e) -> p t e", e=8)
        i8f = col(2, NT * 2).rearrange("p (t k) -> p t k", k=2)
        oh = [col(3 + k).rearrange("p (t e) -> p t e", e=8) for k in range(2)]
        m16 = col(5, 128).bitcast(F16)
        tot = col(6).rearrange("p (e t) -> p e t", e=8)
        inc = col(7).rearrange("p (e t) -> p e t", e=8)
        cmp = col(8, 128).rearrange("p (e j) -> p e j", e=8)
        nt = col(9, 8)
        endt = ring[:, 9 * 256 + 8:9 * 256 + 16]
        start = ring[:, 9 * 256 + 16:9 * 256 + 24]
        off = col(10).rearrange("p (t e) -> p t e", e=8)
        prod = [col(11 + k).rearrange("p (t e) -> p t e", e=8) for k in range(2)]
        posf = col(13, NT * 2).rearrange("p (k t) -> p k t", k=2)
        tcmp = ring[:, 14 * 256:14 * 256 + SLOT_TILES * 7].rearrange("p (j e) -> p j e", e=7)
        dif = ring[:, 13 * 256 + 64:13 * 256 + 96]
        edif = ring[:, 13 * 256 + 96:13 * 256 + 128]
        one = ring[:, 13 * 256 + 128:13 * 256 + 160]
        exf = ring[:, 13 * 256 + 160:13 * 256 + 160 + SLOT_TILES]
        LATE = 2 * (NE - EARLY)

        def late(i, part):
            return upc(2 * EARLY + i, part)

        def dnc(e, part):
            return w_dn[:, ds(e * (2 * DNW), 2 * DNW)].rearrange("p (k a d) -> p k a d", k=3, a=2)[:, :, part, :]

        def tiles3(e, s1, s2, s3, n):
            s1(0, 0, False)
            s1(1, 1, False), s2(0, 0, False)
            s1(2, 0, True), s2(1, 1, False), s3(0, 0, False)
            s1(3, 1, True), s2(2, 0, True), s3(1, 1, False)
            with e.Fori(0, n // 2 - 2) as i:
                for j in range(2):
                    k = i * 2 + j
                    s1(k + 4, j, True), s2(k + 3, 1 - j, True), s3(k + 2, j, True)
            s2(n - 1, 1, True), s3(n - 2, 0, True)
            s3(n - 1, 1, True)

        def none3(t, s, again):
            pass

        prep = nc.Block()
        prep.__enter__()

        @prep.sync
        def _(sp):
            for i in range(LATE + NE):
                if i >= 2:
                    sp.wait_ge(w2l, i - 1)
                o = (2 * EARLY + i) * CH if i < LATE else NE * UPW + (i - LATE) * DNW
                sp.dma_start(st_sm[i % 2], experts[:, o:o + CH]).then_inc(w2_in[i % 2], 16)

        @prep.scalar
        def _(act):
            act.wait_ge(st2, NT + 1)
            nc.scalar.activation(rstd[:, :], rstd[:, :], ACT.Sqrt).then_inc(rs2, 1)

            def s2(t, s, again):
                act.wait_ge(xn2_ready, t + 1)
                nc.scalar.activation(xs[:, ds(t, 1), 0:D], xn2[s].unsqueeze(1), ACT.Copy).then_inc(hi2, 1)
                act.wait_ge(t2_ready, t + 1)
                if again:
                    act.wait_ge(lg_ready, t - 1)
                nc.scalar.activation(xf[s], banks[s][:, 0:D].rearrange("p (k c) -> p k c", k=KD), ACT.Copy).then_inc(xf_ready, 1)

            tiles3(act, none3, s2, none3, NT)
            act.wait_ge(rch, 1)
            nc.scalar.activation(edif, dif, ACT.Exp).then_inc(ew, 1)
            for i in range(LATE + NE):
                act.wait_ge(w2_in[i % 2], (i // 2 + 1) * 16)
                if i < LATE:
                    nc.scalar.activation(late(i, 0), st_sm[i % 2], ACT.Copy, scale=XS_).then_inc(w2h, 1)
                else:
                    nc.scalar.activation(dnc(i - LATE, 0), st_sm[i % 2].rearrange("p (k d) -> p k d", k=3), ACT.Copy,
                                         scale=XS_).then_inc(w2h, 1)

        @prep.tensor
        def _(pe):
            pe.wait_ge(g_in, 16)

            def s2(t, s, again):
                pe.wait_ge(xn2_ready, t + 1)
                if again:
                    pe.wait_ge(xf_ready, t - 1)
                for c in range(KD):
                    m = nc.tensor.transpose(banks[s][:, c * P:(c + 1) * P], xn2[s][:, c * P:(c + 1) * P], idf[:, :])
                m.then_inc(t2_ready, 1)

            def s3(t, s, again):
                pe.wait_ge(xf_ready, t + 1)
                if again:
                    pe.wait_ge(lg_kept, t - 1)
                for c in range(KD):
                    m = nc.tensor.matmul(banks[2 + s][:, 0:8], xf[s][:, c, :], gate[:, c, :], start=(c == 0), stop=(c == KD - 1))
                m.then_inc(lg_ready, 1)

            tiles3(pe, none3, s2, s3, NT)
            pe.wait_ge(cnt_in, 1)
            nc.tensor.matmul(banks[4][:, 0:NT * 8], tri[:, :], m16, start=True, stop=True)
            nc.tensor.matmul(banks[5][:, 0:NT * 8], oneh[:, :], m16, start=True, stop=True).then_inc(cnt, 1)

        @prep.vector
        def _(dve):
            row_stats(dve, bn_done, st2, NT)
            dve.wait_ge(st2, NT)
            nc.vector.tensor_scalar(rstd[:, :], mv[:, :, 1], EPS, None, ALU.add).then_inc(st2, 1)
            dve.wait_ge(rs2, 1)
            nc.vector.reciprocal(rstd[:, :], rstd[:, :]).then_inc(rs2, 1)
            dve.wait_ge(rs2, 2)

            def s1(t, s, again):
                if again:
                    dve.wait_ge(t2_ready, t - 1)
                    dve.wait_ge(lo2, t - 1)
                nc.vector.tensor_scalar(xn2[s], xres[:, ds(t, 1), :].rearrange("p a d -> p (a d)"),
                                        mv[:, ds(t, 1), 0], rstd[:, ds(t, 1)], ALU.subtract, ALU.mult).then_inc(xn2_ready, 1)

            def s2(t, s, again):
                dve.wait_ge(hi2, t + 1)
                nc.vector.tensor_tensor(xs[:, ds(t, 1), D:2 * D], xn2[s].unsqueeze(1), xs[:, ds(t, 1), 0:D],
                                        ALU.subtract).then_inc(lo2, 1)

            def s3(t, s, again):
                dve.wait_ge(lg_ready, t + 1)
                nc.vector.tensor_copy(lg[:, ds(t, 1), :], banks[2 + s][:, 0:8].unsqueeze(1)).then_inc(lg_kept, 1)

            tiles3(dve, s1, s2, s3, NT)
            chain = [0]

            def link(ins):
                chain[0] += 1
                ins.then_inc(rch, 1)
                dve.wait_ge(rch, chain[0])

            dve.wait_ge(lg_kept, NT)
            for t in range(NT):
                nc.vector.max(v8[:, t, :], lg[:, t, :]).then_inc(top_v, 1)
            dve.wait_ge(top_v, NT)
            for t in range(NT):
                nc.vector.max_index(i8[:, t, :], v8[:, t, :], lg[:, t, :]).then_inc(top_i, 1)
            link(nc.vector.tensor_tensor(dif, v8[:, :, 1], v8[:, :, 0], ALU.subtract))
            dve.wait_ge(top_i, NT)
            link(nc.vector.tensor_copy(i8f, i8[:, :, 0:2]))
            for k in range(2):
                link(nc.vector.tensor_tensor(oh[k], iot[:, 0:8].unsqueeze(1).broadcast_to([P, NT, 8]),
                                             i8f[:, :, k:k + 1].broadcast_to([P, NT, 8]), ALU.is_equal))
            nc.vector.tensor_tensor(m16.rearrange("p (t e) -> p t e", e=8), oh[0], oh[1], ALU.add).then_inc(cnt_in, 1)
            link(nc.vector.memset(one, 1.0))
            dve.wait_ge(cnt, 1)
            link(nc.vector.tensor_copy(tot, banks[5][:, 0:NT * 8].rearrange("p (t e) -> p e t", e=8)))
            for e in range(8):
                link(nc.vector.tensor_tensor_scan(inc[:, e, :], one, tot[:, e, :], 0.0, ALU.mult, ALU.add))
            link(nc.vector.tensor_tensor(cmp, inc[:, :, NT - 1:NT].broadcast_to([P, 8, 16]),
                                         iot[:, SLOT_TILES:SLOT_TILES + 16].unsqueeze(1).broadcast_to([P, 8, 16]), ALU.is_gt))
            link(nc.vector.tensor_reduce(nt, cmp, AX.X, ALU.add))
            link(nc.vector.tensor_tensor_scan(endt, one[:, 0:8], nt, 0.0, ALU.mult, ALU.add))
            link(nc.vector.tensor_tensor(start, endt, nt, ALU.subtract))
            link(nc.vector.tensor_scalar(start, start, float(MT), None, ALU.mult))
            link(nc.vector.tensor_tensor(inc, inc, tot, ALU.subtract))
            link(nc.vector.tensor_tensor(inc, inc, start.unsqueeze(2).broadcast_to([P, 8, NT]), ALU.add))
            link(nc.vector.tensor_tensor(off, banks[4][:, 0:NT * 8].rearrange("p (t e) -> p t e", e=8),
                                         inc.rearrange("p e t -> p t e"), ALU.add))
            for k in range(2):
                link(nc.vector.tensor_tensor(prod[k], oh[k], off, ALU.mult))
                link(nc.vector.tensor_reduce(posf[:, k, :], prod[k], AX.X, ALU.add))
            link(nc.vector.tensor_copy(pos[:, :, :], posf))
            link(nc.vector.tensor_tensor(tcmp, iot[:, 0:SLOT_TILES].unsqueeze(2).broadcast_to([P, SLOT_TILES, 7]),
                                         endt[:, 0:7].unsqueeze(1).broadcast_to([P, SLOT_TILES, 7]), ALU.is_ge))
            link(nc.vector.tensor_reduce(exf, tcmp, AX.X, ALU.add))
            link(nc.vector.tensor_copy(exid[:, :], exf))
            dve.wait_ge(ew, 1)
            link(nc.vector.tensor_scalar(dif, edif, 1.0, None, ALU.add))
            link(nc.vector.reciprocal(dif, dif))
            link(nc.vector.tensor_scalar(wts[:, 0, :], dif, XS_ ** -2, None, ALU.mult))
            link(nc.vector.tensor_tensor(wts[:, 1, :], edif, wts[:, 0, :], ALU.mult))
            for i in range(LATE + NE):
                dve.wait_ge(w2h, i + 1)
                if i < LATE:
                    nc.vector.scalar_tensor_tensor(out=late(i, 1), in0=st_sm[i % 2], scalar=XS_, in1=late(i, 0),
                                                   op0=ALU.mult, op1=ALU.subtract).then_inc(w2l, 1)
                else:
                    nc.vector.scalar_tensor_tensor(out=dnc(i - LATE, 1), in0=st_sm[i % 2].rearrange("p (k d) -> p k d", k=3),
                                                   scalar=XS_, in1=dnc(i - LATE, 0), op0=ALU.mult, op1=ALU.subtract).then_inc(w2l, 1)

        prep.__exit__(None, None, None)

        def part(base, s, n):
            return ring[:, base + s * n:base + (s + 1) * n]
        XT = [part(0, s, 512).bitcast(F16).rearrange("p (a c t) -> p a c t", a=2, c=KD) for s in range(2)]
        SG = [part(1024, s, MT) for s in range(2)]
        HF = [part(1536, s, MT) for s in range(2)]
        HH = [part(2048, s, 384).bitcast(F16).rearrange("p (f t) -> p f t", f=3) for s in range(2)]
        HL = [part(2816, s, 384).bitcast(F16).rearrange("p (f t) -> p f t", f=3) for s in range(2)]
        xr = [accp[:, s, :].bitcast(F16).rearrange("p (u n) -> p u n", u=2) for s in range(2)]
        ys = [accd[:, s, :].rearrange("p (u d) -> p u d", u=2) for s in range(2)]
        gbuf = wide[:, UPC + DNC:UPC + DNC + GS * 2 * D].bitcast(F32)[:, 0:GS * D].rearrange("p (s d) -> p s d", s=GS)
        ST, RT = SHARED_TILES, SLOT_TILES

        def tiles(e, load, up, down, evac, t0, c0, n, also=None):
            def at(i, j):
                return t0 + i, (c0 + j) % 2, c0 + i

            def step(i, j, more=True, before=True):
                up(*at(i, j), (lambda: load(*at(i + 1, j + 1))) if more else None,
                   (lambda: (down(*at(i - 1, j - 1)), evac(*at(i - 1, j - 1)))) if before else None)
            load(*at(0, 0))
            step(0, 0, before=False)
            step(1, 1)
            pairs = 0 if also else (n - 3) // 2
            if pairs:
                with e.Fori(0, pairs) as i:
                    for j in range(2):
                        step(i * 2 + (j + 2), j)
            for k in range(2 * pairs + 2, n):
                step(k, k, more=k < n - 1)
                if also:
                    also(k)
            down(*at(n - 1, n - 1)), evac(*at(n - 1, n - 1))

        def fs(s, f):
            return (s + f) % 2

        nothing = lambda *a: None

        moe = nc.Block()
        moe.__enter__()

        @moe.sync
        def _(sp):
            sp.wait_ge(scat, 16 * 2 * NT)
            for j in range(2):
                sp.dma_start(xr[j], slots[j * MT:(j + 1) * MT, :].rearrange("(u p) n -> p u n", p=P)).then_inc(xr_in[j], 16)
            def rows_in(i, j):
                sp.wait_ge(xtT, i * 2 + (S1 + j + 1))
                sp.dma_start(xr[j], slots[ds((i * 2 + j + 2) * MT, MT), :].rearrange("(u p) n -> p u n", p=P)).then_inc(xr_in[j], 16)
            with sp.Fori(0, RT // 2 - 1) as i:
                rows_in(i, 0), rows_in(i, 1)
            rows_in(RT // 2 - 1, 0)
            for c in range(8):
                sp.wait_ge(comb2, 4 * c + 4)
                sp.dma_start(out[c * 512:(c + 1) * 512, :].rearrange("(t p) d -> p t d", p=P),
                             xres[:, 4 * c:4 * c + 4, :]).then_inc(done, 16)
            sp.wait_ge(done, 128)

        @moe.gpsimd
        def _(pool):
            pool.wait_ge(z_out, 16 * 6)
            for t in range(NT):
                for k in range(2):
                    pool.indirect_dma_start(out=slots, out_offset=bass.IndirectOffsetOnAxis(ap=pos[:, k, t:t + 1], axis=0),
                                            in_=xs[:, t, :], in_offset=None).then_inc(scat, 16)
            pool.wait_ge(xte, S1 + RT)
            pool.wait_ge(y_out[0], 16 * (RT // 2 + RT % 2) + 16)
            pool.wait_ge(y_out[1], 16 * (RT // 2) + 16)
            for t in range(NT):
                for k in range(2):
                    i = 2 * t + k
                    if i >= GS:
                        pool.wait_ge(comb1 if k == 0 else comb2, (i - GS) // 2 + 1)
                    pool.indirect_dma_start(out=gbuf[:, i % GS, :], out_offset=None, in_=ydram,
                                            in_offset=bass.IndirectOffsetOnAxis(ap=pos[:, k, t:t + 1], axis=0)).then_inc(gat[i % GS], 16)

        @moe.scalar
        def _(act):
            for s in range(2):
                act.sem_inc(y_out[s], 16)
            def make(shared):
                def load(t, s, c):
                    act.wait_ge(xtT, c + 1)
                    nc.scalar.activation(XT[s], half(4 + s).rearrange("p (a c t) -> p a c t", a=2, c=KD), ACT.Copy).then_inc(xte, 1)

                def up(t, s, c, mid, late_):
                    for f in range(3):
                        act.wait_ge(g_ready, c * 3 + f + 1)
                        nc.scalar.activation(SG[fs(s, f)], banks[fs(s, f)][:, 0:MT], ACT.Silu, scale=1.0 / XS_).then_inc(silu, 1)
                        act.wait_ge(h_ready, c * 3 + f + 1)
                        nc.scalar.activation(HH[s][:, f, :], HF[fs(s, f)], ACT.Copy).then_inc(hh_ready, 1)
                        if f == 0 and mid:
                            mid()
                        if f == 1 and late_:
                            late_()

                def evac(t, s, c):
                    if shared:
                        return
                    act.wait_ge(y_ready, c + 1)
                    act.wait_ge(y_out[s], t * 8 - 8 * s + 16)
                    nc.scalar.activation(ys[s], banks[6 + s].rearrange("p (u d) -> p u d", u=2), ACT.Copy).then_inc(y_read, 1)
                    act.wait_ge(y_read, c + 1)
                    act.dma_start(ydram[ds(t * MT, MT), :].rearrange("(u p) d -> p u d", p=P), ys[s]).then_inc(y_out[s], 16)
                return load, up, nothing, evac

            tiles(act, *make(True), 0, 0, S1)
            tiles(act, *make(False), 0, S1, RT)
            tiles(act, *make(True), S1, S1 + RT, ST - S1)

        @moe.vector
        def _(dve):
            def make(shared):
                def up(t, s, c, mid, late_):
                    for f in range(3):
                        dve.wait_ge(silu, c * 3 + f + 1)
                        dve.wait_ge(u_ready, c * 3 + f + 1)
                        nc.vector.tensor_tensor(HF[fs(s, f)], banks[2 + fs(s, f)][:, 0:MT], SG[fs(s, f)], ALU.mult).then_inc(h_ready, 1)
                        dve.wait_ge(hh_ready, c * 3 + f + 1)
                        nc.vector.tensor_tensor(HL[s][:, f, :], HF[fs(s, f)], HH[s][:, f, :], ALU.subtract).then_inc(hl_ready, 1)
                        if f == 1 and late_:
                            late_()

                def evac(t, s, c):
                    if not shared:
                        return
                    dve.wait_ge(y_ready, c + 1)
                    x2 = xres[:, ds(t * 2, 2), :].rearrange("p u d -> p (u d)")
                    nc.vector.scalar_tensor_tensor(out=x2, in0=banks[6 + s], scalar=XS_ ** -2, in1=x2,
                                                   op0=ALU.mult, op1=ALU.add).then_inc(y_read, 1)
                return nothing, up, nothing, evac

            def combine(i):
                dve.wait_ge(y_read, S1 + RT if i < 2 * S1 // 4 else ST + RT)
                for t in range(4 * i, 4 * i + 4):
                    for k in range(2):
                        g = 2 * t + k
                        dve.wait_ge(gat[g % GS], 16 * (g // GS + 1))
                        if k:
                            dve.wait_ge(comb1, t + 1)
                        nc.vector.scalar_tensor_tensor(out=xres[:, t, :], in0=gbuf[:, g % GS, :], scalar=wts[:, k, t:t + 1],
                                                       in1=xres[:, t, :], op0=ALU.mult, op1=ALU.add).then_inc(comb2 if k else comb1, 1)

            with_tile = {3: 0, 5: 1, 6: 2, 7: 3}

            def beside(k):
                if k in with_tile:
                    combine(with_tile[k])

            tiles(dve, *make(True), 0, 0, S1)
            tiles(dve, *make(False), 0, S1, RT)
            tiles(dve, *make(True), S1, S1 + RT, ST - S1, beside)
            for i in range(len(with_tile), NT // 4):
                combine(i)

        @moe.tensor
        def _(pe):
            def make(shared):
                def expert(t):
                    return NE - 1 if shared else pe.value_load(exid[0:1, ds(t, 1)], min_val=0, max_val=NE - 2)

                def load(t, s, c):
                    if not shared:
                        pe.wait_ge(xr_in[s], t * 8 + (16 - 8 * s))
                    if not (isinstance(c, int) and c < 2):
                        pe.wait_ge(xte, c - 1)
                    for a in range(2):
                        for ch in range(KD):
                            for u in range(2):
                                src = xs[:, ds(t * 2 + u, 1), :].rearrange("p a n -> p (a n)") if shared else xr[s][:, u, :]
                                o = a * D + ch * P
                                j = (a * KD + ch) * 2 + u
                                m = nc.tensor.transpose(half(4 + s)[:, j * P:(j + 1) * P], src[:, o:o + P], idh[:, :])
                    m.then_inc(xtT, 1)

                def up(t, s, c, mid, late_):
                    pe.wait_ge(xte, c + 1)
                    e = expert(t)
                    for f in range(3):
                        for gu, sm_ in ((0, g_ready), (1, u_ready)):
                            b_ = banks[2 * gu + fs(s, f)][:, 0:MT]
                            if not (isinstance(c, int) and c * 3 + f < 2):
                                pe.wait_ge((silu, h_ready)[gu], c * 3 + (f - 1))
                            j = 0
                            for wp, xp in ((0, 0), (0, 1), (1, 0)):
                                for ch in range(KD):
                                    o = ch * 4 * FF + wp * 2 * FF + gu * FF + f * P
                                    m = nc.tensor.matmul(b_, w_up[:, ds(e * (2 * UPW) + o, P)], XT[s][:, xp, ch, :],
                                                         start=(j == 0), stop=(j == 5))
                                    j += 1
                            m.then_inc(sm_, 1)
                        if f == 0 and mid:
                            mid()
                        if f == 1 and late_:
                            late_()

                def down(t, s, c):
                    e = expert(t)
                    pe.wait_ge(hl_ready, c * 3 + 3)
                    if not (isinstance(c, int) and c < 2):
                        pe.wait_ge(y_read, c - 1)
                    for u in range(2):
                        j = 0
                        for f in range(3):
                            for hp_, wp in ((0, 0), (0, 1), (1, 0)):
                                hx = (HH, HL)[hp_][s]
                                m = nc.tensor.matmul(banks[6 + s][:, u * D:(u + 1) * D], hx[:, f, u * P:(u + 1) * P],
                                                     w_dn[:, ds(e * (2 * DNW) + (f * 2 + wp) * D, D)], start=(j == 0), stop=(j == 8))
                                j += 1
                    m.then_inc(y_ready, 1)
                return load, up, down, nothing

            tiles(pe, *make(True), 0, 0, S1)
            tiles(pe, *make(False), 0, S1, RT)
            tiles(pe, *make(True), S1, S1 + RT, ST - S1)

        moe.__exit__(None, None, None)


_INS = ["x", "wq", "bq", "wk", "bk", "wv", "bv", "wo", "bo", "freq", "gate_t", "experts"]


def kernel(L0_attn_x, L0_attn_Wq, L0_attn_bq, L0_attn_Wk, L0_attn_bk, L0_attn_Wv, L0_attn_bv, L0_attn_Wo, L0_attn_bo,
           L0_attn_nrope_freq, L0_ffn_gate_w, L0_ffn_w_up, L0_ffn_w_down, L0_ffn_sg_gate, L0_ffn_sg_up, L0_ffn_sg_down):
    import numpy as _np
    import concourse.bacc as _bacc
    from concourse import mybir as _mybir
    from concourse.bass_utils import run_bass_kernel_spmd as _run

    x = _np.asarray(L0_attn_x)
    D, P = x.shape[-1], 128
    sg = _np.concatenate([_np.asarray(L0_ffn_sg_gate), _np.asarray(L0_ffn_sg_up)], 0)[None]
    up = _np.concatenate([_np.asarray(L0_ffn_w_up), sg], 0)
    up = up.transpose(0, 2, 1).reshape(up.shape[0], D // P, P, -1).transpose(2, 0, 1, 3).reshape(P, -1)
    down = _np.concatenate([_np.asarray(L0_ffn_w_down), _np.asarray(L0_ffn_sg_down)[None]], 0)
    down = down.transpose(0, 2, 1).reshape(down.shape[0], -1, P, D).transpose(2, 0, 1, 3).reshape(P, -1)
    given = dict(x=x.reshape(-1, D), wq=L0_attn_Wq, bq=L0_attn_bq, wk=L0_attn_Wk, bk=L0_attn_bk, wv=L0_attn_Wv,
                 bv=L0_attn_bv, wo=L0_attn_Wo, bo=L0_attn_bo, freq=L0_attn_nrope_freq,
                 gate_t=_np.asarray(L0_ffn_gate_w).T, experts=_np.concatenate([up, down], 1))
    nc = _bacc.Bacc("TRN2", target_bir_lowering=False, num_devices=1)
    arrays, args = {}, []
    for name in _INS:
        a = _np.ascontiguousarray(given[name])
        arrays[f"in_{name}"] = a
        args.append(nc.dram_tensor(f"in_{name}", a.shape, _mybir.dt.from_np(a.dtype), kind="ExternalInput").ap())
    args.append(nc.dram_tensor("out_rows", (x.size // D, D), _mybir.dt.float32, kind="ExternalOutput").ap())
    add_ffn_kernel(nc, *args)
    r = _run(nc, [arrays], core_ids=[0])
    return r.results[0]["out_rows"].reshape(x.shape)
```

```python
import concourse.bass as bass
from concourse import mybir
from contextlib import ExitStack
import numpy as np


def add_ffn_kernel(nc, x, wq, bq, wk, bk, wv, bv, wo, bo, freq, gate_t, experts, out):
    F32, F16, I32, U32 = mybir.dt.float32, mybir.dt.float16, mybir.dt.int32, mybir.dt.uint32
    ALU, ACT, AX = mybir.AluOpType, mybir.ActivationFunctionType, mybir.AxisListType
    ds = bass.ds

    P = 128
    N, D = x.shape
    B, H, HD = 2, 4, 64
    T = N // B
    NT, TB = N // P, T // P
    KD = D // P
    QB = 512
    NQ = T // QB
    NK = T // P
    HP = H // 2
    RH = HD // 4
    EPS = 1e-5
    AHEAD = 1
    ROW = 2 + 2 * D
    WS = 16.0
    ES = 32.0
    NE, FF = 9, 384
    UPW = KD * 2 * FF
    DNW = 3 * D
    EARLY = 6
    CH = 2 * FF
    MT = 256
    SHARED_TILES = N // MT
    S1 = 12
    SLOT_TILES = 2 * N // MT + 7
    SDT = (10000.0 - (1.0 - 17 / 100.0) * 10000.0) * 2.0
    MINB = (1.0 - 17 / 100.0) * 10000.0
    ROT = 2.0 * np.pi / (T - 1)

    ctx = ExitStack()
    with ctx:
        def sb(name, shape, dt):
            return ctx.enter_context(nc.sbuf_tensor(name, shape, dt))

        def sem(name):
            return ctx.enter_context(nc.semaphore(name))

        UP16 = EARLY * UPW * 2
        QK16 = H * T
        wide = sb("wide", [P, UP16 + 4 * QK16 + 2 * TB * D], F16)
        UPC, DNC = NE * UPW * 2, NE * DNW * 2
        w_up = wide[:, 0:UPC]
        w_dn = wide[:, UPC:UPC + DNC]
        xrow = wide[:, UPC + DNC:UPC + DNC + NT * ROW].rearrange("p (t n) -> p t n", t=NT)
        xs = xrow[:, :, 2:ROW]
        K1 = wide[:, UP16:UP16 + QK16].rearrange("p (h t) -> p h t", h=H)
        K2 = wide[:, UP16 + QK16:UP16 + 2 * QK16].rearrange("p (h t) -> p h t", h=H)
        Q1 = wide[:, UP16 + 2 * QK16:UP16 + 3 * QK16].rearrange("p (h t) -> p h t", h=H)
        Q2 = wide[:, UP16 + 3 * QK16:UP16 + 4 * QK16].rearrange("p (h t) -> p h t", h=H)
        V = wide[:, UP16 + 4 * QK16:].bitcast(F32).rearrange("p (t d) -> p t d", t=TB)
        xres = sb("xres", [P, NT, D], F32)
        ring = sb("ring", [P, 4 * 2 * QB], F32)
        Pr = ring[:, :].rearrange("p (s h q) -> p s h q", s=4, h=2)
        accp = sb("accp", [P, 2, QB], F32)
        accd = sb("accd", [P, 2, QB], F32)
        pvraw = sb("pvraw", [P, QB], F32)
        recip = sb("recip", [P, QB], F32)
        OT = sb("OT", [P, HP, QB], F32)
        stage = sb("stage", [P, 2, CH], F32)
        wqkv = sb("wqkv", [P, 2, KD, 3 * D], F16)
        wo_sb = sb("wo_sb", [P, KD, D], F32)
        bias = sb("bias", [P, 3 * D], F32)
        bo_sb = sb("bo_sb", [P, D], F32)
        cos = sb("cos", [P, TB, RH], F32)
        sin = sb("sin", [P, TB, RH], F32)
        mt = sb("mt", [P, 2 * QB // P, P], F16)
        mx = sb("mx", [P, 2 * QB // P, T // 512], F32)
        m8 = sb("m8", [P, 2 * QB // P], F32)
        idf = sb("idf", [P, P], F32)
        idh = sb("idh", [P, P], F16)
        ones = sb("ones", [P, HD], F32)
        stats = sb("stats", [P, NT, 6], F32)
        mean = sb("mean", [P, NT], F32)
        dm = sb("dm", [P, TB], F32)
        var = sb("var", [P, TB], F32)
        rstd = sb("rstd", [P, NT], F32)
        sm = sb("sm", [P, 8], F32)
        jpos = sb("jpos", [P, RH + TB], F32)
        ang = stage[:, 0, 0:TB * RH].rearrange("p (t j) -> p t j", t=TB)
        empty_ids = stage[:, 1, 0:SLOT_TILES * MT // P].bitcast(U32)
        wst = ring[:, 0:KD * 3 * D].rearrange("p (k n) -> p k n", k=KD)
        def slot(base, s, n):
            return ring[:, base + s * n:base + (s + 1) * n]
        xn = [slot(0, s, D) for s in range(2)]
        xh = [slot(512, s, D).bitcast(F16).rearrange("p (a d) -> p a d", a=2) for s in range(2)]
        xT = [slot(1024, s, D).bitcast(F16).rearrange("p (a c) -> p a c", a=4) for s in range(2)]
        qk = [slot(1536, s, 2 * D) for s in range(2)]
        ra = slot(2560, 0, 256).rearrange("p (h c j) -> p h c j", h=2 * H, c=2)
        rb = slot(2816, 0, 256).rearrange("p (h c j) -> p h c j", h=2 * H, c=2)
        qtok = [slot(3072, s, 256).bitcast(F16).rearrange("p (h c) -> p h c", h=H) for s in range(2)]
        ktok = [slot(3584, s, 256).bitcast(F16).rearrange("p (h c) -> p h c", h=H) for s in range(2)]
        zt = sb("zt", [P, ROW], F16)
        kept = sb("kept", [P, 2, 2], U32)
        ids = sb("ids", [P, 2, 2], U32)
        gate = sb("gate", [P, KD, 8], F32)
        tri = sb("tri", [P, P], F16)
        oneh = sb("oneh", [P, P], F16)
        iot = sb("iot", [P, SLOT_TILES + 16 + 8], F32)
        pos = sb("pos", [P, 2, NT], U32)
        wts = sb("wts", [P, 2, NT], F32)
        exid = sb("exid", [P, SLOT_TILES], I32)
        slots = nc.dram_tensor("slots", (SLOT_TILES * MT, ROW), F16, kind="Internal").ap()
        ytok = nc.dram_tensor("ytok", (2 * N + SLOT_TILES * MT, D), F32, kind="Internal").ap()
        qlo = [accp[:, s, 0:128].bitcast(F16).rearrange("p (h c) -> p h c", h=H) for s in range(2)]

        psum = ctx.enter_context(nc.psum_tensor("psum", [P, 8, 512], F32))
        banks = [psum[:, i, :] for i in range(8)]

        def half(i):
            return banks[i].bitcast(F16)

        def spair(s):
            return psum[:, 2 * s:2 * s + 2, :]
        xtp = [half(4 + s)[:, 0:512].rearrange("p (a c) -> p a c", a=4) for s in range(2)]
        q1ps = half(6)[:, 0:512].rearrange("p (h c) -> p h c", h=H)
        qlps = half(6)[0:HD, 512:1024].rearrange("p (h c) -> p h c", h=H)
        kps = half(7)[:, 0:512].rearrange("p (h c) -> p h c", h=H)
        mtps = half(7).rearrange("p (h c) -> p h c", h=2)
        pvps = banks[6]

        def upc(m, part):
            return w_up[:, ds(m * (4 * FF) + part * 2 * FF, 2 * FF)]

        x_in = [sem(f"x_in{b}") for b in range(B)]; f_in = sem("f_in"); w_in = sem("w_in"); b_in = sem("b_in"); k_in = sem("k_in")
        pset = sem("pset"); aset = sem("aset"); ln_ready = sem("ln_ready")
        dch = sem("dch"); sums_done = sem("sums_done"); mom = sem("mom"); w_high = sem("w_high"); pcos = sem("pcos"); root = sem("root")
        xn_ready = sem("xn_ready"); xhi_ready = sem("xhi_ready"); xlo_ready = sem("xlo_ready")
        xtp_ready = sem("xtp_ready"); xt_ready = sem("xt_ready")
        qkv_ready = sem("qkv_ready"); qk_ready = sem("qk_ready"); v_ready = sem("v_ready")
        ra_ready = sem("ra_ready"); rope_done = sem("rope_done")
        hi_done = sem("hi_done"); qlo_done = sem("qlo_done"); tr_q = sem("tr_q"); tr_k = sem("tr_k")
        q_stored = sem("q_stored"); k_stored = sem("k_stored")
        a_ready = sem("a_ready"); max_done = sem("max_done"); m8_done = sem("m8_done")
        negm = sem("negm"); mT_ready = sem("mT_ready"); mrow = sem("mrow")
        s_ready = sem("s_ready"); exp_done = sem("exp_done"); pv_done = sem("pv_done")
        pacc = sem("pacc"); dacc = sem("dacc"); accp_free = sem("accp_free")
        den_ready = sem("den_ready"); recip_done = sem("recip_done"); pv_copied = sem("pv_copied")
        ot_ready = sem("ot_ready"); quarter = sem("quarter"); wo_ready = sem("wo_ready"); wo_added = sem("wo_added")
        bo_added = sem("bo_added"); st_in = [sem(f"st_in{s}") for s in range(2)]; wh_done = sem("wh_done"); wl_done = sem("wl_done")
        z_out = sem("z_out"); e_out = sem("e_out"); done = sem("done"); g_in = sem("g_in")
        xn2_ready = sem("xn2_ready"); hi2 = sem("hi2"); lo2 = sem("lo2")
        t2_ready = sem("t2_ready"); xf_ready = sem("xf_ready"); lt_ready = sem("lt_ready"); lt_kept = sem("lt_kept"); lg_ready = sem("lg_ready"); top_v = sem("top_v")
        top_i = sem("top_i"); lg_kept = sem("lg_kept"); rch = sem("rch"); cnt_in = sem("cnt_in"); cnt = sem("cnt"); ew = sem("ew")
        placed = sem("placed"); routed = sem("routed"); w2_in = [sem(f"w2_in{s}") for s in range(4)]; w2h = sem("w2h"); w2l = sem("w2l")
        scat = [sem(f"scat{h}") for h in range(2)]; xr_in = [sem(f"xr_in{s}") for s in range(2)]; xtT = sem("xtT"); xte = sem("xte")
        g_ready = sem("g_ready"); u_ready = sem("u_ready"); silu = sem("silu"); h_ready = sem("h_ready")
        hh_ready = sem("hh_ready"); hl_ready = sem("hl_ready"); y_ready = sem("y_ready"); y_read = sem("y_read")
        y_out = [sem(f"y_out{s}") for s in range(2)]; gat = [sem(f"gat{g}") for g in range(SHARED_TILES)]; ids_set = sem("ids_set"); ids_kept = sem("ids_kept"); ids_moved = sem("ids_moved")
        weighed = sem("weighed"); comb = [[sem(f"comb_{n}{k}") for k in range(2)] for n in ("pool", "dve")]

        NORM, SPLIT, TURNX, PROJ, SPLITQK, STORE = 5, 4, 3, 2, 1, 0

        def reused(k):
            return not (isinstance(k, int) and k < 2)

        def schedule(e, b, *stages):
            def tick(k):
                for ahead, stage_ in stages:
                    if 0 <= k + ahead < TB:
                        stage_(b, k + ahead, (k + ahead) % 2)
            for k in range(-NORM, 0):
                tick(k)
            with e.Fori(0, (TB - NORM) // 2) as i:
                for j in range(2):
                    for ahead, stage_ in stages:
                        stage_(b, i * 2 + j + ahead, (j + ahead) % 2)
            for k in range((TB - NORM) // 2 * 2, TB):
                tick(k)

        def row_sums(dve, t):
            nc.vector.bn_stats(stats[:, ds(t, 1), :].rearrange("p a n -> p (a n)"),
                               xres[:, ds(t, 1), :].rearrange("p a d -> p (a d)")).then_inc(sums_done, 1)

        def moments(dve, t, c):
            st, mu, va = stats[:, ds(t, TB), :], mean[:, ds(t, TB)], var[:, :]
            dve.wait_ge(sums_done, c * TB + TB)
            nc.vector.tensor_tensor(dm[:, :], st[:, :, 1], st[:, :, 4], ALU.subtract).then_inc(mom, 1)
            nc.vector.tensor_tensor(mu, st[:, :, 1], st[:, :, 4], ALU.add).then_inc(mom, 1)
            nc.vector.tensor_tensor(va, st[:, :, 2], st[:, :, 5], ALU.add).then_inc(mom, 1)
            dve.wait_ge(mom, c * 7 + 3)
            nc.vector.tensor_tensor(dm[:, :], dm[:, :], dm[:, :], ALU.mult).then_inc(mom, 1)
            nc.vector.tensor_scalar(mu, mu, 0.5, None, ALU.mult).then_inc(mom, 1)
            dve.wait_ge(mom, c * 7 + 5)
            nc.vector.scalar_tensor_tensor(out=va, in0=dm[:, :], scalar=D / 4.0, in1=va,
                                           op0=ALU.mult, op1=ALU.add).then_inc(mom, 1)
            dve.wait_ge(mom, c * 7 + 6)
            nc.vector.tensor_scalar(va, va, 1.0 / D, EPS, ALU.mult, ALU.add).then_inc(mom, 1)

        def moments_root(act, c):
            act.wait_ge(mom, c * 7 + 7)
            nc.scalar.activation(var[:, :], var[:, :], ACT.Sqrt).then_inc(root, 1)

        def moments_end(dve, t, c):
            dve.wait_ge(root, c * 3 + 1)
            nc.vector.reciprocal(var[:, :], var[:, :]).then_inc(root, 1)
            dve.wait_ge(root, c * 3 + 2)
            nc.vector.tensor_copy(rstd[:, ds(t, TB)], var[:, :]).then_inc(root, 1)
            dve.wait_ge(root, c * 3 + 3)

        ROWS = [1, 2, 3, 3, 3, 3, 3, 3, 3, 3, 3, 2, 0, 0, 0, 0]
        OUT0, OUT1, TURN = 6, 9, 13

        def rows_of(kt):
            return list(range(sum(ROWS[:kt]), sum(ROWS[:kt + 1])))

        def blocks(e, b, prologue, block, last):
            n = b * (NQ * HP)
            prologue(n, b)
            block(n, b, 0, 0, (0, 1), False, None)
            with e.Fori(0, NQ - 1) as q:
                m = b * (2 * NQ - 2) + q * 2
                block(n + q * 2 + 1, b, q, 1, (q + 1, 0), False, m)
                block(n + q * 2 + 2, b, q + 1, 0, (q + 1, 1), True, m + 1)
            block(n + 2 * NQ - 1, b, NQ - 1, 1, None, False, None)
            last(n, b)

        block_ = nc.Block()
        block_.__enter__()

        @block_.sync
        def _(sp):
            def rows(c):
                sp.dma_start(xres[:, 8 * c:8 * c + 8, :],
                             x[c * 1024:(c + 1) * 1024, :].rearrange("(t p) d -> p t d", p=P)).then_inc(x_in[c // 2], 16)
            rows(0), rows(1)
            for i, w in enumerate((wq, wk, wv)):
                sp.dma_start(wst[:, :, i * D:(i + 1) * D], w.rearrange("(k p) n -> p k n", p=P)).then_inc(w_in, 16)
            rows(2), rows(3)
            sp.dma_start(wo_sb[:, :, :], wo.rearrange("(k p) n -> p k n", p=P)).then_inc(k_in, 16)
            sp.dma_start(gate[:, :, :], gate_t.rearrange("(k p) e -> p k e", p=P)).then_inc(g_in, 16)
            sp.wait_ge(pset, 13)
            zrows = slots.rearrange("(c n p) d -> c p n d", p=P, n=13)
            for c in range(SLOT_TILES * MT // P // 13):
                sp.dma_start(zrows[c], zt[:, :].unsqueeze(1).broadcast_to([P, 13, ROW])).then_inc(z_out, 16)
            sp.wait_ge(z_out, 16 * 6)
            sp.dma_start(slots[:, 0:2].rearrange("(c p) n -> p c n", p=P),
                         empty_ids.bitcast(F16).rearrange("p (c n) -> p c n", n=2)).then_inc(e_out, 16)
            for i in range(2):
                if i == 0:
                    sp.wait_ge(dch, 8)
                else:
                    sp.wait_ge(e_out, 16)
                sp.dma_start(stage[:, i, :], experts[:, i * CH:(i + 1) * CH]).then_inc(st_in[i], 16)
            with sp.Fori(0, EARLY - 1) as i:
                for j in range(2):
                    sp.wait_ge(wl_done, i * 2 + j + 1)
                    sp.dma_start(stage[:, j, :], experts[:, ds((i * 2 + j + 2) * CH, CH)]).then_inc(st_in[j], 16)

        @block_.gpsimd
        def _(pool):
            pool.memset(idf[:, :], 0.0).then_inc(pset, 1)
            pool.memset(idh[:, :], 0.0).then_inc(pset, 1)
            pool.iota(jpos[:, 0:RH], pattern=[[1, RH]], base=0, channel_multiplier=0,
                      allow_small_or_imprecise_dtypes=True).then_inc(pset, 1)
            pool.iota(jpos[:, RH:RH + TB], pattern=[[P, TB]], base=0, channel_multiplier=1,
                      allow_small_or_imprecise_dtypes=True).then_inc(pset, 1)
            pool.wait_ge(pset, 4)
            for m in (idf, idh):
                pool.affine_select(out=m[:, :], in_=m[:, :], compare_op=ALU.not_equal, fill=1.0,
                                   base=0, pattern=[[-1, P]], channel_multiplier=1).then_inc(pset, 1)
            pool.memset(ones[:, :], 1.0).then_inc(pset, 1)
            pool.memset(mt[:, :, :].rearrange("p a c -> p (a c)").bitcast(U32), 0).then_inc(pset, 1)
            pool.wait_ge(pset, 8)
            pool.memset(K2[HD:P, :, :].rearrange("p a c -> p (a c)").bitcast(U32), 0).then_inc(pset, 1)
            pool.memset(Q2[HD:P, :, :].rearrange("p a c -> p (a c)").bitcast(U32), 0).then_inc(pset, 1)
            pool.wait_ge(pset, 10)
            pool.memset(K2[HD:HD + 1, :, :].rearrange("p a c -> p (a c)"), 1.0).then_inc(pset, 1)
            pool.wait_ge(pset, 11)
            pool.memset(zt[:, :].bitcast(U32), 0).then_inc(pset, 1)
            pool.iota(empty_ids, pattern=[[P, SLOT_TILES * MT // P]], base=2 * N, channel_multiplier=1).then_inc(pset, 1)
            pool.memset(tri[:, :], 1.0).then_inc(pset, 1)
            pool.memset(oneh[:, :], 1.0).then_inc(pset, 1)
            pool.iota(iot[:, 0:SLOT_TILES], pattern=[[1, SLOT_TILES]], base=0, channel_multiplier=0,
                      allow_small_or_imprecise_dtypes=True).then_inc(pset, 1)
            pool.iota(iot[:, SLOT_TILES:SLOT_TILES + 16], pattern=[[MT, 16]], base=0, channel_multiplier=0,
                      allow_small_or_imprecise_dtypes=True).then_inc(pset, 1)
            pool.wait_ge(pset, 17)
            pool.affine_select(out=tri[:, :], in_=tri[:, :], compare_op=ALU.is_gt, fill=0.0,
                               base=0, pattern=[[1, P]], channel_multiplier=-1).then_inc(pset, 1)
            pool.sem_inc(accp_free, 1)
            for ahead in (rope_done, pacc):
                pool.sem_inc(ahead, AHEAD)

            def rope(b, k, s):
                g = b * TB + k
                X = qk[s].rearrange("p (h c j) -> p h c j", h=2 * H, c=4)[:, :, 2:4, :]
                cb = cos[:, ds(k, 1), :].unsqueeze(2).broadcast_to([P, 2 * H, 2, RH])
                sbb = sin[:, ds(k, 1), :].unsqueeze(2).broadcast_to([P, 2 * H, 2, RH])
                pool.wait_ge(qk_ready, g + 1)
                pool.wait_ge(rope_done, g * 2 + AHEAD)
                pool.tensor_tensor(ra, X, cb, ALU.mult).then_inc(ra_ready, 1)
                pool.tensor_tensor(rb, X, sbb, ALU.mult).then_inc(ra_ready, 1)
                pool.wait_ge(ra_ready, (g + 1) * 2)
                pool.tensor_tensor(X[:, :, 0, :], ra[:, :, 0, :], rb[:, :, 1, :], ALU.subtract).then_inc(rope_done, 1)
                pool.tensor_tensor(X[:, :, 1, :], ra[:, :, 1, :], rb[:, :, 0, :], ALU.add).then_inc(rope_done, 1)

            def prologue(n, b):
                pool.wait_ge(xn_ready, b * TB + TB)
                bo4 = bo_sb[:, :].unsqueeze(1).broadcast_to([P, 4, D])
                for c in range(4):
                    xs = xres[:, ds(b * TB + 4 * c, 4), :]
                    pool.tensor_tensor(xs, xs, bo4, ALU.add).then_inc(bo_added, 1)

            def block(n, b, q, hp, nxt, add, m):
                pool.wait_ge(accp_free, n + 1)
                for j in range(1, 13):
                    pool.wait_ge(exp_done, n * NK + j + 1)
                    if j == 1:
                        pool.tensor_tensor(accp[:, :, :], Pr[:, 0, :, :], Pr[:, 1, :, :], ALU.add).then_inc(pacc, 1)
                    else:
                        pool.wait_ge(pacc, n * 12 + j - 1 + AHEAD)
                        pool.tensor_tensor(accp[:, :, :], accp[:, :, :], Pr[:, j % 4, :, :], ALU.add).then_inc(pacc, 1)

            pool.wait_ge(aset, 5)
            pool.tensor_tensor(cos[:, :, :], cos[:, :, :], cos[:, :, :], ALU.mult).then_inc(pcos, 1)
            pool.wait_ge(pcos, 1)
            pool.tensor_scalar(cos[:, :, :], cos[:, :, :], -2.0, 1.0, ALU.mult, ALU.add).then_inc(pcos, 1)
            pool.wait_ge(pcos, 2)
            pool.wait_ge(k_in, 16)
            pool.wait_ge(b_in, 64)
            with pool.Fori(0, B) as b:
                schedule(pool, b, (PROJ, rope))
                blocks(pool, b, prologue, block, lambda n, b: None)

        @block_.scalar
        def _(act):
            for ahead in (q_stored, pv_copied):
                act.sem_inc(ahead, AHEAD)
            act.dma_start(sm[:, 0:1], freq.rearrange("(a n) -> a n", a=1).broadcast_to([P, 1])).then_inc(f_in, 16)
            for i, v in enumerate((bq, bk, bv)):
                act.dma_start(bias[:, i * D:(i + 1) * D],
                              v.rearrange("(a n) -> a n", a=1).broadcast_to([P, D])).then_inc(b_in, 16)
            act.dma_start(bo_sb[:, :], bo.rearrange("(a n) -> a n", a=1).broadcast_to([P, D])).then_inc(b_in, 16)
            act.wait_ge(f_in, 16)
            nc.scalar.activation(sm[:, 1:2], sm[:, 0:1], ACT.Exp, scale=-1.0).then_inc(aset, 1)
            act.wait_ge(dch, 3)
            nc.scalar.activation(sm[:, 5:6], sm[:, 4:5], ACT.Ln).then_inc(aset, 1)
            act.wait_ge(dch, 4)
            nc.scalar.activation(jpos[:, 0:RH], jpos[:, 0:RH], ACT.Exp, scale=-1.0 / RH).then_inc(aset, 1)
            act.wait_ge(w_in, 48)
            nc.scalar.activation(wqkv[:, 0, :, :], wst, ACT.Copy, scale=WS).then_inc(w_high, 1)
            moments_root(act, 0)
            act.wait_ge(dch, 8)
            nc.scalar.activation(sin[:, :, :], sin[:, :, :], ACT.Sin).then_inc(aset, 1)
            nc.scalar.activation(cos[:, :, :], cos[:, :, :], ACT.Sin).then_inc(aset, 1)

            def split_high(b, k, s):
                g = b * TB + k
                act.wait_ge(xn_ready, g + 1)
                if reused(k):
                    act.wait_ge(xtp_ready, g - 1)
                nc.scalar.activation(xh[s][:, 0, :], xn[s], ACT.Copy).then_inc(xhi_ready, 1)

            def copy_turned(b, k, s):
                g = b * TB + k
                act.wait_ge(xtp_ready, g + 1)
                if reused(k):
                    act.wait_ge(qkv_ready, g - 1)
                nc.scalar.activation(xT[s], xtp[s], ACT.Copy).then_inc(xt_ready, 1)

            def split_qk_high(b, k, s):
                g = b * TB + k
                act.wait_ge(rope_done, (g + 1) * 2 + AHEAD)
                qv = qk[s][:, 0:D].rearrange("p (h c) -> p h c", h=H)
                kv = qk[s][:, D:2 * D].rearrange("p (h c) -> p h c", h=H)
                nc.scalar.activation(qtok[s].rearrange("p h (a c) -> p h a c", a=2),
                                     qv.unsqueeze(2).broadcast_to([P, H, 2, HD]), ACT.Copy).then_inc(hi_done, 1)
                nc.scalar.activation(ktok[s][:, :, 0:HD], kv, ACT.Copy).then_inc(hi_done, 1)

            def store_q(b, k, s):
                g = b * TB + k
                act.wait_ge(tr_q, g + 1)
                nc.scalar.activation(Q1[:, :, ds(k * P, P)], q1ps, ACT.Copy).then_inc(q_stored, 1)
                nc.scalar.activation(Q2[0:HD, :, ds(k * P, P)], qlps, ACT.Copy).then_inc(q_stored, 1)

            def none(*a):
                pass

            def block(n, b, q, hp, nxt, add, m):
                for kt in range(NK):
                    act.wait_ge(s_ready, n * NK + kt + 1)
                    if kt == 0:
                        act.wait_ge(pacc, n * 12 + AHEAD)
                    elif kt < 3:
                        act.wait_ge(dacc, n * 3 + 1)
                    elif kt == 3:
                        act.wait_ge(dacc, n * 3 + 3)
                    else:
                        act.wait_ge(pacc, n * 12 + max(kt - 4, 1) + AHEAD)
                    nc.scalar.activation(Pr[:, kt % 4, :, :], spair(kt % 2), ACT.Exp, scale=HD ** -0.5).then_inc(exp_done, 1)
                    if kt == 5 and m is not None:
                        act.wait_ge(st_in[1 - hp], b * ((NQ - 1) * 16) + (q + (hp == 1)) * 16)
                        nc.scalar.activation(upc(m, 0), stage[:, 1 - hp, :], ACT.Copy, scale=ES).then_inc(wh_done, 1)
                act.wait_ge(pv_done, n + 1)
                act.wait_ge(ot_ready, n + AHEAD)
                nc.scalar.activation(pvraw[:, :], pvps, ACT.Copy).then_inc(pv_copied, 1)

            with act.Fori(0, B) as b:
                schedule(act, b, (SPLIT, split_high), (TURNX, copy_turned), (SPLITQK, split_qk_high), (STORE, store_q))
                blocks(act, b, none, block, lambda n, b: moments_root(act, b + 1))

        @block_.vector
        def _(dve):
            chain = [0]

            def link(ins, n=1):
                chain[0] += n
                ins.then_inc(dch, 1)
                dve.wait_ge(dch, chain[0])

            dve.wait_ge(aset, 1)
            link(nc.vector.tensor_scalar(sm[:, 2:3], sm[:, 1:2], 1.0, None, ALU.add))
            link(nc.vector.reciprocal(sm[:, 3:4], sm[:, 2:3]))
            link(nc.vector.tensor_scalar(sm[:, 4:5], sm[:, 3:4], SDT, MINB, ALU.mult, ALU.add))
            dve.wait_ge(aset, 2)
            dve.wait_ge(pset, 4)
            link(nc.vector.tensor_scalar(jpos[:, 0:RH], jpos[:, 0:RH], sm[:, 5:6], None, ALU.mult))
            dve.wait_ge(x_in[0], 32)
            for t in range(TB):
                row_sums(dve, t)
            moments(dve, 0, 0)
            dve.wait_ge(aset, 3)
            link(nc.vector.tensor_tensor(ang, jpos[:, RH:RH + TB].unsqueeze(2).broadcast_to([P, TB, RH]),
                                         jpos[:, 0:RH].unsqueeze(1).broadcast_to([P, TB, RH]), ALU.mult))
            PI = 3.1415925
            nc.vector.tensor_scalar(cos[:, :, :], ang, ROT / 2, PI, ALU.mult, ALU.min).then_inc(dch, 1)
            link(nc.vector.tensor_scalar(sin[:, :, :], ang, -ROT, float(np.pi), ALU.mult, ALU.add), 2)
            nc.vector.tensor_scalar(sin[:, :, :], sin[:, :, :], PI, -PI, ALU.min, ALU.max).then_inc(dch, 1)
            moments_end(dve, 0, 0)
            dve.wait_ge(w_high, 1)
            nc.vector.scalar_tensor_tensor(out=wqkv[:, 1, :, :].rearrange("p k n -> p (k n)"),
                                           in0=wst.rearrange("p k n -> p (k n)"), scalar=WS,
                                           in1=wqkv[:, 0, :, :].rearrange("p k n -> p (k n)"),
                                           op0=ALU.mult, op1=ALU.subtract).then_inc(ln_ready, 1)
            dve.wait_ge(ln_ready, 1)
            dve.wait_ge(b_in, 64)
            nc.vector.sem_inc(dacc, 3)
            for ahead in (ot_ready, recip_done, k_stored, wo_added):
                dve.sem_inc(ahead, AHEAD)

            def norm(b, k, s):
                g = b * TB + k
                if reused(k):
                    dve.wait_ge(xlo_ready, g - 1)
                nc.vector.tensor_scalar(xn[s], xres[:, ds(g, 1), :].rearrange("p a d -> p (a d)"),
                                        mean[:, ds(g, 1)], rstd[:, ds(g, 1)], ALU.subtract, ALU.mult).then_inc(xn_ready, 1)

            def split_low(b, k, s):
                g = b * TB + k
                dve.wait_ge(xhi_ready, g + 1)
                nc.vector.tensor_tensor(xh[s][:, 1, :], xn[s], xh[s][:, 0, :], ALU.subtract).then_inc(xlo_ready, 1)

            def add_bias(b, k, s):
                g = b * TB + k
                dve.wait_ge(qkv_ready, g + 1)
                if reused(k):
                    dve.wait_ge(qlo_done, (g - 1) * 2)
                nc.vector.scalar_tensor_tensor(out=qk[s], in0=banks[2 * s], scalar=1.0 / WS, in1=bias[:, 0:2 * D],
                                               op0=ALU.mult, op1=ALU.add).then_inc(qk_ready, 1)
                nc.vector.scalar_tensor_tensor(out=V[:, ds(k, 1), :].rearrange("p a d -> p (a d)"),
                                               in0=banks[2 * s + 1][:, 0:D], scalar=1.0 / WS,
                                               in1=bias[:, 2 * D:3 * D], op0=ALU.mult, op1=ALU.add).then_inc(v_ready, 1)

            def split_qk_low(b, k, s):
                g = b * TB + k
                dve.wait_ge(hi_done, (g + 1) * 2)
                qv = qk[s][:, 0:D].rearrange("p (h c) -> p h c", h=H)
                kv = qk[s][:, D:2 * D].rearrange("p (h c) -> p h c", h=H)
                nc.vector.tensor_tensor(qlo[s][:, :, :], qv, qtok[s][:, :, 0:HD], ALU.subtract).then_inc(qlo_done, 1)
                nc.vector.tensor_tensor(ktok[s][:, :, HD:P], kv, ktok[s][:, :, 0:HD], ALU.subtract).then_inc(qlo_done, 1)

            def store_k(b, k, s):
                g = b * TB + k
                dve.wait_ge(tr_k, g + 1)
                nc.vector.tensor_copy(K1[:, :, ds(k * P, P)], kps).then_inc(k_stored, 1)
                nc.vector.tensor_copy(K2[0:HD, :, ds(k * P, P)], kps[0:HD]).then_inc(k_stored, 1)

            def row_max(n, a):
                dve.wait_ge(a_ready, n * 32 + a + 1)
                nc.vector.tensor_reduce(mx[:, a // 4, a % 4:a % 4 + 1], banks[4 + a % 2][:, :], AX.X, ALU.max).then_inc(max_done, 1)

            def max_col(n):
                dve.wait_ge(max_done, (n + 1) * 32)
                nc.vector.tensor_reduce(m8[:, :], mx[:, :, :], AX.X, ALU.max).then_inc(m8_done, 1)
                dve.wait_ge(m8_done, n + 1)
                nc.vector.tensor_scalar(mt[:, :, HD:HD + 1], m8[:, :].unsqueeze(2), -1.0, None, ALU.mult).then_inc(negm, 1)

            def max_row(n, b, q, hp):
                dve.wait_ge(mT_ready, n + 1)
                nc.vector.tensor_copy(Q2[HD:HD + 1, 2 * hp:2 * hp + 2, ds(q * QB, QB)], mtps[HD:HD + 1]).then_inc(mrow, 1)

            def reciprocals(n, j):
                dve.wait_ge(den_ready, n + AHEAD)
                nc.vector.reciprocal(recip[:, j * P:(j + 1) * P], banks[7][:, j * P:(j + 1) * P]).then_inc(recip_done, 1)

            def normed(n, hp):
                dve.wait_ge(recip_done, n * 4 + AHEAD)
                dve.wait_ge(pv_copied, n + AHEAD)
                nc.vector.tensor_tensor(OT[:, hp, :], pvraw[:, :], recip[:, :], ALU.mult).then_inc(ot_ready, 1)

            def add_out(b, q, r, bank=banks[7]):
                dve.wait_ge(wo_ready, (b * NQ + q) * 2 + r + 1)
                xs = xres[:, ds(b * TB + q * 4 + 2 * r, 2), :]
                nc.vector.tensor_tensor(xs, bank.rearrange("p (a d) -> p a d", a=2), xs, ALU.add).then_inc(wo_added, 1)

            def prologue(n, b):
                for i in range(8):
                    dve.wait_ge(a_ready, n * 32 + 4 * i + 4)
                    nc.vector.tensor_reduce(mx[:, i, :], psum[:, 4 * (i % 2):4 * (i % 2) + 4, :], AX.X, ALU.max).then_inc(max_done, 4)
                max_col(n)
                max_row(n, b, 0, 0)

            def block(n, b, q, hp, nxt, add, m):
                for kt in range(NK):
                    if kt < 4 and (hp or add):
                        reciprocals(n, kt)
                    if kt == 4 and (hp or add):
                        normed(n, 1 - hp)
                    if nxt:
                        for a in rows_of(kt):
                            row_max(n + 1, a)
                    if add and kt == OUT0:
                        dve.wait_ge(bo_added, b * 4 + 4)
                        add_out(b, q - 1, 0)
                    if add and kt == OUT1:
                        add_out(b, q - 1, 1)
                    if hp and 8 <= kt < 12:
                        if kt == 8:
                            dve.wait_ge(x_in[1], 32)
                            dve.wait_ge(wo_added, b * (2 * NQ) + AHEAD)
                        row_sums(dve, b * -TB + (q * 4 + (TB + kt - 8)))
                    if hp and not nxt and kt == 12:
                        moments(dve, b * -TB + TB, b + 1)
                    if nxt and kt == 11:
                        max_col(n + 1)
                    if nxt and kt == TURN:
                        max_row(n + 1, b, *nxt)
                    if kt == 12 and m is not None:
                        dve.wait_ge(wh_done, m + 1)
                        nc.vector.scalar_tensor_tensor(out=upc(m, 1), in0=stage[:, 1 - hp, :], scalar=ES, in1=upc(m, 0),
                                                       op0=ALU.mult, op1=ALU.subtract).then_inc(wl_done, 1)
                    if kt == 14:
                        dve.wait_ge(exp_done, n * NK + 15)
                        nc.vector.tensor_tensor(accd[:, :, :], Pr[:, 1, :, :], Pr[:, 2, :, :], ALU.add).then_inc(dacc, 1)
                        dve.wait_ge(pacc, n * 12 + 12 + AHEAD)
                        dve.wait_ge(dacc, n * 3 + 4)
                        nc.vector.tensor_tensor(accd[:, :, :], accd[:, :, :], accp[:, :, :], ALU.add).then_inc(dacc, 1)
                        dve.wait_ge(dacc, n * 3 + 5)
                        nc.vector.sem_inc(accp_free, 1)
                dve.wait_ge(exp_done, n * NK + 16)
                nc.vector.tensor_tensor(accd[:, :, :], accd[:, :, :], Pr[:, 3, :, :], ALU.add).then_inc(dacc, 1)

            def last(n, b):
                dve.wait_ge(pv_copied, n + 8 + AHEAD)
                for j in range(4):
                    reciprocals(n + 8, j)
                    dve.wait_ge(recip_done, (n + 7) * 4 + (j + 1 + AHEAD))
                    nc.vector.tensor_tensor(OT[:, 1, j * P:(j + 1) * P], pvraw[:, j * P:(j + 1) * P],
                                            recip[:, j * P:(j + 1) * P], ALU.mult).then_inc(quarter, 1)
                dve.wait_ge(quarter, b * 4 + 4)
                dve.sem_inc(ot_ready, 1)
                moments_end(dve, b * -TB + TB, b + 1)
                add_out(b, NQ - 1, 0, banks[0])
                add_out(b, NQ - 1, 1, banks[1])

            with dve.Fori(0, B) as b:
                schedule(dve, b, (NORM, norm), (SPLIT, split_low), (PROJ, add_bias), (STORE, store_k), (SPLITQK, split_qk_low))
                blocks(dve, b, prologue, block, last)

        @block_.tensor
        def _(pe):
            pe.sem_inc(den_ready, AHEAD)
            pe.wait_ge(pset, 18)
            pe.wait_ge(ln_ready, 1)
            pe.wait_ge(k_in, 16)

            def turn_x(b, k, s):
                g = b * TB + k
                pe.wait_ge(xlo_ready, g + 1)
                if reused(k):
                    pe.wait_ge(xt_ready, g - 1)
                for a in range(4):
                    m = nc.tensor.transpose(xtp[s][:, a, :], xh[s][:, a // 2, (a % 2) * P:(a % 2 + 1) * P], idh[:, :])
                m.then_inc(xtp_ready, 1)

            def project(b, k, s):
                g = b * TB + k
                pe.wait_ge(xt_ready, g + 1)
                if reused(k):
                    pe.wait_ge(v_ready, g - 1)
                parts = [(xp, wp, c) for xp, wp in ((0, 0), (0, 1), (1, 0)) for c in range(KD)]
                for o, (bank, lo, hi) in enumerate(((2 * s, 0, 2 * D), (2 * s + 1, 2 * D, 3 * D))):
                    for j, (xp, wp, c) in enumerate(parts):
                        m = nc.tensor.matmul(banks[bank][:, 0:hi - lo], xT[s][:, 2 * xp + c, :], wqkv[:, wp, c, lo:hi],
                                             start=(j == 0), stop=(j == len(parts) - 1))
                m.then_inc(qkv_ready, 1)

            def turn_qk(b, k, s):
                g = b * TB + k
                pe.wait_ge(qlo_done, (g + 1) * 2)
                pe.wait_ge(k_stored, g * 2 + AHEAD)
                for h in range(H):
                    m = nc.tensor.transpose(kps[:, h, :], ktok[s][:, h, :], idh[:, :])
                m.then_inc(tr_k, 1)
                pe.wait_ge(q_stored, g * 2 + AHEAD)
                for h in range(H):
                    nc.tensor.transpose(q1ps[:, h, :], qtok[s][:, h, :], idh[:, :])
                for h in range(H):
                    m = nc.tensor.transpose(qlps[:, h, :], qlo[s][:, h, :], idh[:, :])
                m.then_inc(tr_q, 1)

            def a_mm(n, q, hp, a):
                hh, qt, kc = a // 16, a // 4 % 4, a % 4
                h = 2 * hp + hh
                if a >= 2:
                    pe.wait_ge(max_done, n * 32 + a - 1)
                nc.tensor.matmul(banks[4 + a % 2][:, :], Q1[:, h, ds(q * QB + qt * P, P)], K1[:, h, kc * 512:(kc + 1) * 512],
                                 start=True, stop=True).then_inc(a_ready, 1)

            def m_turn(n):
                pe.wait_ge(negm, n + 1)
                for j in range(8):
                    m = nc.tensor.transpose(mtps[:, j // 4, (j % 4) * P:(j % 4 + 1) * P], mt[:, j, :], idh[:, :])
                m.then_inc(mT_ready, 1)

            def scores(n, q, hp, kt, between=None):
                for hh in range(2):
                    if hh and between:
                        between()
                    h = 2 * hp + hh
                    o = banks[2 * (kt % 2) + hh][:, :]
                    nc.tensor.matmul(o, K1[:, h, kt * P:(kt + 1) * P], Q1[:, h, ds(q * QB, QB)], start=True, stop=False)
                    m = nc.tensor.matmul(o, K2[:, h, kt * P:(kt + 1) * P], Q2[:, h, ds(q * QB, QB)], start=False, stop=True)
                m.then_inc(s_ready, 1)

            def sums(n):
                pe.wait_ge(dacc, n * 3 + 3)
                for hh in range(2):
                    m = nc.tensor.matmul(banks[7][hh * HD:(hh + 1) * HD, :], ones[:, :], accd[:, hh, :], start=True, stop=True)
                m.then_inc(den_ready, 1)

            def out_proj(b, q, r, bank=banks[7], by_quarters=False):
                for j in range(2):
                    c = 2 * r + j
                    if by_quarters:
                        pe.wait_ge(quarter, b * 4 + (c + 1))
                    for hp in range(HP):
                        m = nc.tensor.matmul(bank[:, j * D:(j + 1) * D], OT[:, hp, c * P:(c + 1) * P], wo_sb[:, hp, :],
                                             start=(hp == 0), stop=(hp == HP - 1))
                m.then_inc(wo_ready, 1)

            def prologue(n, b):
                pe.wait_ge(q_stored, (b + 1) * (2 * TB) + AHEAD)
                pe.wait_ge(k_stored, (b + 1) * (2 * TB) + AHEAD)
                for i in range(8):
                    if i >= 2:
                        pe.wait_ge(max_done, n * 32 + 4 * i - 4)
                    for kc in range(4):
                        m = nc.tensor.matmul(banks[4 * (i % 2) + kc][:, :], Q1[:, i // 4, (i % 4) * P:(i % 4 + 1) * P],
                                             K1[:, i // 4, kc * 512:(kc + 1) * 512], start=True, stop=True)
                    m.then_inc(a_ready, 4)
                pe.wait_ge(wo_added, b * (2 * NQ) + AHEAD)
                m_turn(n)
                pe.wait_ge(mrow, n + 1)
                scores(n, 0, 0, 0)
                scores(n, 0, 0, 1)

            def block(n, b, q, hp, nxt, add, m):
                for kt in range(NK):
                    rows = rows_of(kt) if nxt else []

                    def next_row():
                        if rows:
                            a_mm(n + 1, nxt[0], nxt[1], rows.pop(0))
                    if add and kt == OUT0:
                        pe.wait_ge(ot_ready, n + AHEAD)
                        out_proj(b, q - 1, 0)
                    if add and kt == OUT1:
                        pe.wait_ge(wo_added, (b * NQ + q - 1) * 2 + 1 + AHEAD)
                        out_proj(b, q - 1, 1)
                    if nxt and kt == TURN:
                        if add:
                            pe.wait_ge(wo_added, (b * NQ + q) * 2 + AHEAD)
                        elif hp:
                            pe.wait_ge(recip_done, n * 4 + AHEAD)
                        m_turn(n + 1)
                    if kt:
                        next_row()
                    pe.wait_ge(exp_done, n * NK + kt + 1)
                    if kt == 0:
                        pe.wait_ge(pv_copied, n + AHEAD)
                    for hh in range(2):
                        h = 2 * hp + hh
                        m = nc.tensor.matmul(banks[6][hh * HD:(hh + 1) * HD, :], V[:, kt, h * HD:(h + 1) * HD],
                                             Pr[:, kt % 4, hh, :], start=(kt == 0), stop=(kt == NK - 1))
                    if kt == NK - 1:
                        m.then_inc(pv_done, 1)
                    if kt == 0 and (hp or add):
                        sums(n)
                    next_row()
                    if kt < NK - 2:
                        scores(n, q, hp, kt + 2, next_row)
                    elif nxt:
                        if kt == NK - 2:
                            pe.wait_ge(mrow, n + 2)
                        scores(n + 1, nxt[0], nxt[1], kt + 2 - NK, next_row)
                    while rows:
                        next_row()
            def last(n, b):
                sums(n + 8)
                for r in range(2):
                    out_proj(b, NQ - 1, r, banks[r], True)

            with pe.Fori(0, B) as b:
                schedule(pe, b, (TURNX, turn_x), (PROJ, project), (STORE, turn_qk))
                blocks(pe, b, prologue, block, last)

        block_.__exit__(None, None, None)

        NP2 = NT // 2
        FIRST = TB // 3 + 1
        xn2 = [ring[:, (3 + s) * 2 * D:(4 + s) * 2 * D] for s in range(4)]
        xf = [(accp, accd)[s // 2][:, s % 2, :].rearrange("p (k c) -> p k c", k=2 * KD) for s in range(4)]
        lt = [pvraw[0:8, s * 2 * P:(s + 1) * 2 * P] for s in range(2)]
        st_w = [stage[:, 0, :], stage[:, 1, :], ring[:, 0:CH], ring[:, CH:2 * CH]]
        spare = [stage[:, :, :].rearrange("p a n -> p (a n)"), OT[:, :, :].rearrange("p a n -> p (a n)"),
                 wqkv[:, :, :, :].rearrange("p a k n -> p (a k n)").bitcast(F32)]

        def col(i, n=NT * 8, o=0):
            m, j = (0, i) if i < 6 else (1, i - 6) if i < 10 else (2, i - 10)
            return spare[m][:, j * 256 + o:j * 256 + o + n]
        lg = col(12).rearrange("p (t e) -> p t e", e=8)
        v8 = col(6).rearrange("p (t e) -> p t e", e=8)
        i8 = col(7).bitcast(U32).rearrange("p (t e) -> p t e", e=8)
        i8f = col(2, NT * 2).rearrange("p (t k) -> p t k", k=2)
        oh = [col(3 + k).rearrange("p (t e) -> p t e", e=8) for k in range(2)]
        m16 = col(5, 128).bitcast(F16)
        tot = col(6).rearrange("p (e t) -> p e t", e=8)
        inc = col(7).rearrange("p (e t) -> p e t", e=8)
        cmp = col(8, 128).rearrange("p (e j) -> p e j", e=8)
        nt = col(9, 8)
        endt = col(9, 8, 8)
        start = col(9, 8, 16)
        off = col(10).rearrange("p (t e) -> p t e", e=8)
        prod = [col(11 + k).rearrange("p (t e) -> p t e", e=8) for k in range(2)]
        posf = col(13, NT * 2).rearrange("p (k t) -> p k t", k=2)
        tcmp = col(14, SLOT_TILES * 7).rearrange("p (j e) -> p j e", e=7)
        dif = col(13, 32, 64)
        edif = col(13, 32, 96)
        one = col(13, 32, 128)
        exf = col(13, SLOT_TILES, 160)
        LATE = 2 * (NE - EARLY)

        def late(i, part):
            return upc(2 * EARLY + i, part)

        def dnc(e, part):
            return w_dn[:, ds(e * (2 * DNW), 2 * DNW)].rearrange("p (k a d) -> p k a d", k=3, a=2)[:, :, part, :]

        def source(d):
            return NE * UPW + d * DNW

        def piece(i):
            if i < LATE:
                return (2 * EARLY + i) * CH, (late(i, 0), late(i, 1)), lambda v: v
            return source(i - LATE), (dnc(i - LATE, 0), dnc(i - LATE, 1)), lambda v: v.rearrange("p (k d) -> p k d", k=3)

        def flow(*stages):
            for k in range(-4, NP2):
                for ahead, stage_ in stages:
                    if 0 <= k + ahead < NP2:
                        stage_(k + ahead, (k + ahead) % 4)

        prep = nc.Block()
        prep.__enter__()

        @prep.sync
        def _(sp):
            for i in range(LATE + NE):
                if i >= 4:
                    sp.wait_ge(w2l, i - 3)
                o, _, _ = piece(i)
                sp.dma_start(st_w[i % 4], experts[:, o:o + CH]).then_inc(w2_in[i % 4], 16)

        @prep.gpsimd
        def _(pool):
            def low(t, s):
                pool.wait_ge(hi2, t + 1)
                pool.tensor_tensor(xs[:, 2 * t:2 * t + 2, D:2 * D], xn2[s].rearrange("p (t d) -> p t d", t=2),
                                   xs[:, 2 * t:2 * t + 2, 0:D], ALU.subtract).then_inc(lo2, 1)
            flow((2, low))

        @prep.scalar
        def _(act):
            def high(t, s):
                act.wait_ge(xn2_ready, 2 * t + 2)
                nc.scalar.activation(xs[:, 2 * t:2 * t + 2, 0:D], xn2[s].rearrange("p (t d) -> p t d", t=2),
                                     ACT.Copy).then_inc(hi2, 1)

            def columns(t, s):
                act.wait_ge(t2_ready, t + 1)
                if t >= 4:
                    act.wait_ge(lt_ready, t - 3)
                nc.scalar.activation(xf[s], banks[s].rearrange("p (k c) -> p k c", k=2 * KD), ACT.Copy).then_inc(xf_ready, 1)

            def weights(t, s):
                if t < LATE + NE:
                    _, (high_, _), shape = piece(t)
                    act.wait_ge(w2_in[t % 4], (t // 4 + 1) * 16)
                    nc.scalar.activation(high_, shape(st_w[t % 4]), ACT.Copy, scale=ES).then_inc(w2h, 1)

            def root2(t, s):
                if t == FIRST:
                    moments_root(act, 3)
            def rows8(t, s):
                act.wait_ge(lt_ready, t + 1)
                if t >= 2:
                    act.wait_ge(lg_ready, t - 1)
                nc.scalar.activation(lt[t % 2], banks[4 + t % 2][0:8, 0:2 * P], ACT.Copy).then_inc(lt_kept, 1)
            flow((3, high), (4, root2), (2, columns), (3, weights), (1, rows8))

        @prep.tensor
        def _(pe):
            pe.wait_ge(g_in, 16)

            def turn(t, s):
                pe.wait_ge(xn2_ready, 2 * t + 2)
                if t >= 4:
                    pe.wait_ge(xf_ready, t - 3)
                for c in range(2 * KD):
                    m = nc.tensor.transpose(banks[s][:, c * P:(c + 1) * P], xn2[s][:, c * P:(c + 1) * P], idf[:, :])
                m.then_inc(t2_ready, 1)

            def logits(t, s):
                pe.wait_ge(xf_ready, t + 1)
                if t >= 2:
                    pe.wait_ge(lt_kept, t - 1)
                for c in range(KD):
                    m = nc.tensor.matmul(banks[4 + t % 2][0:8, 0:2 * P].rearrange("p (u n) -> p u n", u=2), gate[:, c, :],
                                         xf[s].rearrange("p (u k) n -> p u k n", u=2)[:, :, c, :], start=(c == 0), stop=(c == KD - 1))
                m.then_inc(lt_ready, 1)

            def turn_back(t, s):
                pe.wait_ge(lt_kept, t + 1)
                if t >= 4:
                    pe.wait_ge(lg_kept, t // 2 - 1)
                for u in range(2):
                    o = (2 * (t % 2) + u) * 8
                    m = nc.tensor.transpose(banks[6 + t // 2 % 2][:, o:o + 8], lt[t % 2][:, u * P:(u + 1) * P], idf[0:8, 0:8])
                m.then_inc(lg_ready, 1)

            flow((3, turn), (1, logits), (0, turn_back))

        @prep.vector
        def _(dve):
            def norm(t, s):
                if t >= 4:
                    dve.wait_ge(t2_ready, t - 3)
                    dve.wait_ge(lo2, t - 3)
                for u in range(2):
                    nc.vector.tensor_scalar(xn2[s][:, u * D:(u + 1) * D], xres[:, 2 * t + u, :], mean[:, 2 * t + u:2 * t + u + 1],
                                            rstd[:, 2 * t + u:2 * t + u + 1], ALU.subtract, ALU.mult).then_inc(xn2_ready, 1)

            def weights(t, s):
                if t < LATE + NE:
                    _, (high_, low_), shape = piece(t)
                    dve.wait_ge(w2h, t + 1)
                    nc.vector.scalar_tensor_tensor(out=low_, in0=shape(st_w[t % 4]), scalar=ES, in1=high_,
                                                   op0=ALU.mult, op1=ALU.subtract).then_inc(w2l, 1)

            def statistics(t, s):
                for j in range(3 * t, min(3 * t + 3, TB)):
                    row_sums(dve, TB + j)
                if t == FIRST:
                    moments(dve, TB, 3)
                if t == FIRST + 1:
                    moments_end(dve, TB, 3)

            def keep(g):
                dve.wait_ge(lg_ready, 2 * g + 2)
                nc.vector.tensor_copy(lg[:, 4 * g:4 * g + 4, :], banks[6 + g % 2][:, 0:32]
                                      .rearrange("p (t e) -> p t e", e=8)).then_inc(lg_kept, 1)

            def best(g):
                dve.wait_ge(lg_kept, g + 1)
                for t in range(4 * g, 4 * g + 4):
                    nc.vector.max(v8[:, t, :], lg[:, t, :]).then_inc(top_v, 1)
                dve.wait_ge(top_v, 4 * g + 4)
                for t in range(4 * g, 4 * g + 4):
                    nc.vector.max_index(i8[:, t, :], v8[:, t, :], lg[:, t, :]).then_inc(top_i, 1)

            def choice(t, s):
                if t and t % 2 == 0:
                    keep(t // 2 - 1)
                if t > NP2 // 2:
                    best(t - NP2 // 2 - 1)

            flow((4, norm), (4, statistics), (2, weights), (0, choice))
            keep(NP2 // 2 - 1)
            best(NP2 // 2 - 1)

        prep.__exit__(None, None, None)

        def part(base, s, n):
            return ring[:, base + s * n:base + (s + 1) * n]
        XT = [part(0, s, 512).bitcast(F16).rearrange("p (a c t) -> p a c t", a=2, c=KD) for s in range(2)]
        SG = [part(1024, s, MT) for s in range(2)]
        HF = [part(1536, s, MT) for s in range(2)]
        HH = [part(2048, s, 384).bitcast(F16).rearrange("p (f t) -> p f t", f=3) for s in range(2)]
        HL = [part(2816, s, 384).bitcast(F16).rearrange("p (f t) -> p f t", f=3) for s in range(2)]
        xr = [stage[:, :, :].rearrange("p a n -> p (a n)").bitcast(F16)[:, s * 2 * ROW:(s + 1) * 2 * ROW]
              .rearrange("p (u n) -> p u n", u=2) for s in range(2)]
        ys = [accd[:, s, :].rearrange("p (u d) -> p u d", u=2) for s in range(2)]
        GROW = 8 * D
        G0 = 4
        assert G0 * GROW <= 2 * S1 * ROW and (SHARED_TILES - G0) * GROW <= (NE - 1) * 2 * UPW
        gbuf = [(wide[:, UPC + DNC + g * GROW:UPC + DNC + (g + 1) * GROW] if g < G0
                 else w_up[:, (g - G0) * GROW:(g - G0 + 1) * GROW])
                .bitcast(F32).rearrange("p (t k d) -> p t k d", t=2, k=2) for g in range(SHARED_TILES)]
        ST, RT = SHARED_TILES, SLOT_TILES

        def tiles(e, *parts):
            before = [sum(n for _, _, n, _ in parts[:p]) for p in range(len(parts))]

            def at(p, i, j):
                return parts[p][1] + i, (before[p] + j) % 2, before[p] + i

            def step(p, i, j):
                (load, up, down, evac), _, n, _ = parts[p]
                following, last = (load, at(p, i + 1, j + 1)), (down, evac, at(p, i - 1, j - 1))
                if isinstance(i, int) and i == n - 1:
                    following = (parts[p + 1][0][0], at(p + 1, 0, 0)) if p + 1 < len(parts) else None
                if isinstance(i, int) and i == 0:
                    m = parts[p - 1][2] - 1
                    last = (parts[p - 1][0][2], parts[p - 1][0][3], at(p - 1, m, m)) if p else None

                def turn_next():
                    if following:
                        following[0](*following[1])

                def finish_last():
                    if last:
                        last[0](*last[2]), last[1](*last[2])
                up(*at(p, i, j), turn_next, finish_last)

            parts[0][0][0](*at(0, 0, 0))
            for p, (_, _, n, written_out) in enumerate(parts):
                step(p, 0, 0)
                step(p, 1, 1)
                pairs = 0 if written_out else (n - 3) // 2
                if pairs:
                    with e.Fori(0, pairs) as i:
                        for j in range(2):
                            step(p, i * 2 + (j + 2), j)
                for k in range(2 * pairs + 2, n):
                    step(p, k, k)
            p, m = len(parts) - 1, parts[-1][2] - 1
            parts[p][0][2](*at(p, m, m)), parts[p][0][3](*at(p, m, m))

        def fs(s, f):
            return (s + f) % 2

        GROUPS = [[g for g in range(ST) if g % 3 == 1 and g < ST - 2], [g for g in range(ST) if g % 3 != 1 or g >= ST - 2]]

        def combine_waits(e, g):
            e.wait_ge(y_read, S1 + RT if g < S1 else g + RT + 1)
            e.wait_ge(gat[g], 16)

        nothing = lambda *a: None

        moe = nc.Block()
        moe.__enter__()

        @moe.sync
        def _(sp):
            for h in range(2):
                sp.wait_ge(scat[h], 16 * 2 * (NT // 2))
            for j in range(2):
                sp.dma_start(xr[j], slots[j * MT:(j + 1) * MT, :].rearrange("(u p) n -> p u n", p=P)).then_inc(xr_in[j], 16)

            def rows_in(i, j):
                sp.wait_ge(ids_kept, i * 2 + (j + 1))
                sp.dma_start(xr[j], slots[ds((i * 2 + j + 2) * MT, MT), :].rearrange("(u p) n -> p u n", p=P)).then_inc(xr_in[j], 16)
            with sp.Fori(0, RT // 2 - 1) as i:
                rows_in(i, 0), rows_in(i, 1)
            rows_in(RT // 2 - 1, 0)
            sp.wait_ge(y_read, S1 + RT)
            for s in range(2):
                sp.wait_ge(y_out[s], 32 * ((RT + 1 - s) // 2))
            for g in range(ST):
                sp.dma_start(gbuf[g], ytok[g * 2 * MT:(g + 1) * 2 * MT, :]
                             .rearrange("(t p k) d -> p t k d", p=P, k=2)).then_inc(gat[g], 16)
            for g in range(ST):
                if g in GROUPS[0]:
                    sp.wait_ge(comb[0][1], GROUPS[0].index(g) + 1)
                else:
                    sp.wait_ge(comb[1][1], 2 * GROUPS[1].index(g) + 2)
                sp.dma_start(out[g * MT:(g + 1) * MT, :].rearrange("(t p) d -> p t d", p=P),
                             xres[:, 2 * g:2 * g + 2, :]).then_inc(done, 16)
            sp.wait_ge(done, 16 * ST)

        @moe.gpsimd
        def _(pool):
            pool.wait_ge(e_out, 16)
            ids_of = wide[:, UPC + DNC:UPC + DNC + NT * ROW].bitcast(U32).rearrange("p (t n) -> p t n", t=NT)[:, :, 0]
            TH = NT // 2
            for k in range(2):
                for h in range(2):
                    if k:
                        pool.wait_ge(scat[h], 16 * TH)
                    pool.iota(ids_of[:, h * TH:(h + 1) * TH], pattern=[[2 * P, TH]], base=h * TH * 2 * P + k,
                              channel_multiplier=2).then_inc(ids_set, 1)
                    pool.wait_ge(ids_set, 2 * k + h + 1)
                    if k == 0 and h == 0:
                        pool.wait_ge(placed, 1)
                    for t in range(h * TH, (h + 1) * TH):
                        pool.indirect_dma_start(out=slots, out_offset=bass.IndirectOffsetOnAxis(ap=pos[:, k, t:t + 1], axis=0),
                                                in_=xrow[:, t, :], in_offset=None).then_inc(scat[h], 16)

            def keep_ids(t, s, loads):
                pool.wait_ge(xtT, t + (S1 + 1))
                pool.wait_ge(xr_in[s], loads)
                if not (isinstance(t, int) and t < 2):
                    pool.wait_ge(ids_moved, t - 1)
                pool.tensor_tensor(kept[:, s, :].unsqueeze(2), xr[s][:, :, 0:2].bitcast(U32),
                                   zt[:, 0:4].bitcast(U32).unsqueeze(2), ALU.add).then_inc(ids_kept, 1)

            def move_ids(t, s, stores):
                pool.wait_ge(ids_kept, t + 1)
                if not (isinstance(t, int) and t < 1):
                    pool.wait_ge(y_read, t + S1)
                if stores is not None:
                    pool.wait_ge(y_out[s], stores)
                pool.tensor_tensor(ids[:, s, :], kept[:, s, :], zt[:, 0:4].bitcast(U32), ALU.add).then_inc(ids_moved, 1)

            def products_out(s):
                for u in range(2):
                    pool.indirect_dma_start(out=ytok, out_offset=bass.IndirectOffsetOnAxis(ap=ids[:, s, u:u + 1], axis=0),
                                            in_=ys[s][:, u, :], in_offset=None).then_inc(y_out[s], 16)
            keep_ids(0, 0, 16), keep_ids(1, 1, 16), move_ids(0, 0, None)
            keep_ids(2, 0, 32), move_ids(1, 1, None), products_out(0)
            with pool.Fori(0, RT // 2 - 1) as i:
                for j in range(2):
                    t = i * 2 + (j + 2)
                    keep_ids(t + 1, 1 - j, i * 16 + 16 * (j + 2)), move_ids(t, j, i * 32 + 32), products_out(1 - j)
            move_ids(RT - 1, 0, 32 * (RT // 2)), products_out(1)
            pool.wait_ge(y_read, S1 + RT)
            pool.wait_ge(ids_moved, RT)
            products_out(0)
            pool.wait_ge(routed, 1)
            for n, g in enumerate(GROUPS[0]):
                combine_waits(pool, g)
                for k in range(2):
                    y = gbuf[g][:, :, k, :]
                    pool.tensor_tensor(y, y, wts[:, k, 2 * g:2 * g + 2].unsqueeze(2).broadcast_to([P, 2, D]),
                                       ALU.mult).then_inc(weighed, 1)
                x2 = xres[:, 2 * g:2 * g + 2, :]
                for k in range(2):
                    pool.wait_ge(weighed, 2 * n + k + 1)
                    if k:
                        pool.wait_ge(comb[0][0], n + 1)
                    pool.tensor_tensor(x2, gbuf[g][:, :, k, :], x2, ALU.add).then_inc(comb[0][k], 1)

        @moe.scalar
        def _(act):
            def make(shared):
                def load(t, s, c):
                    act.wait_ge(xtT, c + 1)
                    nc.scalar.activation(XT[s], half(4 + s).rearrange("p (a c t) -> p a c t", a=2, c=KD), ACT.Copy).then_inc(xte, 1)

                def up(t, s, c, turn_next, finish_last):
                    for f in range(3):
                        act.wait_ge(g_ready, c * 3 + f + 1)
                        nc.scalar.activation(SG[fs(s, f)], banks[fs(s, f)][:, 0:MT], ACT.Silu, scale=1.0 / ES).then_inc(silu, 1)
                        act.wait_ge(h_ready, c * 3 + f + 1)
                        nc.scalar.activation(HH[s][:, f, :], HF[fs(s, f)], ACT.Copy).then_inc(hh_ready, 1)
                        if f == 0:
                            turn_next()
                        if f == 1:
                            finish_last()

                def evac(t, s, c):
                    if shared:
                        return
                    act.wait_ge(y_ready, c + 1)
                    act.wait_ge(ids_moved, t + 1)
                    nc.scalar.activation(ys[s], banks[6 + s].rearrange("p (u d) -> p u d", u=2), ACT.Copy).then_inc(y_read, 1)
                return load, up, nothing, evac

            act.wait_ge(rch, 1)
            nc.scalar.activation(edif, dif, ACT.Exp).then_inc(ew, 1)
            tiles(act, (make(True), 0, S1, False), (make(False), 0, RT, False), (make(True), S1, ST - S1, False))

        @moe.vector
        def _(dve):
            chain = [0]

            def link(ins):
                chain[0] += 1
                ins.then_inc(rch, 1)
                dve.wait_ge(rch, chain[0])

            link(nc.vector.tensor_tensor(dif, v8[:, :, 1], v8[:, :, 0], ALU.subtract))
            dve.wait_ge(top_i, NT)
            link(nc.vector.tensor_copy(i8f, i8[:, :, 0:2]))
            for k in range(2):
                link(nc.vector.tensor_tensor(oh[k], iot[:, 0:8].unsqueeze(1).broadcast_to([P, NT, 8]),
                                             i8f[:, :, k:k + 1].broadcast_to([P, NT, 8]), ALU.is_equal))
            nc.vector.tensor_tensor(m16.rearrange("p (t e) -> p t e", e=8), oh[0], oh[1], ALU.add).then_inc(cnt_in, 1)
            link(nc.vector.memset(one, 1.0))
            dve.wait_ge(cnt, 1)
            link(nc.vector.tensor_copy(tot, banks[7][:, 0:NT * 8].rearrange("p (t e) -> p e t", e=8)))
            for e in range(8):
                link(nc.vector.tensor_tensor_scan(inc[:, e, :], one, tot[:, e, :], 0.0, ALU.mult, ALU.add))
            link(nc.vector.tensor_tensor(cmp, inc[:, :, NT - 1:NT].broadcast_to([P, 8, 16]),
                                         iot[:, SLOT_TILES:SLOT_TILES + 16].unsqueeze(1).broadcast_to([P, 8, 16]), ALU.is_gt))
            link(nc.vector.tensor_reduce(nt, cmp, AX.X, ALU.add))
            link(nc.vector.tensor_tensor_scan(endt, one[:, 0:8], nt, 0.0, ALU.mult, ALU.add))
            link(nc.vector.tensor_tensor(start, endt, nt, ALU.subtract))
            link(nc.vector.tensor_scalar(start, start, float(MT), None, ALU.mult))
            link(nc.vector.tensor_tensor(inc, inc, tot, ALU.subtract))
            link(nc.vector.tensor_tensor(inc, inc, start.unsqueeze(2).broadcast_to([P, 8, NT]), ALU.add))
            link(nc.vector.tensor_tensor(off, banks[6][:, 0:NT * 8].rearrange("p (t e) -> p t e", e=8),
                                         inc.rearrange("p e t -> p t e"), ALU.add))
            for k in range(2):
                link(nc.vector.tensor_tensor(prod[k], oh[k], off, ALU.mult))
                link(nc.vector.tensor_reduce(posf[:, k, :], prod[k], AX.X, ALU.add))
            link(nc.vector.tensor_copy(pos[:, :, :], posf))
            dve.sem_inc(placed, 1)
            link(nc.vector.tensor_tensor(tcmp, iot[:, 0:SLOT_TILES].unsqueeze(2).broadcast_to([P, SLOT_TILES, 7]),
                                         endt[:, 0:7].unsqueeze(1).broadcast_to([P, SLOT_TILES, 7]), ALU.is_ge))
            link(nc.vector.tensor_reduce(exf, tcmp, AX.X, ALU.add))
            link(nc.vector.tensor_copy(exid[:, :], exf))
            dve.wait_ge(ew, 1)
            link(nc.vector.tensor_scalar(dif, edif, 1.0, None, ALU.add))
            link(nc.vector.reciprocal(dif, dif))
            link(nc.vector.tensor_scalar(wts[:, 0, :], dif, ES ** -2, None, ALU.mult))
            link(nc.vector.tensor_tensor(wts[:, 1, :], edif, wts[:, 0, :], ALU.mult))
            dve.sem_inc(routed, 1)

            def combine(n):
                g = GROUPS[1][n]
                combine_waits(dve, g)
                for k in range(2):
                    for u in range(2):
                        t = 2 * g + u
                        if k:
                            dve.wait_ge(comb[1][0], 2 * n + u + 1)
                        nc.vector.scalar_tensor_tensor(out=xres[:, t, :], in0=gbuf[g][:, u, k, :], scalar=wts[:, k, t:t + 1],
                                                       in1=xres[:, t, :], op0=ALU.mult, op1=ALU.add).then_inc(comb[1][k], 1)

            def beside(k, f):
                return min(max(0, 3 * k + f - 3), len(GROUPS[1]) - 4)

            def make(shared, more=None):
                def up(t, s, c, turn_next, finish_last):
                    for f in range(3):
                        if more:
                            k = c - S1 - RT
                            for n in range(beside(k, f - 1), beside(k, f)):
                                more(n)
                        dve.wait_ge(silu, c * 3 + f + 1)
                        dve.wait_ge(u_ready, c * 3 + f + 1)
                        nc.vector.tensor_tensor(HF[fs(s, f)], banks[2 + fs(s, f)][:, 0:MT], SG[fs(s, f)], ALU.mult).then_inc(h_ready, 1)
                        dve.wait_ge(hh_ready, c * 3 + f + 1)
                        nc.vector.tensor_tensor(HL[s][:, f, :], HF[fs(s, f)], HH[s][:, f, :], ALU.subtract).then_inc(hl_ready, 1)
                        if f == 1:
                            finish_last()

                def evac(t, s, c):
                    if not shared:
                        return
                    if more and c == ST + RT - 1:
                        for n in range(len(GROUPS[1]) - 4, len(GROUPS[1]) - 1):
                            more(n)
                    dve.wait_ge(y_ready, c + 1)
                    x2 = xres[:, ds(t * 2, 2), :].rearrange("p u d -> p (u d)")
                    nc.vector.scalar_tensor_tensor(out=x2, in0=banks[6 + s], scalar=ES ** -2, in1=x2,
                                                   op0=ALU.mult, op1=ALU.add).then_inc(y_read, 1)
                return nothing, up, nothing, evac

            tiles(dve, (make(True), 0, S1, False), (make(False), 0, RT, False), (make(True, combine), S1, ST - S1, True))
            combine(len(GROUPS[1]) - 1)

        @moe.tensor
        def _(pe):
            def make(shared):
                def expert(t):
                    return NE - 1 if shared else pe.value_load(exid[0:1, ds(t, 1)], min_val=0, max_val=NE - 2)

                def load(t, s, c):
                    if not shared:
                        pe.wait_ge(xr_in[s], t * 8 + (16 - 8 * s))
                    if not (isinstance(c, int) and c < 2):
                        pe.wait_ge(xte, c - 1)
                    for a in range(2):
                        for ch in range(KD):
                            for u in range(2):
                                src = xs[:, ds(t * 2 + u, 1), :].rearrange("p a n -> p (a n)") if shared else xr[s][:, u, 2:ROW]
                                o = a * D + ch * P
                                j = (a * KD + ch) * 2 + u
                                m = nc.tensor.transpose(half(4 + s)[:, j * P:(j + 1) * P], src[:, o:o + P], idh[:, :])
                    m.then_inc(xtT, 1)

                def up(t, s, c, turn_next, finish_last):
                    pe.wait_ge(xte, c + 1)
                    if not shared and isinstance(t, int) and t == 0:
                        pe.wait_ge(routed, 1)
                    e = expert(t)
                    for f in range(3):
                        for gu, sm_ in ((0, g_ready), (1, u_ready)):
                            b_ = banks[2 * gu + fs(s, f)][:, 0:MT]
                            if not (isinstance(c, int) and c * 3 + f < 2):
                                pe.wait_ge((silu, h_ready)[gu], c * 3 + (f - 1))
                            j = 0
                            for wp, xp in ((0, 0), (0, 1), (1, 0)):
                                for ch in range(KD):
                                    o = ch * 4 * FF + wp * 2 * FF + gu * FF + f * P
                                    m = nc.tensor.matmul(b_, w_up[:, ds(e * (2 * UPW) + o, P)], XT[s][:, xp, ch, :],
                                                         start=(j == 0), stop=(j == 5))
                                    j += 1
                            m.then_inc(sm_, 1)
                        if f == 0:
                            turn_next()
                        if f == 1:
                            finish_last()

                def down(t, s, c):
                    e = expert(t)
                    pe.wait_ge(hl_ready, c * 3 + 3)
                    if not (isinstance(c, int) and c < 2):
                        pe.wait_ge(y_read, c - 1)
                    for u in range(2):
                        j = 0
                        for f in range(3):
                            for hp_, wp in ((0, 0), (0, 1), (1, 0)):
                                hx = (HH, HL)[hp_][s]
                                m = nc.tensor.matmul(banks[6 + s][:, u * D:(u + 1) * D], hx[:, f, u * P:(u + 1) * P],
                                                     w_dn[:, ds(e * (2 * DNW) + (f * 2 + wp) * D, D)], start=(j == 0), stop=(j == 8))
                                j += 1
                    m.then_inc(y_ready, 1)
                return load, up, down, nothing

            pe.wait_ge(cnt_in, 1)
            nc.tensor.matmul(banks[6][:, 0:NT * 8], tri[:, :], m16, start=True, stop=True)
            nc.tensor.matmul(banks[7][:, 0:NT * 8], oneh[:, :], m16, start=True, stop=True).then_inc(cnt, 1)
            tiles(pe, (make(True), 0, S1, False), (make(False), 0, RT, False), (make(True), S1, ST - S1, False))

        moe.__exit__(None, None, None)


_INS = ["x", "wq", "bq", "wk", "bk", "wv", "bv", "wo", "bo", "freq", "gate_t", "experts"]


def kernel(L0_attn_x, L0_attn_Wq, L0_attn_bq, L0_attn_Wk, L0_attn_bk, L0_attn_Wv, L0_attn_bv, L0_attn_Wo, L0_attn_bo,
           L0_attn_nrope_freq, L0_ffn_gate_w, L0_ffn_w_up, L0_ffn_w_down, L0_ffn_sg_gate, L0_ffn_sg_up, L0_ffn_sg_down):
    import numpy as _np
    import concourse.bacc as _bacc
    from concourse import mybir as _mybir
    from concourse.bass_utils import run_bass_kernel_spmd as _run

    x = _np.asarray(L0_attn_x)
    D, P = x.shape[-1], 128
    sg = _np.concatenate([_np.asarray(L0_ffn_sg_gate), _np.asarray(L0_ffn_sg_up)], 0)[None]
    up = _np.concatenate([_np.asarray(L0_ffn_w_up), sg], 0)
    up = up.transpose(0, 2, 1).reshape(up.shape[0], D // P, P, -1).transpose(2, 0, 1, 3).reshape(P, -1)
    down = _np.concatenate([_np.asarray(L0_ffn_w_down), _np.asarray(L0_ffn_sg_down)[None]], 0)
    down = down.transpose(0, 2, 1).reshape(down.shape[0], -1, P, D).transpose(2, 0, 1, 3).reshape(P, -1)
    given = dict(x=x.reshape(-1, D), wq=L0_attn_Wq, bq=L0_attn_bq, wk=L0_attn_Wk, bk=L0_attn_bk, wv=L0_attn_Wv,
                 bv=L0_attn_bv, wo=L0_attn_Wo, bo=L0_attn_bo, freq=L0_attn_nrope_freq,
                 gate_t=_np.asarray(L0_ffn_gate_w).T, experts=_np.concatenate([up, down], 1))
    nc = _bacc.Bacc("TRN2", target_bir_lowering=False, num_devices=1)
    arrays, args = {}, []
    for name in _INS:
        a = _np.ascontiguousarray(given[name])
        arrays[f"in_{name}"] = a
        args.append(nc.dram_tensor(f"in_{name}", a.shape, _mybir.dt.from_np(a.dtype), kind="ExternalInput").ap())
    args.append(nc.dram_tensor("out_rows", (x.size // D, D), _mybir.dt.float32, kind="ExternalOutput").ap())
    add_ffn_kernel(nc, *args)
    r = _run(nc, [arrays], core_ids=[0])
    return r.results[0]["out_rows"].reshape(x.shape)
```
